# Optimizing a Trainium2 kernel written in Bass

```python
import numpy as np
import jax
import jax.numpy as jnp

def _softmax(x, axis=-1):
    return jax.nn.softmax(x, axis=axis)

def _gelu(x):
    return jax.nn.gelu(x, approximate=True)

def _silu(x):
    return jax.nn.silu(x)

def _sigmoid(x):
    return jax.nn.sigmoid(x)

def _layernorm(x, axis=-1, eps=1e-05):
    m = jnp.mean(x, axis=axis, keepdims=True)
    v = jnp.var(x, axis=axis, keepdims=True)
    return (x - m) / jnp.sqrt(v + eps)

def _scatter_add(tgt, idx, src, axis=0):
    return tgt.at[idx].add(src)

def _segment_sum(src, seg, n):
    return jax.ops.segment_sum(src, seg, n)
kernel_name = 'mk_cond_seq_d2_seqx_r8_b1f871'

def setup_inputs(seed: int=0):
    np.random.seed(seed)
    _w = jnp.asarray

    def _rec_inputs():
        import jax
        import jax.numpy as jnp
        _rk = jax.random.key(seed)
        x = 7.22e-05 + 1 * jax.random.normal(jax.random.fold_in(_rk, 1), (2, 512, 128), jnp.float32)
        _lenS = 512 - jax.random.randint(jax.random.fold_in(_rk, 7), (2,), 0, max(1, 512 // 4) + 1, jnp.int32)
        _lenS2 = 512 - jax.random.randint(jax.random.fold_in(_rk, 8), (2,), 0, max(1, 512 // 4) + 1, jnp.int32)
        cond_1024 = 0.0061147 + 1.02565 * jax.random.normal(jax.random.fold_in(_rk, 11), (2, 128), jnp.float32)
        return (x, cond_1024)
    x, cond_1024 = _rec_inputs()

    def _L0_cond_setup():
        import jax, jax.numpy as jnp
        import numpy as np
        DIM = 128
        MLP_RATIO = 4
        EPS = 1e-06

        def rmsnorm(x, w):
            return x * jax.lax.rsqrt(jnp.mean(x * x, axis=-1, keepdims=True) + EPS) * w

        def film(x, cond, w, b):
            ss = cond @ w + b
            scale, shift = jnp.split(ss, 2, axis=-1)
            return x * (1.0 + scale[:, None, :]) + shift[:, None, :]
        key = jax.random.key(seed)
        ks = jax.random.split(key, 16)
        B, N, D = (4, 256, DIM)
        H = D * MLP_RATIO
        s = lambda fan_in: 1.0 / np.sqrt(fan_in)
        return {'x': jax.random.normal(ks[0], (B, N, D), jnp.float32), 'cond': jax.random.normal(ks[1], (B, D), jnp.float32), 'norm1_w': jnp.ones((D,), jnp.float32), 'film1_w': jax.random.normal(ks[2], (D, 2 * D), jnp.float32) * s(D), 'film1_b': jnp.zeros((2 * D,), jnp.float32), 'q_w': jax.random.normal(ks[3], (D, D), jnp.float32) * s(D), 'q_b': jnp.zeros((D,), jnp.float32), 'k_w': jax.random.normal(ks[4], (D, D), jnp.float32) * s(D), 'k_b': jnp.zeros((D,), jnp.float32), 'v_w': jax.random.normal(ks[5], (D, D), jnp.float32) * s(D), 'v_b': jnp.zeros((D,), jnp.float32), 'proj_w': jax.random.normal(ks[6], (D, D), jnp.float32) * s(D), 'proj_b': jnp.zeros((D,), jnp.float32), 'norm2_w': jnp.ones((D,), jnp.float32), 'film2_w': jax.random.normal(ks[7], (D, 2 * D), jnp.float32) * s(D), 'film2_b': jnp.zeros((2 * D,), jnp.float32), 'mlp_w1': jax.random.normal(ks[8], (D, H), jnp.float32) * s(D), 'mlp_b1': jnp.zeros((H,), jnp.float32), 'mlp_w2': jax.random.normal(ks[9], (H, D), jnp.float32) * s(H), 'mlp_b2': jnp.zeros((D,), jnp.float32)}
    _L0_cond_all = _L0_cond_setup()
    _L0_cond_in = {k: v for k, v in _L0_cond_all.items() if k in ('norm1_w', 'film1_w', 'film1_b', 'q_w', 'q_b', 'k_w', 'k_b', 'v_w', 'v_b', 'proj_w', 'proj_b', 'norm2_w', 'film2_w', 'film2_b', 'mlp_w1', 'mlp_b1', 'mlp_w2', 'mlp_b2')}
    del _L0_cond_all

    def _L1_cond_setup():
        import jax, jax.numpy as jnp
        import numpy as np
        B, N, D = (2, 256, 128)
        H, HD = (16, 64)
        E, DD = (8, 512)
        EPS = 1e-05

        def _ln(x, g, b):
            m = jnp.mean(x, axis=-1, keepdims=True)
            v = jnp.var(x, axis=-1, keepdims=True)
            return (x - m) * jax.lax.rsqrt(v + EPS) * g + b
        key = jax.random.key(seed)
        ks = jax.random.split(key, 16)
        s = 0.02
        return {'x': jax.random.normal(ks[0], (B, N, D), jnp.float32), 't': jax.random.normal(ks[1], (B, 1, D), jnp.float32), 'W_ada': jax.random.normal(ks[2], (D, D), jnp.float32) * s, 'b_ada': jnp.zeros((D,), jnp.float32), 'ln1_g': jnp.ones((D,), jnp.float32), 'ln1_b': jnp.zeros((D,), jnp.float32), 'Wqkv': jax.random.normal(ks[3], (3 * H * HD, D), jnp.float32) * s, 'qn_g': jnp.ones((HD,), jnp.float32), 'qn_b': jnp.zeros((HD,), jnp.float32), 'kn_g': jnp.ones((HD,), jnp.float32), 'kn_b': jnp.zeros((HD,), jnp.float32), 'Wout': jax.random.normal(ks[4], (D, H * HD), jnp.float32) * s, 'mlp_g': jnp.ones((D,), jnp.float32), 'mlp_b': jnp.zeros((D,), jnp.float32), 'Wgate': jax.random.normal(ks[5], (E, D), jnp.float32) * s, 'fc1s': jax.random.normal(ks[6], (E, DD, D), jnp.float32) * s, 'b1s': jnp.zeros((E, DD), jnp.float32), 'fc2s': jax.random.normal(ks[7], (E, D, DD), jnp.float32) * s, 'b2s': jnp.zeros((E, D), jnp.float32)}
    _L1_cond_all = _L1_cond_setup()
    _L1_cond_in = {k: v for k, v in _L1_cond_all.items() if k in ('W_ada', 'b_ada', 'ln1_g', 'ln1_b', 'Wqkv', 'qn_g', 'qn_b', 'kn_g', 'kn_b', 'Wout', 'mlp_g', 'mlp_b', 'Wgate', 'fc1s', 'b1s', 'fc2s', 'b2s')}
    del _L1_cond_all
    return {'x': x, 'cond_1024': cond_1024, 'L0_cond_norm1_w': _L0_cond_in['norm1_w'], 'L0_cond_film1_w': _L0_cond_in['film1_w'], 'L0_cond_film1_b': _L0_cond_in['film1_b'], 'L0_cond_q_w': _L0_cond_in['q_w'], 'L0_cond_q_b': _L0_cond_in['q_b'], 'L0_cond_k_w': _L0_cond_in['k_w'], 'L0_cond_k_b': _L0_cond_in['k_b'], 'L0_cond_v_w': _L0_cond_in['v_w'], 'L0_cond_v_b': _L0_cond_in['v_b'], 'L0_cond_proj_w': _L0_cond_in['proj_w'], 'L0_cond_proj_b': _L0_cond_in['proj_b'], 'L0_cond_norm2_w': _L0_cond_in['norm2_w'], 'L0_cond_film2_w': _L0_cond_in['film2_w'], 'L0_cond_film2_b': _L0_cond_in['film2_b'], 'L0_cond_mlp_w1': _L0_cond_in['mlp_w1'], 'L0_cond_mlp_b1': _L0_cond_in['mlp_b1'], 'L0_cond_mlp_w2': _L0_cond_in['mlp_w2'], 'L0_cond_mlp_b2': _L0_cond_in['mlp_b2'], 'L1_cond_W_ada': _L1_cond_in['W_ada'], 'L1_cond_b_ada': _L1_cond_in['b_ada'], 'L1_cond_ln1_g': _L1_cond_in['ln1_g'], 'L1_cond_ln1_b': _L1_cond_in['ln1_b'], 'L1_cond_Wqkv': _L1_cond_in['Wqkv'], 'L1_cond_qn_g': _L1_cond_in['qn_g'], 'L1_cond_qn_b': _L1_cond_in['qn_b'], 'L1_cond_kn_g': _L1_cond_in['kn_g'], 'L1_cond_kn_b': _L1_cond_in['kn_b'], 'L1_cond_Wout': _L1_cond_in['Wout'], 'L1_cond_mlp_g': _L1_cond_in['mlp_g'], 'L1_cond_mlp_b': _L1_cond_in['mlp_b'], 'L1_cond_Wgate': _L1_cond_in['Wgate'], 'L1_cond_fc1s': _L1_cond_in['fc1s'], 'L1_cond_b1s': _L1_cond_in['b1s'], 'L1_cond_fc2s': _L1_cond_in['fc2s'], 'L1_cond_b2s': _L1_cond_in['b2s']}

def reference(x, cond_1024, L0_cond_norm1_w, L0_cond_film1_w, L0_cond_film1_b, L0_cond_q_w, L0_cond_q_b, L0_cond_k_w, L0_cond_k_b, L0_cond_v_w, L0_cond_v_b, L0_cond_proj_w, L0_cond_proj_b, L0_cond_norm2_w, L0_cond_film2_w, L0_cond_film2_b, L0_cond_mlp_w1, L0_cond_mlp_b1, L0_cond_mlp_w2, L0_cond_mlp_b2, L1_cond_W_ada, L1_cond_b_ada, L1_cond_ln1_g, L1_cond_ln1_b, L1_cond_Wqkv, L1_cond_qn_g, L1_cond_qn_b, L1_cond_kn_g, L1_cond_kn_b, L1_cond_Wout, L1_cond_mlp_g, L1_cond_mlp_b, L1_cond_Wgate, L1_cond_fc1s, L1_cond_b1s, L1_cond_fc2s, L1_cond_b2s):
    import jax
    import jax.numpy as jnp

    def _L0_cond_ref(x, cond, norm1_w, film1_w, film1_b, q_w, q_b, k_w, k_b, v_w, v_b, proj_w, proj_b, norm2_w, film2_w, film2_b, mlp_w1, mlp_b1, mlp_w2, mlp_b2):
        import jax, jax.numpy as jnp
        import numpy as np
        DIM = 128
        MLP_RATIO = 4
        EPS = 1e-06

        def rmsnorm(x, w):
            return x * jax.lax.rsqrt(jnp.mean(x * x, axis=-1, keepdims=True) + EPS) * w

        def film(x, cond, w, b):
            ss = cond @ w + b
            scale, shift = jnp.split(ss, 2, axis=-1)
            return x * (1.0 + scale[:, None, :]) + shift[:, None, :]
        B, N, D = x.shape
        x_in = x
        h = film(rmsnorm(x, norm1_w), cond, film1_w, film1_b)
        Q = h @ q_w + q_b
        K = h @ k_w + k_b
        V = h @ v_w + v_b
        scores = jnp.einsum('bnd,bmd->bnm', Q, K) * D ** (-0.5)
        attn = jax.nn.softmax(scores, axis=-1)
        out = jnp.einsum('bnm,bmd->bnd', attn, V)
        x = x_in + (out @ proj_w + proj_b)
        x_in = x
        h = film(rmsnorm(x, norm2_w), cond, film2_w, film2_b)
        h = jax.nn.gelu(h @ mlp_w1 + mlp_b1, approximate=False) @ mlp_w2 + mlp_b2
        return x_in + h

    def _L1_cond_ref(x, t, W_ada, b_ada, ln1_g, ln1_b, Wqkv, qn_g, qn_b, kn_g, kn_b, Wout, mlp_g, mlp_b, Wgate, fc1s, b1s, fc2s, b2s):
        import jax, jax.numpy as jnp
        import numpy as np
        B, N, D = (2, 256, 128)
        H, HD = (16, 64)
        E, DD = (8, 512)
        EPS = 1e-05

        def _ln(x, g, b):
            m = jnp.mean(x, axis=-1, keepdims=True)
            v = jnp.var(x, axis=-1, keepdims=True)
            return (x - m) * jax.lax.rsqrt(v + EPS) * g + b
        b, n, d = x.shape
        shift = jax.nn.silu(t) @ W_ada.T + b_ada
        h = _ln(x, ln1_g, ln1_b) + shift
        qkv = (h @ Wqkv.T).reshape(b, n, 3, H, HD)
        q = _ln(qkv[:, :, 0].transpose(0, 2, 1, 3), qn_g, qn_b)
        k = _ln(qkv[:, :, 1].transpose(0, 2, 1, 3), kn_g, kn_b)
        v = qkv[:, :, 2].transpose(0, 2, 1, 3)
        scores = jnp.einsum('bhnd,bhmd->bhnm', q, k) / jnp.sqrt(jnp.float32(HD))
        attn = jax.nn.softmax(scores, axis=-1)
        o = jnp.einsum('bhnm,bhmd->bhnd', attn, v)
        o = o.transpose(0, 2, 1, 3).reshape(b, n, H * HD)
        x = x + o @ Wout.T
        tok = x.reshape(-1, d)
        bs = tok.shape[0]
        gate = jax.nn.softmax(tok @ Wgate.T, axis=-1)
        k_cap = bs // E
        vals, idx = jax.lax.top_k(gate.T, k_cap)
        idx_flat = idx.T.reshape(-1)
        w = vals.T
        g = _ln(tok[idx_flat], mlp_g, mlp_b).reshape(k_cap, E, d)
        y = jnp.einsum('ked,ehd->keh', g, fc1s) + b1s
        y = jax.nn.gelu(y, approximate=True)
        y = jnp.einsum('keh,edh->ked', y, fc2s) + b2s
        y = y * w[..., None]
        tok = tok.at[idx_flat].add(y.reshape(-1, d))
        return tok.reshape(x.shape)
    x = _L0_cond_ref(x, cond_1024, L0_cond_norm1_w, L0_cond_film1_w, L0_cond_film1_b, L0_cond_q_w, L0_cond_q_b, L0_cond_k_w, L0_cond_k_b, L0_cond_v_w, L0_cond_v_b, L0_cond_proj_w, L0_cond_proj_b, L0_cond_norm2_w, L0_cond_film2_w, L0_cond_film2_b, L0_cond_mlp_w1, L0_cond_mlp_b1, L0_cond_mlp_w2, L0_cond_mlp_b2)
    x = _L1_cond_ref(x, cond_1024[:, None, :], L1_cond_W_ada, L1_cond_b_ada, L1_cond_ln1_g, L1_cond_ln1_b, L1_cond_Wqkv, L1_cond_qn_g, L1_cond_qn_b, L1_cond_kn_g, L1_cond_kn_b, L1_cond_Wout, L1_cond_mlp_g, L1_cond_mlp_b, L1_cond_Wgate, L1_cond_fc1s, L1_cond_b1s, L1_cond_fc2s, L1_cond_b2s)
    return x

_drawn_inputs = setup_inputs


def setup_inputs(seed=0):
    import zlib

    import numpy as np

    out = dict(_drawn_inputs(seed))
    spreads = {'L0_cond_norm1_w': (1.0, 0.2),
     'L0_cond_film1_b': (0.0, 0.1),
     'L0_cond_q_b': (0.0, 0.1),
     'L0_cond_k_b': (0.0, 0.8),
     'L0_cond_v_b': (0.0, 0.1),
     'L0_cond_proj_b': (0.0, 0.1),
     'L0_cond_norm2_w': (1.0, 0.2),
     'L0_cond_film2_b': (0.0, 0.1),
     'L0_cond_mlp_b1': (0.0, 0.1),
     'L0_cond_mlp_b2': (0.0, 0.1),
     'L1_cond_b_ada': (0.0, 0.8),
     'L1_cond_ln1_g': (1.0, 0.6),
     'L1_cond_ln1_b': (0.0, 0.8),
     'L1_cond_qn_g': (1.0, 0.6),
     'L1_cond_qn_b': (0.0, 0.8),
     'L1_cond_kn_g': (1.0, 0.6),
     'L1_cond_kn_b': (0.0, 0.8),
     'L1_cond_mlp_g': (1.0, 0.6),
     'L1_cond_mlp_b': (0.0, 0.8),
     'L1_cond_b1s': (0.0, 0.8),
     'L1_cond_b2s': (0.0, 0.797)}
    factors = {'L1_cond_W_ada': 5.964, 'L1_cond_Wgate': 4.989, 'L1_cond_fc1s': 8.0, 'L1_cond_fc2s': 8.0}
    for name, (base, spread) in spreads.items():
        noise = np.random.default_rng([zlib.crc32(name.encode()), seed]).standard_normal(out[name].shape)
        drawn = base * np.exp(spread * noise) if base else spread * noise
        out[name] = jnp.asarray(drawn.astype(out[name].dtype))
    for name, factor in factors.items():
        out[name] = (out[name] * factor).astype(out[name].dtype)
    return out
```

```python
from contextlib import ExitStack

import concourse.bass as bass
from concourse import mybir

P = 128
F32 = mybir.dt.float32
F32R = mybir.dt.float32r
BF16 = mybir.dt.bfloat16
I32 = mybir.dt.int32
ALU = mybir.AluOpType
ACT = mybir.ActivationFunctionType
AX = mybir.AxisListType.X
BYTES = {F32: 4, F32R: 4, BF16: 2, I32: 4}

ROWS = {}
for _name, _n in (("cond", 2), ("norm1_w", 1), ("film1_b", 2), ("q_b", 1), ("k_b", 1), ("norm2_w", 1),
                  ("film2_b", 2), ("mlp_b1", 4), ("b_ada", 1), ("ln1_g", 1), ("ln1_b", 1), ("qk_g", 1),
                  ("qk_b", 1), ("mlp_g", 1), ("mlp_b", 1), ("b1s", 32)):
    ROWS[_name] = (sum(n for _, n in ROWS.values()), _n)
NROWS = sum(n for _, n in ROWS.values())


def wait(eng, semaphore, value):
    if isinstance(value, int) and value <= 0:
        return
    eng.wait_ge(semaphore, value)


def spread(ap, shape):
    return ap.unsqueeze(len(shape) - 1).to_broadcast(shape)


def film_attention_then_expert_choice(
        nc, x, cond, norm1_w, film1_w, film1_b, q_w, q_b, k_w, k_b, v_w, v_b, proj_w, proj_b,
        norm2_w, film2_w, film2_b, mlp_w1, mlp_b1, mlp_w2, mlp_b2,
        W_ada, b_ada, ln1_g, ln1_b, Wqkv, qn_g, qn_b, kn_g, kn_b, Wout, mlp_g, mlp_b,
        Wgate, fc1s, b1s, fc2s, b2s, out):
    B, N, D = x.shape
    TOK = B * N
    TC = TOK // P
    NC = N // P
    HD = qn_g.shape[0]
    H = Wqkv.shape[0] // 3 // HD
    WC = Wqkv.shape[0] // P
    KC = H * HD // P
    HID = mlp_w1.shape[1]
    HC = HID // P
    E, DD, _ = fc1s.shape
    CAP = TOK // E
    DC = DD // P
    UNITS = H * B
    PER = 4
    STEPS = UNITS // PER
    EPS0, EPS1 = 1e-6, 1e-5
    BITS = 30
    NOWHERE = 255.0
    assert D == P and CAP == P and B == 2 and NC == 4 and HD == 64 and HC == DC == 4 and E == 8

    ctx = ExitStack()
    with ctx:
        class Area:
            def __init__(self, start):
                self.at = start

            def __call__(self, name, shape, dt=F32):
                size = BYTES[dt]
                for n in shape[1:]:
                    size *= n
                t = nc.alloc_sbuf_tensor_at(name, shape, dt, offset=self.at)
                self.at += (size + 31) // 32 * 32
                return t

        def sem(name):
            return ctx.enter_context(nc.semaphore(name))

        bank = [ctx.enter_context(nc.psum_tensor(f"bank{i}", [P, 512], F32)) for i in range(6)]
        pair = ctx.enter_context(nc.psum_tensor("pair", [P, 2, 512], F32))
        bank += [pair[:, 0, :], pair[:, 1, :]]

        keep = Area((nc.sbuf_base + 31) // 32 * 32)
        ident = keep("ident", [P, P])
        ones_bf = keep("ones_bf", [P, P], BF16)
        before_bf = keep("before_bf", [P, P], BF16)
        iota_row = keep("iota_row", [P, P])
        minus_half = keep("minus_half", [P, TC])
        rows = keep("rows", [NROWS, P])
        cols = keep("cols", [P, NROWS])
        affine = keep("affine", [P, 3, 2, B])
        silu = keep("silu", [P, 3, B])
        b2_all = keep("b2_all", [P, E, D])
        x_blk = keep("x_blk", [P, TC, D])
        x_att = keep("x_att", [P, TC, D])
        wout_T = keep("wout_T", [P, KC, D])
        wgate_T = keep("wgate_T", [P, E])
        centre = keep("centre", [P, TC])
        sumsq = keep("sumsq", [P, TC])
        meansq = keep("meansq", [P, TC])
        rstd = keep("rstd", [P, TC])
        o_start = keep.at
        o_all = keep("o_all", [P, TC, H * HD])
        area_start = keep.at

        early = Area(area_start)
        x_in = early("x_in", [P, TC, D])
        h_T = early("h_T", [P, TOK])
        h_hi = early("h_hi", [P, TOK], F32R)
        h_lo = early("h_lo", [P, TOK], F32R)
        fc_start = early.at
        sq0 = early("sq0", [P, TC, D])
        xn = early("xn", [P, TC, D])
        mlp_start = early.at
        qT0 = early("qT0", [P, TOK])
        kT0 = early("kT0", [P, TOK])
        v0 = early("v0", [P, TC, D])
        oT0 = early("oT0", [P, TOK])
        u0 = Area(mlp_start)("u0", [P, HC, TOK])
        x_mid = early("x_mid", [P, TC, D])
        p0 = early("p0", [P, 2, N])
        pT0 = early("pT0", [P, 2, NC, P])
        soft0 = early("soft0", [P, TC, 3])
        film1 = early("film1", [P, 2 * D])
        film2 = early("film2", [P, 2 * D])
        wq0 = early("wq0", [P, D])
        wk0 = early("wk0", [P, D])
        wv0 = early("wv0", [P, D])
        wp0 = early("wp0", [P, D])
        w10 = early("w10", [P, HID])
        w20 = early("w20", [P, HC, D])
        wada = early("wada", [P, D])
        wada_T = early("wada_T", [P, D])
        wgate = early("wgate", [E, D])
        vb0 = early("vb0", [P, D])
        pb0 = early("pb0", [P, D])
        mb0 = early("mb0", [P, D])
        wqkv_raw = early("wqkv_raw", [P, WC, D])
        wqkv_T = early("wqkv_T", [P, H, 3, HD])
        wmean = early("wmean", [P, H, 2])

        experts = Area(fc_start)
        fc1_raw = experts("fc1_raw", [P, E, DC, D])
        fc2_raw = experts("fc2_raw", [P, E, DD])
        fc1_T = experts("fc1_T", [P, E, DD])
        fc2_T = experts("fc2_T", [P, E, DC, D])
        xg = experts("xg", [P, E, CAP])
        ug = experts("ug", [P, 2, DC, CAP])

        loop = Area(max(early.at, experts.at))
        w_hi = loop("w_hi", [P, H, 3 * HD], F32R)
        w_lo = loop("w_lo", [P, H, 3 * HD], F32R)
        loop2_start = loop.at
        qk_sq = loop("qk_sq", [P, NC, 2, HD])
        qk_ss = loop("qk_ss", [P, NC, 2])
        qk_ms = loop("qk_ms", [P, NC, 2])
        qk_rstd = loop("qk_rstd", [P, NC, 2])
        qk_n = loop("qk_n", [P, 2, NC, 2, HD])
        v_s = loop("v_s", [P, PER, NC, HD + 1])
        qk32 = loop("qk32", [P, N])
        q_s = loop("q_s", [P, 2, N], F32R)
        k_s = loop("k_s", [P, 2, N], F32R)
        k_x = loop("k_x", [P, 2, N], F32R)
        negmax = loop("negmax", [P, 4])
        probs = loop("probs", [P, 2, N])
        probs_T = loop("probs_T", [P, 2, NC, P])
        o_rec = loop("o_rec", [P, NC])
        oT = loop("oT", [P, 2, KC, P])

        moe = Area(loop2_start)
        moe2 = Area(loop2_start - 2 * 4 * H * 3 * HD)
        onehot_T = Area(o_start)("onehot_T", [P, E, TOK], F32R)
        onehot = moe("onehot", [P, TC, E, CAP], F32R)
        tn = moe2("tn", [P, TC, D])
        tn_hi = moe2("tn_hi", [P, TC, D], F32R)
        tn_lo = moe2("tn_lo", [P, TC, D], F32R)
        xa_T = moe2("xa_T", [P, TOK])
        tn_sq = moe2("tn_sq", [P, TC, D])
        y_hi = Area(area_start)("y_hi", [P, E, D], F32R)
        y_lo = Area(area_start + 4 * E * D)("y_lo", [P, E, D], F32R)
        y_sum = Area(area_start + 8 * E * D)("y_sum", [P, 2, D])
        final = Area(area_start + 12 * E * D)("final", [P, TC, D])
        moe = Area(max(moe.at, loop.at))
        gate = moe("gate", [P, TC, E])
        gate_x = moe("gate_x", [P, TC, E])
        gate_m = moe("gate_m", [P, 2, TC])
        gate_r = moe("gate_r", [P, TC, E, 2], F32R)
        at_least = moe("at_least", [P, TC, E], BF16)
        above = moe("above", [P, TC, E], BF16)
        ties = moe("ties", [P, TC, E], BF16)
        taken = moe("taken", [P, TC, E], BF16)
        rank = moe("rank", [P, TC, E])
        slot_of = moe("slot_of", [P, TC, E])
        need = moe("need", [P, E])
        thr = moe("thr", [P, E], I32)
        thr_bit = moe("thr_bit", [P, E], I32)
        cand = moe("cand", [P, E], I32)
        next_bit = moe("next_bit", [P, E], I32)
        hit = moe("hit", [P, E], I32)
        bit = moe("bit", [P, E])
        w_slot = moe("w_slot", [P, E])

        rows_in, films_in, wada_in, x_loaded, qkvo_in, bcast_in, mlp_in, wqkv_in, wout_in, fc_in = (
            sem(n) for n in ("rows_in", "films_in", "wada_in", "x_loaded", "qkvo_in", "bcast_in", "mlp_in",
                             "wqkv_in", "wout_in", "fc_in"))
        consts = sem("consts")
        act_step, dve_step, pool_step = sem("act_step"), sem("dve_step"), sem("pool_step")
        cols_T, cols_ready, cond_exp, silu_ready, ada_T, ada_copied, ada_done, affine_ready = (
            sem(n) for n in ("cols_T", "cols_ready", "cond_exp", "silu_ready", "ada_T",
                             "ada_copied", "ada_done", "affine_ready"))
        norm_in, norm_sq, norm_ss, norm_rstd, norm_done, norm_T, h_act, h_dve, h_split = (
            sem(n) for n in ("norm_in", "norm_sq", "norm_ss", "norm_rstd", "norm_done", "norm_T",
                             "h_act", "h_dve", "h_split"))
        xpb_ready, xmb_ready = sem("xpb_ready"), sem("xmb_ready")
        qkv0_done, q0_ready, k0_ready, v0_ready = (
            sem(n) for n in ("qkv0_done", "q0_ready", "k0_ready", "v0_ready"))
        s0_done, max0_done, exp0_done, p0_ready, pT0_done, pT0_copied, o0_done, o0_copied, proj0_done, mid_ready = (
            sem(n) for n in ("s0_done", "max0_done", "exp0_done", "p0_ready", "pT0_done", "pT0_copied",
                             "o0_done", "o0_copied", "proj0_done", "mid_ready"))
        u0_done, gelu0_done, y0_done = sem("u0_done"), sem("gelu0_done"), sem("y0_done")
        wT_done, wT_copied, w_summed, w_centred, w_split = (
            sem(n) for n in ("wT_done", "wT_copied", "w_summed", "w_centred", "w_split"))
        woT_done, woT_copied = sem("woT_done"), sem("woT_copied")
        qkv_done, sq_done, ss_done, rstd_done, normed, v_copied = (
            sem(n) for n in ("qkv_done", "sq_done", "ss_done", "rstd_done", "normed", "v_copied"))
        qkT_done, qk_affine, k_hi_done, q_hi_done, k_lo_done, split_done, o_normed = (
            sem(n) for n in ("qkT_done", "qk_affine", "k_hi_done", "q_hi_done", "k_lo_done", "split_done",
                             "o_normed"))
        o_rec_done = sem("o_rec_done")
        sq_summed = sem("sq_summed")
        scores_done, max_done, exp_done, probsT_done, even_copied, odd_copied, pv_done = (
            sem(n) for n in ("scores_done", "max_done", "exp_done", "probsT_done", "even_copied",
                             "odd_copied", "pv_done"))
        oT_done, oT_act, oT_dve, out_done, att_ready = (
            sem(n) for n in ("oT_done", "oT_act", "oT_dve", "out_done", "att_ready"))
        xaT_done, xaT_act, xaT_dve, logits_done, logits_sub, gate_exp, gate_ready = (
            sem(n) for n in ("xaT_done", "xaT_act", "xaT_dve", "logits_done", "logits_sub", "gate_exp",
                             "gate_ready"))
        tn_centred, tn_squared, tn_ss, tn_split = (
            sem(n) for n in ("tn_centred", "tn_squared", "tn_ss", "tn_split"))
        bit_step, cmp_done, count_done = sem("bit_step"), sem("cmp_done"), sem("count_done")
        masks_ready, ranks_done, taken_ready, slots_done, slots_ready, hot_dve, hot_pool, gate_split = (
            sem(n) for n in ("masks_ready", "ranks_done", "taken_ready", "slots_done", "slots_ready",
                             "hot_dve", "hot_pool", "gate_split"))
        fcT_done, fcT_copied = sem("fcT_done"), sem("fcT_copied")
        xg_done, xg_ready, wslot_done, wslot_ready, hotT_done, hotT_act, hotT_dve = (
            sem(n) for n in ("xg_done", "xg_ready", "wslot_done", "wslot_ready", "hotT_done", "hotT_act",
                             "hotT_dve"))
        fc1_done, gelu_done, fc2_done, y_ready, sum_done, final_ready, stored = (
            sem(n) for n in ("fc1_done", "gelu_done", "fc2_done", "y_ready", "sum_done", "final_ready",
                             "stored"))

        def col(name, i=0):
            return cols[:, ROWS[name][0] + i:ROWS[name][0] + i + 1]

        N_ROW_DMAS = 18

        block = ctx.enter_context(nc.Block())

        @block.sync
        def _(sp):
            def row(name, src, n=None, at=0):
                r = ROWS[name][0] + at
                sp.dma_start(rows[r:r + (n or ROWS[name][1]), :], src).then_inc(rows_in, 16)

            as_row = lambda v: v.rearrange("(a d) -> a d", d=P)
            row("cond", cond)
            for name, v in (("norm1_w", norm1_w), ("film1_b", film1_b), ("q_b", q_b), ("k_b", k_b),
                            ("norm2_w", norm2_w), ("film2_b", film2_b), ("mlp_b1", mlp_b1), ("b_ada", b_ada),
                            ("ln1_g", ln1_g), ("ln1_b", ln1_b), ("mlp_g", mlp_g), ("mlp_b", mlp_b)):
                row(name, as_row(v))
            row("b1s", b1s.rearrange("e (a d) -> (e a) d", d=P))
            for name, parts in (("qk_g", (qn_g, kn_g)), ("qk_b", (qn_b, kn_b))):
                r = ROWS[name][0]
                for half, v in enumerate(parts):
                    sp.dma_start(rows[r:r + 1, half * HD:half * HD + HD],
                                 v.rearrange("(a d) -> a d", a=1)).then_inc(rows_in, 16)
            sp.dma_start(film1[:, :], film1_w).then_inc(films_in, 16)
            sp.dma_start(film2[:, :], film2_w).then_inc(films_in, 16)
            sp.dma_start(wada[:, :], W_ada).then_inc(wada_in, 16)
            for t, src in ((wq0, q_w), (wk0, k_w), (wv0, v_w), (wp0, proj_w)):
                sp.dma_start(t[:, :], src).then_inc(qkvo_in, 16)
            for t, src in ((vb0, v_b), (pb0, proj_b), (mb0, mlp_b2)):
                sp.dma_start(t[:, :], src.rearrange("(a d) -> a d", a=1).to_broadcast([P, D]))\
                  .then_inc(bcast_in, 16)
            sp.dma_start(w10[:, :], mlp_w1).then_inc(mlp_in, 16)
            sp.dma_start(w20[:, :, :], mlp_w2.rearrange("(c p) d -> p c d", p=P)).then_inc(mlp_in, 16)
            sp.dma_start(o_all[:, 0, :], Wout).then_inc(wout_in, 16)
            sp.dma_start(wgate[:, :], Wgate).then_inc(wout_in, 16)
            sp.dma_start(b2_all[:, :, :], b2s.unsqueeze(0).to_broadcast([P, E, D])).then_inc(fc_in, 16)
            sp.wait_ge(qkv_done, 1)
            sp.wait_ge(h_split, 1)
            sp.wait_ge(w_split, 1)
            sp.dma_start(fc1_raw[:, :, :, :], fc1s.rearrange("e (c p) d -> p e c d", p=P)).then_inc(fc_in, 16)
            sp.dma_start(fc2_raw[:, :, :], fc2s.rearrange("e d h -> d e h")).then_inc(fc_in, 16)
            for half in range(2):
                sp.wait_ge(final_ready, half + 1)
                sp.dma_start(out[half].rearrange("(c p) d -> p c d", p=P),
                             final[:, half * NC:half * NC + NC, :]).then_inc(stored, 16)
            sp.wait_ge(stored, 32)

        @block.gpsimd
        def _(pool):
            steps = [0]

            def link(ins):
                steps[0] += 1
                ins.then_inc(pool_step, 1)
                pool.wait_ge(pool_step, steps[0])

            link(pool.memset(ident[:, :], 0.0))
            pool.affine_select(out=ident[:, :], in_=ident[:, :], compare_op=ALU.not_equal, fill=1.0, base=0,
                               pattern=[[-1, P]], channel_multiplier=1).then_inc(consts, 1)
            pool.memset(minus_half[:, :], -0.5).then_inc(consts, 1)
            link(pool.memset(ones_bf[:, :], 1.0))
            pool.affine_select(out=before_bf[:, :], in_=ones_bf[:, :], compare_op=ALU.is_gt, fill=0.0, base=0,
                               pattern=[[1, P]], channel_multiplier=-1).then_inc(consts, 1)
            pool.iota(iota_row[:, :], [[1, P]], base=0, channel_multiplier=0,
                      allow_small_or_imprecise_dtypes=True).then_inc(consts, 1)
            pool.memset(v_s[:, :, :, HD:HD + 1], 1.0).then_inc(consts, 1)
            pool.wait_ge(consts, 2)

            def norm_scale(k, eps):
                pool.wait_ge(norm_ss, k + 1)
                link(pool.tensor_scalar(meansq[:, :], sumsq[:, :], 1.0 / D, eps, ALU.mult, ALU.add))
                pool.tensor_tensor(rstd[:, :], meansq[:, :], minus_half[:, :], ALU.pow).then_inc(norm_rstd, 1)

            norm_scale(0, EPS0)
            pool.wait_ge(x_loaded, 16)
            pool.wait_ge(bcast_in, 48)
            pool.wait_ge(norm_done, 1)
            bias = lambda t: t[:, :].unsqueeze(1).to_broadcast([P, TC, D])
            pool.tensor_tensor(x_in[:, :, :], x_in[:, :, :], bias(pb0), ALU.add).then_inc(xpb_ready, 1)
            norm_scale(1, EPS0)
            pool.wait_ge(norm_done, 2)
            pool.tensor_tensor(x_mid[:, :, :], x_mid[:, :, :], bias(mb0), ALU.add).then_inc(xmb_ready, 1)
            pool.wait_ge(w_summed, 1)
            for t in range(2):
                last = pool.tensor_tensor(wqkv_T[:, :, t, :], wqkv_T[:, :, t, :],
                                          spread(wmean[:, :, t], [P, H, HD]), ALU.add)
            last.then_inc(w_centred, 1)
            pool.wait_ge(w_centred, 2)
            pool.tensor_tensor(w_lo[:, :, :], wqkv_T[:, :, :, :].rearrange("p h t d -> p h (t d)"),
                               w_hi[:, :, :].bitcast(F32), ALU.subtract).then_inc(w_split, 1)
            norm_scale(2, EPS1)

            def unit_scale(u):
                wait(pool, ss_done, u + 1)
                wait(pool, normed, u)
                wait(pool, k_lo_done, u - 1)
                pool.tensor_tensor(qk_rstd[:, :, :].rearrange("p c t -> p (c t)"),
                                   qk_ms[:, :, :].rearrange("p c t -> p (c t)"),
                                   minus_half[:, 0:2 * NC], ALU.pow).then_inc(rstd_done, 1)

            def unit_low(u, slot, scales):
                wait(pool, rstd_done, scales)
                wait(pool, k_hi_done, u + 1)
                wait(pool, scores_done, 4 * u - 4)
                pool.tensor_tensor(k_s[HD:P, slot, :], qk32[HD:P, :], k_x[HD:P, slot, :].bitcast(F32),
                                   ALU.subtract).then_inc(k_lo_done, 1)

            def body(i, last=False):
                for j in range(PER):
                    u = i * PER + j
                    if not (last and j >= PER - 2):
                        unit_scale(u + 2)
                    if not (last and j == PER - 1):
                        unit_low(u + 1, (j + 1) % 2, UNITS if last and j >= PER - 2 else u + 3)

            unit_scale(0)
            unit_scale(1)
            unit_low(0, 0, 2)
            body(0)
            with pool.Fori(1, STEPS - 1) as i:
                body(i)
            body(STEPS - 1, last=True)

            pool.wait_ge(tn_centred, 1)
            pool.tensor_tensor(tn[:, :, :], x_att[:, :, :], spread(centre[:, :], [P, TC, D]), ALU.add)\
                .then_inc(tn_centred, 1)
            pool.wait_ge(tn_ss, 1)
            link(pool.tensor_scalar(meansq[:, :], sumsq[:, :], 1.0 / D, EPS1, ALU.mult, ALU.add))
            link(pool.tensor_tensor(rstd[:, :], meansq[:, :], minus_half[:, :], ALU.pow))
            link(pool.tensor_tensor(tn[:, :, :], tn[:, :, :], spread(rstd[:, :], [P, TC, D]), ALU.mult))
            link(pool.tensor_copy(tn_hi[:, :, :], tn[:, :, :]))
            pool.tensor_tensor(tn_lo[:, :, :], tn[:, :, :], tn_hi[:, :, :].bitcast(F32), ALU.subtract)\
                .then_inc(tn_split, 1)
            pool.wait_ge(slots_ready, 1)
            for c in range(TC // 4 * 3, TC):
                for e in range(E):
                    last = pool.tensor_scalar(onehot[:, c, e, :], iota_row[:, :], slot_of[:, c, e:e + 1], None,
                                              ALU.is_equal)
                last.then_inc(hot_pool, 1)

        @block.scalar
        def _(act):
            act.dma_start(x_in[:, :, :], x.rearrange("b (c p) d -> p (b c) d", p=P)).then_inc(x_loaded, 16)
            act.dma_start(wqkv_raw[:, :, :], Wqkv.rearrange("(c p) d -> p c d", p=P)).then_inc(wqkv_in, 16)
            act.wait_ge(x_loaded, 16)
            act.activation(sq0[:, :, :], x_in[:, :, :], ACT.Square).then_inc(norm_sq, 1)
            act.wait_ge(cols_ready, 1)
            act.activation(silu[:, 0, :], cols[:, 0:B], ACT.Exp, scale=-1.0).then_inc(cond_exp, 1)

            def into_h(k):
                act.wait_ge(norm_T, 2 * k + 1)
                if k == 0:
                    act.wait_ge(affine_ready, 1)
                act.activation(h_T[:, 0:N], bank[1][:, :], ACT.Identity, bias=affine[:, k, 1, 0:1],
                               scale=affine[:, k, 0, 0:1]).then_inc(h_act, 1)

            into_h(0)
            for b in range(B):
                act.wait_ge(qkv0_done, 3 * b + 2)
                act.activation(kT0[:, b * N:b * N + N], bank[5 + b][:, :], ACT.Identity, bias=col("k_b"))\
                   .then_inc(k0_ready, 1)

            def turned0(g):
                act.wait_ge(pT0_done, g + 1)
                wait(act, o0_done, g - 1)
                act.activation(pT0[:, g % 2, :, :].rearrange("p c n -> p (c n)"), bank[3 + g % 2][:, :],
                               ACT.Copy).then_inc(pT0_copied, 1)

            for g in range(TC):
                act.wait_ge(max0_done, g + 1)
                wait(act, pT0_done, g - 1)
                act.activation(p0[:, g % 2, :], bank[1 + g % 2][:, :], ACT.Exp, bias=soft0[:, g, 0:1],
                               accum_out=soft0[:, g, 1:2]).then_inc(exp0_done, 1)
                if g:
                    turned0(g - 1)
            turned0(TC - 1)
            act.wait_ge(mid_ready, 2)
            act.activation(sq0[:, :, :], x_mid[:, :, :], ACT.Square).then_inc(norm_sq, 1)
            for n in range(WC // 4 + KC // 4):
                if n < WC // 4:
                    act.wait_ge(wT_done, n + 1)
                    kind, h0 = n * 4 // KC, n * 8 % H
                    act.activation(wqkv_T[:, h0:h0 + 8, kind, :],
                                   bank[(6, 7)[n % 2]][:, :].rearrange("p (h d) -> p h d", d=HD), ACT.Copy)\
                       .then_inc(wT_copied, 1)
                else:
                    act.wait_ge(wT_done, n + 1)
                    m = n - WC // 4
                    act.activation(wout_T[:, 4 * m:4 * m + 4, :].rearrange("p c d -> p (c d)"),
                                   bank[(6, 7)[n % 2]][:, :], ACT.Copy).then_inc(wT_copied, 1)
            act.wait_ge(wT_done, WC // 4 + KC // 4 + 1)
            act.activation(wgate_T[:, :], bank[6][:, 0:E], ACT.Copy).then_inc(wT_copied, 1)
            into_h(1)
            for n in range(B * HC):
                b, c = n // HC, n % HC
                act.wait_ge(u0_done, n + 1)
                act.activation(u0[:, c, b * N:b * N + N], bank[3 + n % 2][:, :], ACT.Gelu,
                               bias=col("mlp_b1", c)).then_inc(gelu0_done, 1)
            act.wait_ge(norm_in, 1)
            act.activation(sq0[:, :, :], xn[:, :, :], ACT.Square).then_inc(norm_sq, 1)
            into_h(2)

            qkv = pair[:, :, :].rearrange("p a (c w) -> p (a c) w", c=2)

            def unit_in(u, j):
                wait(act, qkv_done, u + 1)
                wait(act, sq_summed, u)
                act.activation(qk_sq[:, :, :, :].rearrange("p c t d -> p c (t d)"), qkv[:, :, 0:2 * HD],
                               ACT.Square).then_inc(sq_done, 1)
                wait(act, pv_done, 4 * u - 12)
                act.activation(v_s[:, j % PER, :, 0:HD], qkv[:, :, 2 * HD:3 * HD], ACT.Copy)\
                   .then_inc(v_copied, 1)

            def unit_qk(u):
                wait(act, qkT_done, u + 1)
                wait(act, k_lo_done, u)
                wait(act, split_done, u)
                act.activation(qk32[:, :], bank[5][:, :], ACT.Identity, bias=col("qk_b"), scale=col("qk_g"))\
                   .then_inc(qk_affine, 1)

            def chunk_exp(g, s):
                wait(act, max_done, g + 1)
                wait(act, probsT_done, g - 1)
                act.activation(probs[:, s % 2, :], bank[s % 2][:, :], ACT.Exp, bias=negmax[:, s:s + 1])\
                   .then_inc(exp_done, 1)

            def even_copy(g):
                wait(act, probsT_done, g + 1)
                wait(act, pv_done, g - 1)
                act.activation(probs_T[:, 0, :, :].rearrange("p c n -> p (c n)"), bank[2][:, :], ACT.Copy)\
                   .then_inc(even_copied, 1)

            def body(i, first=False, last=False):
                for j in range(PER):
                    u = i * PER + j
                    for c in range(NC):
                        g = u * NC + c
                        if c % 2 == 0 and not (first and j == 0 and c == 0):
                            even_copy(g - 2)
                        if c == 0 and not (last and j >= PER - 2):
                            unit_in(u + 2, j + 2)
                        if c == 1 and not (last and j == PER - 1):
                            unit_qk(u + 1)
                        chunk_exp(g, c)

            unit_in(0, 0)
            unit_in(1, 1)
            unit_qk(0)
            body(0, first=True)
            with act.Fori(1, STEPS - 1) as i:
                body(i)
            body(STEPS - 1, last=True)
            even_copy(UNITS * NC - 2)

            for t in range(TC):
                act.wait_ge(oT_done, 2 * t + 1)
                wait(act, out_done, t - 1)
                act.activation(oT[:, t % 2, 0:4, :].rearrange("p c n -> p (c n)"), bank[2 * (t % 2)][:, :],
                               ACT.Copy).then_inc(oT_act, 1)
            act.wait_ge(xaT_done, 1)
            act.activation(xa_T[:, 0:N], bank[6], ACT.Copy).then_inc(xaT_act, 1)
            act.wait_ge(logits_sub, 1)
            act.activation(gate_x[:, :, :], gate_x[:, :, :], ACT.Exp).then_inc(gate_exp, 1)
            act.wait_ge(tn_centred, 2)
            act.activation(tn_sq[:, :, :], tn[:, :, :], ACT.Square).then_inc(tn_squared, 1)
            for n in range(2 * E):
                act.wait_ge(fcT_done, n + 1)
                dst = fc1_T[:, n, :] if n < E else fc2_T[:, n - E, :, :].rearrange("p c d -> p (c d)")
                act.activation(dst, bank[1 + n % 4][:, :], ACT.Copy).then_inc(fcT_copied, 1)
            for q in range(2):
                act.wait_ge(xg_done, q + 1)
                act.activation(xg[:, 4 * q:4 * q + 4, :].rearrange("p e n -> p (e n)"), bank[1 + q][:, :],
                               ACT.Identity, bias=col("mlp_b"), scale=col("mlp_g")).then_inc(xg_ready, 1)
            for e in range(E):
                act.wait_ge(fc1_done, e + 1)
                wait(act, fc2_done, e - 1)
                for c in range(DC):
                    last = act.activation(ug[:, e % 2, c, :], bank[1 + e % 2][:, c * CAP:c * CAP + CAP],
                                          ACT.Gelu_apprx_tanh, bias=col("b1s", e * DC + c))
                last.then_inc(gelu_done, 1)
                act.wait_ge(hotT_done, 2 * e + 1)
                act.activation(onehot_T[:, e, 0:N], bank[5][:, :], ACT.Copy).then_inc(hotT_act, 1)

        @block.vector
        def _(dve):
            steps = [0]

            def link(ins):
                steps[0] += 1
                ins.then_inc(dve_step, 1)
                dve.wait_ge(dve_step, steps[0])

            def sum_squares(k, sq):
                dve.wait_ge(norm_sq, k + 1)
                dve.tensor_reduce(sumsq[:, :], sq[:, :, :], AX, ALU.add).then_inc(norm_ss, 1)

            def scaled(k, src):
                dve.wait_ge(norm_rstd, k + 1)
                dve.tensor_tensor(xn[:, :, :], src[:, :, :], spread(rstd[:, :], [P, TC, D]), ALU.mult)\
                   .then_inc(norm_done, 1)

            def into_h(k):
                dve.wait_ge(norm_T, 2 * k + 2)
                dve.tensor_scalar(h_T[:, N:TOK], bank[2][:, :], affine[:, k, 0, 1:2], affine[:, k, 1, 1:2],
                                  ALU.mult, ALU.add).then_inc(h_dve, 1)

            sum_squares(0, sq0)
            dve.wait_ge(cols_T, 1)
            link(dve.tensor_copy(cols[:, :], bank[0][:, 0:NROWS]))
            r = ROWS["qk_g"][0]
            dve.tensor_scalar(cols[0:HD, r:r + 2], cols[0:HD, r:r + 2], float(HD) ** -0.5, None, ALU.mult)\
               .then_inc(cols_ready, 1)
            dve.wait_ge(ada_T, 1)
            dve.tensor_copy(wada_T[:, :], bank[3][:, 0:P]).then_inc(ada_copied, 1)
            dve.wait_ge(cond_exp, 1)
            link(dve.tensor_scalar(silu[:, 0, :], silu[:, 0, :], 1.0, None, ALU.add))
            link(dve.reciprocal(silu[:, 1, :], silu[:, 0, :]))
            dve.tensor_tensor(silu[:, 2, :], silu[:, 1, :], cols[:, 0:B], ALU.mult).then_inc(silu_ready, 1)
            scaled(0, x_in)
            dve.wait_ge(ada_done, 1)
            for k, (fb, w) in enumerate((("film1_b", "norm1_w"), ("film2_b", "norm2_w"))):
                film = bank[4][:, 4 * k:4 * k + 4]
                link(dve.tensor_scalar(affine[:, k, 0, :], film[:, 0:B], col(fb), 1.0, ALU.add, ALU.add))
                dve.tensor_scalar(affine[:, k, 0, :], affine[:, k, 0, :], col(w), None, ALU.mult)
                dve.tensor_scalar(affine[:, k, 1, :], film[:, B:2 * B], col(fb, 1), None, ALU.add)
            for b in range(B):
                dve.tensor_copy(affine[:, 2, 0, b:b + 1], col("ln1_g"))
            link(dve.tensor_scalar(affine[:, 2, 1, :], bank[4][:, 8:8 + B], col("b_ada"), col("ln1_b"),
                                   ALU.add, ALU.add))
            dve.tensor_copy(silu[:, 0, :], silu[:, 2, :]).then_inc(affine_ready, 1)
            into_h(0)
            dve.wait_ge(bcast_in, 48)
            for b in range(B):
                dve.wait_ge(qkv0_done, 3 * b + 1)
                dve.tensor_scalar(qT0[:, b * N:b * N + N], bank[3 + b][:, :], col("q_b"), float(D) ** -0.5,
                                  ALU.add, ALU.mult).then_inc(q0_ready, 1)
                dve.wait_ge(qkv0_done, 3 * b + 3)
                dve.tensor_tensor(v0[:, b * NC:b * NC + NC, :],
                                  bank[(7, 0)[b]][:, :].rearrange("p (c d) -> p c d", d=D),
                                  vb0[:, :].unsqueeze(1).to_broadcast([P, NC, D]), ALU.add).then_inc(v0_ready, 1)

            def attended0(b):
                dve.wait_ge(o0_done, NC * (b + 1))
                dve.tensor_copy(oT0[:, b * N:b * N + N], bank[5 + b][:, :]).then_inc(o0_copied, 1)

            def batch_out0(b):
                dve.wait_ge(proj0_done, b + 1)
                dve.wait_ge(xpb_ready, 1)
                dve.tensor_tensor(x_mid[:, b * NC:b * NC + NC, :], x_in[:, b * NC:b * NC + NC, :],
                                  bank[(7, 0)[b]][:, :].rearrange("p (c d) -> p c d", d=D), ALU.add)\
                   .then_inc(mid_ready, 1)

            for g in range(TC + 1):
                if g < TC:
                    dve.wait_ge(s0_done, g + 1)
                    dve.tensor_reduce(soft0[:, g, 0:1], bank[1 + g % 2][:, :], AX, ALU.max, negate=True)\
                       .then_inc(max0_done, 1)
                if g:
                    k = g - 1
                    dve.wait_ge(exp0_done, k + 1)
                    link(dve.reciprocal(soft0[:, k, 2:3], soft0[:, k, 1:2]))
                    dve.tensor_scalar(p0[:, k % 2, :], p0[:, k % 2, :], soft0[:, k, 2:3], None, ALU.mult)\
                       .then_inc(p0_ready, 1)
                if g == NC + 2:
                    attended0(0)
                if g == NC + 4:
                    batch_out0(0)
            attended0(1)
            batch_out0(1)
            sum_squares(1, sq0)
            scaled(1, x_mid)
            into_h(1)
            dve.wait_ge(wT_copied, WC // 4)
            link(dve.tensor_reduce(wmean[:, :, :], wqkv_T[:, :, 0:2, :], AX, ALU.add, negate=True))
            dve.tensor_scalar(wmean[:, :, :], wmean[:, :, :], 1.0 / HD, None, ALU.mult).then_inc(w_summed, 1)
            dve.wait_ge(w_centred, 1)
            dve.tensor_copy(w_hi[:, :, :], wqkv_T[:, :, :, :].rearrange("p h t d -> p h (t d)"))\
               .then_inc(w_centred, 1)
            for b in range(B):
                dve.wait_ge(y0_done, b + 1)
                dve.wait_ge(xmb_ready, 1)
                dve.tensor_tensor(x_blk[:, b * NC:b * NC + NC, :], x_mid[:, b * NC:b * NC + NC, :],
                                  bank[(7, 0)[b]][:, :].rearrange("p (c d) -> p c d", d=D), ALU.add)\
                   .then_inc(dve_step, 1)
                steps[0] += 1
            dve.wait_ge(dve_step, steps[0])
            link(dve.tensor_reduce(centre[:, :], x_blk[:, :, :], AX, ALU.add, negate=True))
            link(dve.tensor_scalar(centre[:, :], centre[:, :], 1.0 / D, None, ALU.mult))
            dve.tensor_tensor(xn[:, :, :], x_blk[:, :, :], spread(centre[:, :], [P, TC, D]), ALU.add)\
               .then_inc(norm_in, 1)
            sum_squares(2, sq0)
            scaled(2, xn)
            into_h(2)
            dve.wait_ge(h_act, 3)
            dve.wait_ge(h_dve, 3)
            link(dve.tensor_copy(h_hi[:, :], h_T[:, :]))
            dve.tensor_tensor(h_lo[:, :], h_T[:, :], h_hi[:, :].bitcast(F32), ALU.subtract)\
               .then_inc(h_split, 1)

            qkv = pair[:, :, :].rearrange("p a (c w) -> p (a c) w", c=2)

            def unit_ss(u):
                wait(dve, sq_done, u + 1)
                dve.tensor_reduce(qk_ss[:, :, :], qk_sq[:, :, :, :], AX, ALU.add).then_inc(sq_summed, 1)
                wait(dve, sq_summed, u + 1)
                wait(dve, rstd_done, u)
                dve.tensor_scalar(qk_ms[:, :, :], qk_ss[:, :, :], 1.0 / HD, EPS1, ALU.mult, ALU.add)\
                   .then_inc(ss_done, 1)

            def unit_norm(u, slot):
                wait(dve, rstd_done, u + 1)
                wait(dve, v_copied, u + 1)
                wait(dve, qkT_done, u - 1)
                dve.tensor_tensor(qk_n[:, slot, :, :, :],
                                  qkv[:, :, 0:2 * HD].rearrange("p c (t d) -> p c t d", d=HD),
                                  spread(qk_rstd[:, :, :], [P, NC, 2, HD]), ALU.mult).then_inc(normed, 1)

            def unit_high(u, slot):
                wait(dve, qk_affine, u + 1)
                wait(dve, scores_done, 4 * u - 4)
                dve.tensor_copy(k_x[HD:P, slot, :], qk32[HD:P, :]).then_inc(k_hi_done, 1)
                dve.tensor_copy(q_s[0:HD, slot, :], qk32[0:HD, :]).then_inc(q_hi_done, 1)
                dve.tensor_copy(k_s[0:HD, slot, :], qk32[HD:P, :])

            def unit_low(u, slot):
                wait(dve, q_hi_done, u + 1)
                dve.tensor_tensor(q_s[HD:P, slot, :], qk32[0:HD, :], q_s[0:HD, slot, :].bitcast(F32),
                                  ALU.subtract)
                wait(dve, k_hi_done, u + 1)
                dve.tensor_tensor(k_x[0:HD, slot, :], qk32[HD:P, :], k_x[HD:P, slot, :].bitcast(F32),
                                  ALU.subtract).then_inc(split_done, 1)

            def chunk_max(g, s):
                wait(dve, scores_done, g + 1)
                dve.tensor_reduce(negmax[:, s:s + 1], bank[s % 2][:, :], AX, ALU.max, negate=True)\
                   .then_inc(max_done, 1)

            def odd_copy(g):
                wait(dve, probsT_done, g + 1)
                wait(dve, pv_done, g - 1)
                dve.tensor_copy(probs_T[:, 1, :, :].rearrange("p c n -> p (c n)"), bank[3][:, :])\
                   .then_inc(odd_copied, 1)

            def unit_out(u, j, head):
                o = bank[4][:, 0:NC * (HD + 1)].rearrange("p (c w) -> p c w", c=NC)
                wait(dve, pv_done, 4 * u + 4)
                dve.reciprocal(o_rec[:, :], o[:, :, HD]).then_inc(o_rec_done, 1)
                wait(dve, o_rec_done, u + 1)
                b = j % B
                dve.tensor_tensor(o_all[:, b * NC:b * NC + NC, bass.ds(head * HD, HD)], o[:, :, 0:HD],
                                  spread(o_rec[:, :], [P, NC, HD]), ALU.mult).then_inc(o_normed, 1)

            def body(i, first=False, last=False):
                for j in range(PER):
                    u = i * PER + j
                    for c in range(NC):
                        g = u * NC + c
                        if c % 2 == 1 and not (first and j == 0 and c == 1):
                            odd_copy(g - 2)
                        if c == 3 and not (first and j == 0):
                            unit_out(u - 1, j + 1, 2 * i + (j + 3) // 2 - 2 + (j == 0) * 0)
                        if c == 2 and not (last and j >= PER - 2):
                            unit_norm(u + 2, j % 2)
                        chunk_max(g, c)
                        if c == 0 and not (last and j >= PER - 2):
                            unit_ss(u + 2)
                        if c == 1 and not (last and j == PER - 1):
                            unit_high(u + 1, (j + 1) % 2)
                        if c == 2 and not (last and j == PER - 1):
                            unit_low(u + 1, (j + 1) % 2)

            unit_ss(0)
            unit_norm(0, 0)
            unit_ss(1)
            unit_norm(1, 1)
            unit_high(0, 0)
            unit_low(0, 0)
            body(0, first=True)
            with dve.Fori(1, STEPS - 1) as i:
                body(i)
            body(STEPS - 1, last=True)
            odd_copy(UNITS * NC - 1)
            unit_out(UNITS - 1, PER - 1, H - 1)

            for t in range(TC + 1):
                if t < TC:
                    dve.wait_ge(oT_done, 2 * t + 2)
                    wait(dve, out_done, t - 1)
                    dve.tensor_copy(oT[:, t % 2, 4:8, :].rearrange("p c n -> p (c n)"),
                                    bank[2 * (t % 2) + 1][:, :]).then_inc(oT_dve, 1)
                if t:
                    dve.wait_ge(out_done, t)
                    dve.tensor_tensor(x_att[:, t - 1, :], x_blk[:, t - 1, :], bank[4 + (t - 1) % 2][:, 0:D],
                                      ALU.add).then_inc(att_ready, 1)
            dve.wait_ge(att_ready, TC)
            link(dve.tensor_reduce(centre[:, :], x_att[:, :, :], AX, ALU.add, negate=True))
            dve.tensor_scalar(centre[:, :], centre[:, :], 1.0 / D, None, ALU.mult).then_inc(tn_centred, 1)
            dve.wait_ge(xaT_done, 2)
            dve.tensor_copy(xa_T[:, N:TOK], bank[7]).then_inc(xaT_dve, 1)
            logits = bank[5][:, 0:TC * E].rearrange("p (c e) -> p c e", e=E)
            dve.wait_ge(logits_done, 1)
            link(dve.tensor_reduce(gate_m[:, 0, :], logits, AX, ALU.max))
            dve.tensor_tensor(gate_x[:, :, :], logits, spread(gate_m[:, 0, :], [P, TC, E]), ALU.subtract)\
               .then_inc(logits_sub, 1)
            dve.wait_ge(gate_exp, 1)
            link(dve.tensor_reduce(gate_m[:, 0, :], gate_x[:, :, :], AX, ALU.add))
            link(dve.reciprocal(gate_m[:, 1, :], gate_m[:, 0, :]))
            link(dve.tensor_tensor(gate[:, :, :], gate_x[:, :, :], spread(gate_m[:, 1, :], [P, TC, E]), ALU.mult))
            link(dve.tensor_copy(gate_r[:, :, :, 0], gate[:, :, :]))
            dve.wait_ge(tn_squared, 1)
            dve.tensor_reduce(sumsq[:, :], tn_sq[:, :, :], AX, ALU.add).then_inc(tn_ss, 1)
            dve.tensor_tensor(gate_r[:, :, :, 1], gate[:, :, :], gate_r[:, :, :, 0].bitcast(F32), ALU.subtract)\
               .then_inc(gate_split, 1)

            over = lambda t: t.unsqueeze(1).to_broadcast([P, TC, E])
            dve.memset(thr[:, :], 0).then_inc(bit_step, 1)
            dve.memset(bit[:, :], float(1 << (BITS - 1))).then_inc(bit_step, 1)
            dve.memset(cand[:, :], 1 << (BITS - 1)).then_inc(bit_step, 1)
            counts = bank[0][:, 0:E]
            INITS, OPS = 3, 6
            with dve.Fori(0, BITS) as n:
                done = INITS + OPS * n
                dve.wait_ge(bit_step, done)
                dve.tensor_tensor(at_least[:, :, :], gate[:, :, :], over(cand[:, :].bitcast(F32)), ALU.is_ge)\
                   .then_inc(cmp_done, 1)
                dve.tensor_scalar(next_bit[:, :], bit[:, :], 0.5, None, ALU.mult).then_inc(bit_step, 1)
                dve.wait_ge(bit_step, done + 1)
                dve.tensor_tensor(thr_bit[:, :], thr[:, :], next_bit[:, :], ALU.bitwise_or).then_inc(bit_step, 1)
                dve.wait_ge(count_done, n + 1)
                dve.scalar_tensor_tensor(out=hit[:, :], in0=counts, scalar=CAP - 0.5, in1=bit[:, :],
                                         op0=ALU.is_ge, op1=ALU.mult).then_inc(bit_step, 1)
                dve.wait_ge(bit_step, done + 3)
                dve.tensor_tensor(cand[:, :], thr_bit[:, :], hit[:, :], ALU.bitwise_or).then_inc(bit_step, 1)
                dve.tensor_tensor(thr[:, :], thr[:, :], hit[:, :], ALU.bitwise_or).then_inc(bit_step, 1)
                dve.tensor_scalar(bit[:, :], bit[:, :], 0.5, None, ALU.mult).then_inc(bit_step, 1)
            dve.wait_ge(bit_step, INITS + OPS * BITS)
            dve.tensor_tensor(above[:, :, :], gate[:, :, :], over(thr[:, :].bitcast(F32)), ALU.is_gt)\
               .then_inc(masks_ready, 1)
            dve.tensor_tensor(ties[:, :, :], gate[:, :, :], over(thr[:, :].bitcast(F32)), ALU.is_equal)\
               .then_inc(masks_ready, 1)
            dve.wait_ge(ranks_done, 1)
            link(dve.tensor_scalar(need[:, :], counts, -1.0, float(CAP), ALU.mult, ALU.add))
            ranks = bank[0][:, 64:64 + TC * E].rearrange("p (c e) -> p c e", e=E)
            link(dve.tensor_tensor(rank[:, :, :], ranks, over(need[:, :]), ALU.is_lt))
            link(dve.tensor_tensor(rank[:, :, :], rank[:, :, :], ties[:, :, :], ALU.mult))
            dve.tensor_tensor(taken[:, :, :], rank[:, :, :], above[:, :, :], ALU.add).then_inc(taken_ready, 1)
            dve.wait_ge(taken_ready, 1)
            dve.wait_ge(slots_done, 1)
            slots = bank[0][:, 128:128 + TC * E].rearrange("p (c e) -> p c e", e=E)
            link(dve.scalar_tensor_tensor(out=slot_of[:, :, :].rearrange("p c e -> p (c e)"),
                                          in0=bank[0][:, 128:128 + TC * E], scalar=-NOWHERE,
                                          in1=taken[:, :, :].rearrange("p c e -> p (c e)"),
                                          op0=ALU.add, op1=ALU.mult))
            dve.tensor_scalar(slot_of[:, :, :], slot_of[:, :, :], NOWHERE, None, ALU.add).then_inc(slots_ready, 1)
            dve.wait_ge(slots_ready, 1)
            for c in range(TC // 4 * 3):
                for e in range(E):
                    last = dve.tensor_scalar(onehot[:, c, e, :], iota_row[:, :], slot_of[:, c, e:e + 1], None,
                                             ALU.is_equal)
                last.then_inc(hot_dve, 1)
            dve.wait_ge(wslot_done, 1)
            dve.tensor_reduce(w_slot[:, :], bank[0][:, 256:256 + 2 * E].rearrange("p (e t) -> p e t", t=2),
                              AX, ALU.add).then_inc(wslot_ready, 1)
            for e in range(E):
                dve.wait_ge(hotT_done, 2 * e + 2)
                dve.tensor_copy(onehot_T[:, e, N:TOK], bank[6]).then_inc(hotT_dve, 1)
                dve.wait_ge(fc2_done, e + 1)
                dve.wait_ge(wslot_ready, 1)
                link(dve.tensor_tensor(y_sum[:, e % 2, :], b2_all[:, e, :], bank[3 + e % 2][:, 0:D], ALU.add))
                link(dve.tensor_scalar(y_hi[:, e, :], y_sum[:, e % 2, :], w_slot[:, e:e + 1], None, ALU.mult))
                dve.scalar_tensor_tensor(out=y_lo[:, e, :], in0=y_sum[:, e % 2, :], scalar=w_slot[:, e:e + 1],
                                         in1=y_hi[:, e, :].bitcast(F32), op0=ALU.mult, op1=ALU.subtract)\
                   .then_inc(y_ready, 1)
            for half in range(2):
                dve.wait_ge(sum_done, half + 1)
                dve.tensor_tensor(final[:, half * NC:half * NC + NC, :], x_att[:, half * NC:half * NC + NC, :],
                                  bank[(7, 1)[half]].rearrange("p (c d) -> p c d", d=D) if half == 0 else
                                  bank[1][:, :].rearrange("p (c d) -> p c d", d=D), ALU.add)\
                   .then_inc(final_ready, 1)

        @block.tensor
        def _(pe):
            def turn4(dst, srcs):
                for n, s in enumerate(srcs):
                    last = pe.transpose(dst[:, n * P:n * P + P], s, ident[:, :])
                return last

            pe.wait_ge(consts, 1)
            pe.wait_ge(rows_in, 16 * N_ROW_DMAS)
            pe.transpose(bank[0][:, 0:NROWS], rows[:, :], ident[0:NROWS, 0:NROWS]).then_inc(cols_T, 1)
            pe.wait_ge(wada_in, 16)
            pe.transpose(bank[3][:, 0:P], wada[:, :], ident[:, :]).then_inc(ada_T, 1)
            pe.wait_ge(cols_ready, 1)
            pe.wait_ge(films_in, 32)
            for k, w in enumerate((film1, film2)):
                for part in range(2):
                    at = 4 * k + 2 * part
                    last = pe.matmul(bank[4][:, at:at + B], w[:, part * D:part * D + D], cols[:, 0:B],
                                     start=True, stop=True)
            pe.wait_ge(ada_copied, 1)
            pe.wait_ge(silu_ready, 1)
            pe.matmul(bank[4][:, 8:8 + B], wada_T[:, :], silu[:, 2, :], start=True, stop=True)\
              .then_inc(ada_done, 1)

            def turn_norm(k):
                pe.wait_ge(norm_done, k + 1)
                for b in range(B):
                    turn4(bank[1 + b], [xn[:, b * NC + c, :] for c in range(NC)]).then_inc(norm_T, 1)

            turn_norm(0)
            pe.wait_ge(qkvo_in, 64)
            pe.wait_ge(h_act, 1)
            for b in range(B):
                hb = h_T[:, b * N:b * N + N]
                if b == 1:
                    pe.wait_ge(h_dve, 1)
                pe.matmul(bank[3 + b][:, :], wq0[:, :], hb, start=True, stop=True).then_inc(qkv0_done, 1)
                pe.matmul(bank[5 + b][:, :], wk0[:, :], hb, start=True, stop=True).then_inc(qkv0_done, 1)
                for c in range(NC):
                    last = pe.matmul(bank[(7, 0)[b]][:, c * D:c * D + D],
                                     h_T[:, (b * NC + c) * P:(b * NC + c + 1) * P], wv0[:, :],
                                     start=True, stop=True)
                last.then_inc(qkv0_done, 1)

            def scores0(g):
                b = g // NC
                pe.wait_ge(q0_ready, b + 1)
                pe.wait_ge(k0_ready, b + 1)
                wait(pe, exp0_done, g - 1)
                pe.matmul(bank[1 + g % 2][:, :], qT0[:, g * P:g * P + P], kT0[:, b * N:b * N + N],
                          start=True, stop=True).then_inc(s0_done, 1)

            def turn0(g):
                pe.wait_ge(p0_ready, g + 1)
                if g < 2:
                    pe.wait_ge(q0_ready, 2)
                wait(pe, pT0_copied, g - 1)
                turn4(bank[3 + g % 2], [p0[:, g % 2, c * P:c * P + P] for c in range(NC)]).then_inc(pT0_done, 1)

            def mix0(g):
                b, n = g // NC, g % NC
                pe.wait_ge(pT0_copied, g + 1)
                pe.wait_ge(v0_ready, b + 1)
                for c in range(NC):
                    last = pe.matmul(bank[5 + b][:, n * P:n * P + P], v0[:, b * NC + c, :],
                                     pT0[:, g % 2, c, :], start=(c == 0), stop=(c == NC - 1))
                last.then_inc(o0_done, 1)

            def proj0(b):
                pe.wait_ge(o0_copied, b + 1)
                for c in range(NC):
                    last = pe.matmul(bank[(7, 0)[b]][:, c * D:c * D + D],
                                     oT0[:, (b * NC + c) * P:(b * NC + c + 1) * P], wp0[:, :],
                                     start=True, stop=True)
                last.then_inc(proj0_done, 1)

            for g in range(TC + 3):
                if g < TC:
                    scores0(g)
                if 1 <= g < TC + 1:
                    turn0(g - 1)
                if 2 <= g < TC + 2:
                    mix0(g - 2)
                if g == NC + 3:
                    proj0(0)
            proj0(1)

            pe.wait_ge(wqkv_in, 16)
            pe.wait_ge(wout_in, 32)
            pe.wait_ge(mid_ready, 2)
            for n in range(WC // 4 + KC // 4):
                wait(pe, wT_copied, n - 1)
                src = [wqkv_raw[:, 4 * n + c, :] for c in range(4)] if n < WC // 4 else \
                    [o_all[:, 0, (4 * (n - WC // 4) + c) * P:(4 * (n - WC // 4) + c + 1) * P] for c in range(4)]
                turn4(bank[6 + n % 2], src).then_inc(wT_done, 1)
            pe.wait_ge(wT_copied, WC // 4 + KC // 4)
            pe.transpose(bank[6][:, 0:E], wgate[:, :], ident[0:E, 0:E]).then_inc(wT_done, 1)

            turn_norm(1)
            pe.wait_ge(mlp_in, 32)
            pe.wait_ge(h_act, 2)
            pe.wait_ge(h_dve, 2)

            def up0(n):
                b, c = n // HC, n % HC
                wait(pe, gelu0_done, n - 1)
                pe.matmul(bank[3 + n % 2][:, :], w10[:, c * P:c * P + P], h_T[:, b * N:b * N + N],
                          start=True, stop=True).then_inc(u0_done, 1)

            def down0(b):
                pe.wait_ge(gelu0_done, HC * (b + 1))
                pe.wait_ge(wT_copied, WC // 4 + KC // 4)
                for c in range(NC):
                    for k in range(HC):
                        last = pe.matmul(bank[(7, 0)[b]][:, c * D:c * D + D],
                                         u0[:, k, (b * NC + c) * P:(b * NC + c + 1) * P], w20[:, k, :],
                                         start=(k == 0), stop=(k == HC - 1))
                last.then_inc(y0_done, 1)

            for n in range(HC + 2):
                up0(n)
            down0(0)
            for n in range(HC + 2, 2 * HC):
                up0(n)
            down0(1)
            turn_norm(2)
            pe.wait_ge(h_split, 1)
            pe.wait_ge(w_split, 1)
            pe.wait_ge(wT_copied, WC // 4 + KC // 4 + 1)

            qkv = pair[:, :, :].rearrange("p a (c w) -> p (a c) w", c=2)

            def project(u, b, head):
                wait(pe, normed, u)
                wait(pe, v_copied, u)
                for c in range(NC):
                    at = (b * NC + c) * P
                    for n, (h_part, w_part) in enumerate(((h_hi, w_hi), (h_hi, w_lo), (h_lo, w_hi))):
                        last = pe.matmul(qkv[:, c, 0:3 * HD], h_part[:, at:at + P],
                                         w_part[:, bass.ds(head, 1), :].rearrange("p h w -> p (h w)"),
                                         start=(n == 0), stop=(n == 2))
                last.then_inc(qkv_done, 1)

            def turn_unit(u, slot):
                wait(pe, normed, u + 1)
                wait(pe, qk_affine, u)
                turn4(bank[5], [qk_n[:, slot, c, :, :].rearrange("p t d -> p (t d)") for c in range(NC)])\
                    .then_inc(qkT_done, 1)

            def scores(g, u, c, slot):
                if c == 0:
                    wait(pe, k_lo_done, u + 1)
                    wait(pe, split_done, u + 1)
                wait(pe, exp_done, g - 1)
                q = q_s[:, slot, c * P:c * P + P]
                pe.matmul(bank[c % 2][:, :], q, k_s[:, slot, :], start=True, stop=False)
                pe.matmul(bank[c % 2][:, :], q, k_x[:, slot, :], start=False, stop=True)\
                  .then_inc(scores_done, 1)

            def turn_probs(g, c):
                wait(pe, exp_done, g + 1)
                wait(pe, (even_copied, odd_copied)[c % 2], half_before(g, c))
                turn4(bank[2 + c % 2], [probs[:, c % 2, k * P:k * P + P] for k in range(NC)])\
                    .then_inc(probsT_done, 1)

            def mix(g, u, c, slot):
                wait(pe, (even_copied, odd_copied)[c % 2], half_before(g, c) + 1)
                if c == 0:
                    wait(pe, v_copied, u + 1)
                    wait(pe, o_normed, u)
                for k in range(NC):
                    last = pe.matmul(bank[4][:, c * (HD + 1):(c + 1) * (HD + 1)], probs_T[:, c % 2, k, :],
                                     v_s[:, slot, k, :], start=(k == 0), stop=(k == NC - 1))
                last.then_inc(pv_done, 1)

            halves = {}

            def half_before(g, c):
                return halves[0] * 2 + c // 2

            def at_unit(u):
                halves[0] = u
                return u

            def body(i, first=False, last=False):
                for j in range(PER):
                    u = i * PER + j
                    for c in range(NC):
                        g = u * NC + c
                        if c == 0 and not (last and j >= PER - 2):
                            project(u + 2, j % B, 2 * i + (j + 2) // 2)
                        if c == 1 and not (last and j == PER - 1):
                            turn_unit(u + 1, (j + 1) % 2)
                        scores(g, u, c, j % 2)
                        if not (first and j == 0 and c < 2):
                            at_unit(u if c >= 2 else u - 1)
                            turn_probs(g - 2, (c - 2) % NC)
                        if not (first and j == 0 and c < 3):
                            back = u if c >= 3 else u - 1
                            at_unit(back)
                            mix(g - 3, back, (c - 3) % NC, j if c >= 3 else (j - 1) % PER)

            project(0, 0, 0)
            project(1, 1, 0)
            turn_unit(0, 0)
            body(0, first=True)
            with pe.Fori(1, STEPS - 1) as i:
                body(i)
            body(STEPS - 1, last=True)
            G = UNITS * NC
            at_unit(UNITS - 1)
            turn_probs(G - 2, 2)
            mix(G - 3, UNITS - 1, 1, PER - 1)
            turn_probs(G - 1, 3)
            mix(G - 2, UNITS - 1, 2, PER - 1)
            mix(G - 1, UNITS - 1, 3, PER - 1)

            def turn_out(t):
                if t < 2:
                    pe.wait_ge(o_normed, UNITS)
                else:
                    pe.wait_ge(oT_act, t - 1)
                    pe.wait_ge(oT_dve, t - 1)
                for half in range(2):
                    turn4(bank[2 * (t % 2) + half],
                          [o_all[:, t, (4 * half + c) * P:(4 * half + c + 1) * P] for c in range(4)])\
                        .then_inc(oT_done, 1)

            turn_out(0)
            for t in range(TC):
                if t + 1 < TC:
                    turn_out(t + 1)
                pe.wait_ge(oT_act, t + 1)
                pe.wait_ge(oT_dve, t + 1)
                wait(pe, att_ready, t - 1)
                for k in range(KC):
                    last = pe.matmul(bank[4 + t % 2][:, 0:D], oT[:, t % 2, k, :], wout_T[:, k, :],
                                     start=(k == 0), stop=(k == KC - 1))
                last.then_inc(out_done, 1)
            pe.wait_ge(att_ready, TC)
            for b in range(B):
                turn4(bank[6 + b], [x_att[:, b * NC + c, :] for c in range(NC)]).then_inc(xaT_done, 1)
            pe.wait_ge(xaT_act, 1)
            pe.wait_ge(xaT_dve, 1)
            for c in range(TC):
                last = pe.matmul(bank[5][:, c * E:c * E + E], xa_T[:, c * P:c * P + P], wgate_T[:, :],
                                 start=True, stop=True)
            last.then_inc(logits_done, 1)
            pe.wait_ge(fc_in, 48)
            for n in range(2 * E):
                wait(pe, fcT_copied, n - 3)
                src = [fc1_raw[:, n, c, :] for c in range(4)] if n < E else \
                    [fc2_raw[:, n - E, c * P:c * P + P] for c in range(4)]
                turn4(bank[1 + n % 4], src).then_inc(fcT_done, 1)

            with pe.Fori(0, BITS) as n:
                pe.wait_ge(cmp_done, n + 1)
                for c in range(TC):
                    last = pe.matmul(bank[0][:, 0:E], ones_bf[:, :], at_least[:, c, :],
                                     start=(c == 0), stop=(c == TC - 1))
                last.then_inc(count_done, 1)

            def before(at, mask, done):
                flat = lambda lo, hi: bank[0][:, at + lo * E:at + hi * E]
                pe.matmul(flat(0, TC), before_bf[:, :], mask[:, :, :].rearrange("p c e -> p (c e)"),
                          start=True, stop=False, skip_group_check=True)
                for c in range(TC - 1):
                    last = pe.matmul(flat(c + 1, TC).rearrange("p (c e) -> p c e", e=E), ones_bf[:, :],
                                     mask[:, c, :].unsqueeze(1).to_broadcast([P, TC - 1 - c, E]),
                                     start=False, stop=(c == TC - 2), skip_group_check=True)
                last.then_inc(done, 1)

            pe.wait_ge(masks_ready, 2)
            for c in range(TC):
                pe.matmul(bank[0][:, 0:E], ones_bf[:, :], above[:, c, :], start=(c == 0), stop=(c == TC - 1))
            before(64, ties, ranks_done)
            pe.wait_ge(taken_ready, 1)
            before(128, taken, slots_done)

            pe.wait_ge(tn_split, 1)
            pe.wait_ge(fcT_copied, 2 * E)
            for q in range(2):
                for c in range(TC):
                    if c < TC // 4 * 3:
                        pe.wait_ge(hot_dve, c + 1)
                    else:
                        pe.wait_ge(hot_pool, c + 1 - TC // 4 * 3)
                    for n, part in enumerate((tn_hi, tn_lo)):
                        last = pe.matmul(bank[1 + q][:, :], part[:, c, :],
                                         onehot[:, c, 4 * q:4 * q + 4, :].rearrange("p e n -> p (e n)"),
                                         start=(c == 0 and n == 0), stop=(c == TC - 1 and n == 1))
                last.then_inc(xg_done, 1)
            pe.wait_ge(gate_split, 1)
            pe.wait_ge(slots_ready, 1)
            for e in range(E):
                for c in range(TC):
                    last = pe.matmul(bank[0][:, 256 + 2 * e:258 + 2 * e], onehot[:, c, e, :], gate_r[:, c, e, :],
                                     start=(c == 0), stop=(c == TC - 1))
            last.then_inc(wslot_done, 1)

            def up(e):
                pe.wait_ge(xg_ready, 2 if e >= 2 or e < 2 else 1)
                wait(pe, gelu_done, e - 1)
                for c in range(DC):
                    last = pe.matmul(bank[1 + e % 2][:, c * CAP:c * CAP + CAP], fc1_T[:, e, c * P:c * P + P],
                                     xg[:, e, :], start=True, stop=True)
                last.then_inc(fc1_done, 1)

            def turn_hot(e):
                wait(pe, hotT_act, e)
                wait(pe, hotT_dve, e)
                for b, dst in enumerate((bank[5], bank[6])):
                    turn4(dst, [onehot[:, b * NC + c, e, :].bitcast(F32) for c in range(NC)])\
                        .then_inc(hotT_done, 1)

            def down(e):
                pe.wait_ge(gelu_done, e + 1)
                wait(pe, y_ready, e - 1)
                for c in range(DC):
                    last = pe.matmul(bank[3 + e % 2][:, 0:D], ug[:, e % 2, c, :], fc2_T[:, e, c, :],
                                     start=(c == 0), stop=(c == DC - 1))
                last.then_inc(fc2_done, 1)

            up(0)
            for e in range(E):
                if e + 1 < E:
                    up(e + 1)
                turn_hot(e)
                down(e)
            pe.wait_ge(y_ready, E)
            pe.wait_ge(hotT_act, E)
            pe.wait_ge(hotT_dve, E)
            for b, dst in enumerate((bank[7], bank[1])):
                for c in range(NC):
                    for e in range(E):
                        for n, part in enumerate((y_hi, y_lo)):
                            last = pe.matmul(dst[:, c * D:c * D + D],
                                             onehot_T[:, e, (b * NC + c) * P:(b * NC + c + 1) * P],
                                             part[:, e, :], start=(e == 0 and n == 0),
                                             stop=(e == E - 1 and n == 1))
                last.then_inc(sum_done, 1)


_INS = ['x', 'cond_1024'] + ['L0_cond_' + n for n in (
    'norm1_w', 'film1_w', 'film1_b', 'q_w', 'q_b', 'k_w', 'k_b', 'v_w', 'v_b', 'proj_w', 'proj_b', 'norm2_w',
    'film2_w', 'film2_b', 'mlp_w1', 'mlp_b1', 'mlp_w2', 'mlp_b2')] + ['L1_cond_' + n for n in (
        'W_ada', 'b_ada', 'ln1_g', 'ln1_b', 'Wqkv', 'qn_g', 'qn_b', 'kn_g', 'kn_b', 'Wout', 'mlp_g', 'mlp_b',
        'Wgate', 'fc1s', 'b1s', 'fc2s', 'b2s')]


def kernel(**inputs):
    import numpy as np
    import concourse.bacc as bacc
    from concourse.bass_utils import run_bass_kernel_spmd

    nc = bacc.Bacc("TRN2", target_bir_lowering=False, num_devices=1)
    arrays, args = {}, []
    for name in _INS:
        a = np.ascontiguousarray(inputs[name])
        arrays[f"in_{name}_dram"] = a
        args.append(nc.dram_tensor(f"in_{name}_dram", a.shape, mybir.dt.from_np(a.dtype),
                                   kind="ExternalInput").ap())
    args.append(nc.dram_tensor("out_dram", inputs["x"].shape, F32, kind="ExternalOutput").ap())
    film_attention_then_expert_choice(nc, *args)
    r = run_bass_kernel_spmd(nc, [arrays], core_ids=[0])
    return r.results[0]["out_dram"]
```

```python
from contextlib import ExitStack

import concourse.bass as bass
from concourse import mybir

P = 128
F32 = mybir.dt.float32
F32R = mybir.dt.float32r
BF16 = mybir.dt.bfloat16
I32 = mybir.dt.int32
ALU = mybir.AluOpType
ACT = mybir.ActivationFunctionType
AX = mybir.AxisListType.X
BYTES = {F32: 4, F32R: 4, BF16: 2, I32: 4}

ROWS = {}
for _name, _n in (("cond", 2), ("norm1_w", 1), ("film1_b", 2), ("q_b", 1), ("k_b", 1), ("norm2_w", 1),
                  ("film2_b", 2), ("mlp_b1", 4), ("b_ada", 1), ("ln1_g", 1), ("ln1_b", 1), ("kq_g", 1),
                  ("kq_b", 1), ("mlp_g", 1), ("mlp_b", 1), ("b1s", 32)):
    ROWS[_name] = (sum(n for _, n in ROWS.values()), _n)
NROWS = sum(n for _, n in ROWS.values())


def wait(eng, semaphore, value):
    if isinstance(value, int) and value <= 0:
        return
    eng.wait_ge(semaphore, value)


def spread(ap, shape):
    return ap.unsqueeze(len(shape) - 1).to_broadcast(shape)


def film_attention_then_expert_choice(
        nc, x, cond, norm1_w, film1_w, film1_b, q_w, q_b, k_w, k_b, v_w, v_b, proj_w, proj_b,
        norm2_w, film2_w, film2_b, mlp_w1, mlp_b1, mlp_w2, mlp_b2,
        W_ada, b_ada, ln1_g, ln1_b, Wqkv, qn_g, qn_b, kn_g, kn_b, Wout, mlp_g, mlp_b,
        Wgate, fc1s, b1s, fc2s, b2s, out):
    B, N, D = x.shape
    TOK = B * N
    TC = TOK // P
    NC = N // P
    HD = qn_g.shape[0]
    H = Wqkv.shape[0] // 3 // HD
    WC = Wqkv.shape[0] // P
    KC = H * HD // P
    HID = mlp_w1.shape[1]
    HC = HID // P
    E, DD, _ = fc1s.shape
    CAP = TOK // E
    DC = DD // P
    UNITS = H * B
    PER = 4
    STEPS = UNITS // PER
    EPS0, EPS1 = 1e-6, 1e-5
    BITS = 30
    DIGIT = 3
    CANDS = (1 << DIGIT) - 1
    DIGITS = BITS // DIGIT
    NOWHERE = 255.0
    assert D == P and CAP == P and B == 2 and NC == 4 and HD == 64 and HC == DC == 4 and E == 8

    ctx = ExitStack()
    with ctx:
        class Area:
            def __init__(self, start):
                self.at = start

            def __call__(self, name, shape, dt=F32):
                size = BYTES[dt]
                for n in shape[1:]:
                    size *= n
                t = nc.alloc_sbuf_tensor_at(name, shape, dt, offset=self.at)
                self.at += (size + 31) // 32 * 32
                return t

        def sem(name):
            return ctx.enter_context(nc.semaphore(name))

        bank = [ctx.enter_context(nc.psum_tensor(f"bank{i}", [P, 512], F32)) for i in range(6)]
        pair = ctx.enter_context(nc.psum_tensor("pair", [P, 2, 512], F32))
        bank += [pair[:, 0, :], pair[:, 1, :]]

        keep = Area((nc.sbuf_base + 31) // 32 * 32)
        ident = keep("ident", [P, P])
        ones_bf = keep("ones_bf", [P, P], BF16)
        before_bf = keep("before_bf", [P, P], BF16)
        iota_row = keep("iota_row", [P, P])
        minus_half = keep("minus_half", [P, TC])
        rows = keep("rows", [NROWS, P])
        cols = keep("cols", [P, NROWS])
        affine = keep("affine", [P, 3, 2, B])
        silu = keep("silu", [P, 3, B])
        b2_all = keep("b2_all", [P, E, D])
        x_blk = keep("x_blk", [P, TC, D])
        x_att = keep("x_att", [P, TC, D])
        wout_T = keep("wout_T", [P, KC, D])
        wgate_T = keep("wgate_T", [P, E])
        centre = keep("centre", [P, TC])
        sumsq = keep("sumsq", [P, TC])
        meansq = keep("meansq", [P, TC])
        rstd = keep("rstd", [P, TC])
        o_start = keep.at
        o_all = keep("o_all", [P, TC, H * HD])
        area_start = keep.at

        early = Area(area_start)
        x_in = early("x_in", [P, TC, D])
        h_T = early("h_T", [P, TOK])
        h_hi = early("h_hi", [P, TOK], F32R)
        h_lo = early("h_lo", [P, TOK], F32R)
        fc_start = early.at
        sq0 = early("sq0", [P, TC, D])
        xn = early("xn", [P, TC, D])
        mlp_start = early.at
        qT0 = early("qT0", [P, TOK])
        kT0 = early("kT0", [P, TOK])
        v0 = early("v0", [P, TC, D])
        oT0 = early("oT0", [P, TOK])
        u0 = Area(mlp_start)("u0", [P, HC, TOK])
        x_mid = early("x_mid", [P, TC, D])
        p0 = early("p0", [P, 2, N])
        pT0 = early("pT0", [P, 2, NC, P])
        soft0 = early("soft0", [P, TC, 3])
        film1 = early("film1", [P, 2 * D])
        film2 = early("film2", [P, 2 * D])
        wq0 = early("wq0", [P, D])
        wk0 = early("wk0", [P, D])
        wv0 = early("wv0", [P, D])
        wp0 = early("wp0", [P, D])
        w10 = early("w10", [P, HID])
        w20 = early("w20", [P, HC, D])
        wada = early("wada", [P, D])
        wada_T = early("wada_T", [P, D])
        wgate = early("wgate", [E, D])
        vb0 = early("vb0", [P, D])
        pb0 = early("pb0", [P, D])
        mb0 = early("mb0", [P, D])
        wqkv_raw = early("wqkv_raw", [P, WC, D])
        wqkv_T = early("wqkv_T", [P, H, 3, HD])
        wmean = early("wmean", [P, H, 2])

        experts = Area(fc_start)
        fc1_raw = experts("fc1_raw", [P, E, DC, D])
        fc2_raw = experts("fc2_raw", [P, E, DD])
        fc1_T = experts("fc1_T", [P, E, DD])
        fc2_T = experts("fc2_T", [P, E, DC, D])
        xg = experts("xg", [P, E, CAP])
        ug = experts("ug", [P, 2, DC, CAP])

        loop = Area(max(early.at, experts.at))
        w_hi = loop("w_hi", [P, H, 3 * HD], F32R)
        w_lo = loop("w_lo", [P, H, 3 * HD], F32R)
        loop2_start = loop.at
        qk_sq = loop("qk_sq", [P, NC, 2, HD])
        qk_ss = loop("qk_ss", [P, NC, 2])
        qk_ms = loop("qk_ms", [P, NC, 2])
        qk_rstd = loop("qk_rstd", [P, NC, 2])
        qk_n = loop("qk_n", [P, 2, NC, 2, HD])
        v_s = loop("v_s", [P, PER, NC, HD + 1])
        kq32 = loop("kq32", [P, N])
        q_s = loop("q_s", [P, 2, N], F32R)
        k_s = loop("k_s", [P, 2, N], F32R)
        lows = loop("lows", [P, 2, N], F32R)
        negmax = loop("negmax", [P, 4])
        probs = loop("probs", [P, 2, N])
        probs_T = loop("probs_T", [P, 2, NC, P])
        o_rec = loop("o_rec", [P, NC])
        oT = loop("oT", [P, 2, KC, P])

        moe = Area(loop2_start)
        moe2 = Area(loop2_start - 2 * 4 * H * 3 * HD)
        onehot_T = Area(o_start)("onehot_T", [P, E, TOK], F32R)
        onehot = moe("onehot", [P, TC, E, CAP], F32R)
        tn = moe2("tn", [P, TC, D])
        tn_hi = moe2("tn_hi", [P, TC, D], F32R)
        tn_lo = moe2("tn_lo", [P, TC, D], F32R)
        xa_T = moe2("xa_T", [P, TOK])
        tn_sq = moe2("tn_sq", [P, TC, D])
        y_hi = Area(area_start)("y_hi", [P, E, D], F32R)
        y_lo = Area(area_start + 4 * E * D)("y_lo", [P, E, D], F32R)
        y_sum = Area(area_start + 8 * E * D)("y_sum", [P, 2, D])
        final = Area(area_start + 12 * E * D)("final", [P, TC, D])
        sum_T = Area(area_start + 16 * E * D)("sum_T", [P, TOK])
        moe = Area(max(moe.at, loop.at))
        gate = moe("gate", [P, TC, E])
        gate_x = moe("gate_x", [P, TC, E])
        gate_m = moe("gate_m", [P, 2, TC])
        gate_r = moe("gate_r", [P, TC, E, 2], F32R)
        at_least = moe("at_least", [P, TC, CANDS, E], BF16)
        above = moe("above", [P, TC, E], BF16)
        ties = moe("ties", [P, TC, E], BF16)
        taken = moe("taken", [P, TC, E], BF16)
        rank = moe("rank", [P, TC, E])
        slot_of = moe("slot_of", [P, TC, E])
        need = moe("need", [P, E])
        thr = moe("thr", [P, E], I32)
        digit = moe("digit", [P, E], I32)
        cand = moe("cand", [P, CANDS, E], I32)
        next_offset = moe("next_offset", [P, CANDS, E], I32)
        hit = moe("hit", [P, CANDS, E])
        next_base = moe("next_base", [P, CANDS, E], I32)
        offset = moe("offset", [P, 2, CANDS, E])
        w_slot = moe("w_slot", [P, E])

        rows_in, films_in, wada_in, x_loaded, qkvo_in, bcast_in, mlp_in, wqkv_in, wout_in, fc_in = (
            sem(n) for n in ("rows_in", "films_in", "wada_in", "x_loaded", "qkvo_in", "bcast_in", "mlp_in",
                             "wqkv_in", "wout_in", "fc_in"))
        consts = sem("consts")
        act_step, dve_step, pool_step = sem("act_step"), sem("dve_step"), sem("pool_step")
        cols_T, cols_ready, cond_exp, silu_ready, ada_T, ada_copied, ada_done, affine_ready = (
            sem(n) for n in ("cols_T", "cols_ready", "cond_exp", "silu_ready", "ada_T",
                             "ada_copied", "ada_done", "affine_ready"))
        norm_in, norm_sq, norm_ss, norm_rstd, norm_done, norm_T, h_act, h_dve, h_split = (
            sem(n) for n in ("norm_in", "norm_sq", "norm_ss", "norm_rstd", "norm_done", "norm_T",
                             "h_act", "h_dve", "h_split"))
        xpb_ready, xmb_ready = sem("xpb_ready"), sem("xmb_ready")
        qkv0_done, q0_ready, k0_ready, v0_ready = (
            sem(n) for n in ("qkv0_done", "q0_ready", "k0_ready", "v0_ready"))
        s0_done, max0_done, exp0_done, p0_ready, pT0_done, pT0_copied, o0_done, o0_copied, proj0_done, mid_ready = (
            sem(n) for n in ("s0_done", "max0_done", "exp0_done", "p0_ready", "pT0_done", "pT0_copied",
                             "o0_done", "o0_copied", "proj0_done", "mid_ready"))
        u0_done, gelu0_done, y0_done = sem("u0_done"), sem("gelu0_done"), sem("y0_done")
        wT_done, wT_copied, w_summed, w_centred, w_split = (
            sem(n) for n in ("wT_done", "wT_copied", "w_summed", "w_centred", "w_split"))
        woT_done, woT_copied = sem("woT_done"), sem("woT_copied")
        qkv_done, sq_done, ss_done, rstd_done, normed, v_copied = (
            sem(n) for n in ("qkv_done", "sq_done", "ss_done", "rstd_done", "normed", "v_copied"))
        kqT_done, kq_affine, highs_done, lows_done, q_hi_moved, split_done, o_normed = (
            sem(n) for n in ("kqT_done", "kq_affine", "highs_done", "lows_done", "q_hi_moved", "split_done",
                             "o_normed"))
        o_rec_done = sem("o_rec_done")
        sq_summed = sem("sq_summed")
        scores_done, max_done, exp_done, probsT_done, probs_copied, pv_done = (
            sem(n) for n in ("scores_done", "max_done", "exp_done", "probsT_done", "probs_copied", "pv_done"))
        oT_done, oT_act, oT_dve, out_done, att_ready = (
            sem(n) for n in ("oT_done", "oT_act", "oT_dve", "out_done", "att_ready"))
        xaT_done, xaT_act, xaT_dve, logits_done, logits_sub, gate_exp, gate_ready = (
            sem(n) for n in ("xaT_done", "xaT_act", "xaT_dve", "logits_done", "logits_sub", "gate_exp",
                             "gate_ready"))
        tn_centred, tn_squared, tn_ss, tn_split = (
            sem(n) for n in ("tn_centred", "tn_squared", "tn_ss", "tn_split"))
        digit_step, cmp_done, count_done = sem("digit_step"), sem("cmp_done"), sem("count_done")
        masks_ready, ranks_done, taken_ready, slots_done, slots_ready, hot_dve, hot_pool, gate_split = (
            sem(n) for n in ("masks_ready", "ranks_done", "taken_ready", "slots_done", "slots_ready",
                             "hot_dve", "hot_pool", "gate_split"))
        fcT_done, fcT_copied = sem("fcT_done"), sem("fcT_copied")
        xg_done, xg_ready, wslot_done, wslot_ready, hotT_done, hotT_copied = (
            sem(n) for n in ("xg_done", "xg_ready", "wslot_done", "wslot_ready", "hotT_done",
                             "hotT_copied"))
        sum_copied, sumT_done = sem("sum_copied"), sem("sumT_done")
        fc1_done, gelu_done, fc2_done, y_ready, sum_done, final_ready, stored = (
            sem(n) for n in ("fc1_done", "gelu_done", "fc2_done", "y_ready", "sum_done", "final_ready",
                             "stored"))

        def col(name, i=0):
            return cols[:, ROWS[name][0] + i:ROWS[name][0] + i + 1]

        N_ROW_DMAS = 18

        block = ctx.enter_context(nc.Block())

        @block.sync
        def _(sp):
            def row(name, src, n=None, at=0):
                r = ROWS[name][0] + at
                sp.dma_start(rows[r:r + (n or ROWS[name][1]), :], src).then_inc(rows_in, 16)

            as_row = lambda v: v.rearrange("(a d) -> a d", d=P)
            row("cond", cond)
            for name, v in (("norm1_w", norm1_w), ("film1_b", film1_b), ("q_b", q_b), ("k_b", k_b),
                            ("norm2_w", norm2_w), ("film2_b", film2_b), ("mlp_b1", mlp_b1), ("b_ada", b_ada),
                            ("ln1_g", ln1_g), ("ln1_b", ln1_b), ("mlp_g", mlp_g), ("mlp_b", mlp_b)):
                row(name, as_row(v))
            row("b1s", b1s.rearrange("e (a d) -> (e a) d", d=P))
            for name, parts in (("kq_g", (kn_g, qn_g)), ("kq_b", (kn_b, qn_b))):
                r = ROWS[name][0]
                for half, v in enumerate(parts):
                    sp.dma_start(rows[r:r + 1, half * HD:half * HD + HD],
                                 v.rearrange("(a d) -> a d", a=1)).then_inc(rows_in, 16)
            sp.dma_start(film1[:, :], film1_w).then_inc(films_in, 16)
            sp.dma_start(film2[:, :], film2_w).then_inc(films_in, 16)
            sp.dma_start(wada[:, :], W_ada).then_inc(wada_in, 16)
            for t, src in ((wq0, q_w), (wk0, k_w), (wv0, v_w), (wp0, proj_w)):
                sp.dma_start(t[:, :], src).then_inc(qkvo_in, 16)
            for t, src in ((vb0, v_b), (pb0, proj_b), (mb0, mlp_b2)):
                sp.dma_start(t[:, :], src.rearrange("(a d) -> a d", a=1).to_broadcast([P, D]))\
                  .then_inc(bcast_in, 16)
            sp.dma_start(w10[:, :], mlp_w1).then_inc(mlp_in, 16)
            sp.dma_start(w20[:, :, :], mlp_w2.rearrange("(c p) d -> p c d", p=P)).then_inc(mlp_in, 16)
            sp.dma_start(o_all[:, 0, :], Wout).then_inc(wout_in, 16)
            sp.dma_start(wgate[:, :], Wgate).then_inc(wout_in, 16)
            sp.dma_start(b2_all[:, :, :], b2s.unsqueeze(0).to_broadcast([P, E, D])).then_inc(fc_in, 16)
            sp.wait_ge(qkv_done, 1)
            sp.wait_ge(h_split, 1)
            sp.wait_ge(w_split, 1)
            sp.dma_start(fc1_raw[:, :, :, :], fc1s.rearrange("e (c p) d -> p e c d", p=P)).then_inc(fc_in, 16)
            sp.dma_start(fc2_raw[:, :, :], fc2s.rearrange("e d h -> d e h")).then_inc(fc_in, 16)
            for half in range(2):
                sp.wait_ge(final_ready, half + 1)
                sp.dma_start(out[half].rearrange("(c p) d -> p c d", p=P),
                             final[:, half * NC:half * NC + NC, :]).then_inc(stored, 16)
            sp.wait_ge(stored, 32)

        @block.gpsimd
        def _(pool):
            steps = [0]

            def link(ins):
                steps[0] += 1
                ins.then_inc(pool_step, 1)
                pool.wait_ge(pool_step, steps[0])

            link(pool.memset(ident[:, :], 0.0))
            pool.affine_select(out=ident[:, :], in_=ident[:, :], compare_op=ALU.not_equal, fill=1.0, base=0,
                               pattern=[[-1, P]], channel_multiplier=1).then_inc(consts, 1)
            pool.memset(minus_half[:, :], -0.5).then_inc(consts, 1)
            link(pool.memset(ones_bf[:, :], 1.0))
            pool.affine_select(out=before_bf[:, :], in_=ones_bf[:, :], compare_op=ALU.is_gt, fill=0.0, base=0,
                               pattern=[[1, P]], channel_multiplier=-1).then_inc(consts, 1)
            pool.iota(iota_row[:, :], [[1, P]], base=0, channel_multiplier=0,
                      allow_small_or_imprecise_dtypes=True).then_inc(consts, 1)
            pool.memset(v_s[:, :, :, HD:HD + 1], 1.0).then_inc(consts, 1)
            pool.wait_ge(consts, 2)

            def norm_scale(k, eps):
                pool.wait_ge(norm_ss, k + 1)
                link(pool.tensor_scalar(meansq[:, :], sumsq[:, :], 1.0 / D, eps, ALU.mult, ALU.add))
                pool.tensor_tensor(rstd[:, :], meansq[:, :], minus_half[:, :], ALU.pow).then_inc(norm_rstd, 1)

            norm_scale(0, EPS0)
            pool.wait_ge(x_loaded, 16)
            pool.wait_ge(bcast_in, 48)
            pool.wait_ge(norm_done, 1)
            bias = lambda t: t[:, :].unsqueeze(1).to_broadcast([P, TC, D])
            pool.tensor_tensor(x_in[:, :, :], x_in[:, :, :], bias(pb0), ALU.add).then_inc(xpb_ready, 1)
            norm_scale(1, EPS0)
            pool.wait_ge(norm_done, 2)
            pool.tensor_tensor(x_mid[:, :, :], x_mid[:, :, :], bias(mb0), ALU.add).then_inc(xmb_ready, 1)
            pool.wait_ge(w_summed, 1)
            for t in range(2):
                last = pool.tensor_tensor(wqkv_T[:, :, t, :], wqkv_T[:, :, t, :],
                                          spread(wmean[:, :, t], [P, H, HD]), ALU.add)
            last.then_inc(w_centred, 1)
            pool.wait_ge(w_centred, 2)
            pool.tensor_tensor(w_lo[:, :, :], wqkv_T[:, :, :, :].rearrange("p h t d -> p h (t d)"),
                               w_hi[:, :, :].bitcast(F32), ALU.subtract).then_inc(w_split, 1)
            norm_scale(2, EPS1)

            def unit_scale(u):
                wait(pool, ss_done, u + 1)
                wait(pool, normed, u)
                wait(pool, lows_done, u)
                pool.tensor_tensor(qk_rstd[:, :, :].rearrange("p c t -> p (c t)"),
                                   qk_ms[:, :, :].rearrange("p c t -> p (c t)"),
                                   minus_half[:, 0:2 * NC], ALU.pow).then_inc(rstd_done, 1)

            def unit_low(u, slot):
                wait(pool, highs_done, u + 1)
                wait(pool, split_done, u - 1)
                wait(pool, scores_done, 4 * u - 4)
                pool.tensor_tensor(lows[:, slot, :], kq32[:, :], k_s[:, slot, :].bitcast(F32),
                                   ALU.subtract).then_inc(lows_done, 1)

            def body(i, last=False):
                for j in range(PER):
                    u = i * PER + j
                    if not (last and j == PER - 1):
                        unit_low(u + 1, (j + 1) % 2)
                    if not (last and j >= PER - 2):
                        unit_scale(u + 2)

            unit_scale(0)
            unit_low(0, 0)
            unit_scale(1)
            body(0)
            with pool.Fori(1, STEPS - 1) as i:
                body(i)
            body(STEPS - 1, last=True)

            pool.wait_ge(tn_centred, 1)
            pool.tensor_tensor(tn[:, :, :], x_att[:, :, :], spread(centre[:, :], [P, TC, D]), ALU.add)\
                .then_inc(tn_centred, 1)
            pool.wait_ge(tn_ss, 1)
            link(pool.tensor_scalar(meansq[:, :], sumsq[:, :], 1.0 / D, EPS1, ALU.mult, ALU.add))
            link(pool.tensor_tensor(rstd[:, :], meansq[:, :], minus_half[:, :], ALU.pow))
            link(pool.tensor_tensor(tn[:, :, :], tn[:, :, :], spread(rstd[:, :], [P, TC, D]), ALU.mult))
            link(pool.tensor_copy(tn_hi[:, :, :], tn[:, :, :]))
            pool.tensor_tensor(tn_lo[:, :, :], tn[:, :, :], tn_hi[:, :, :].bitcast(F32), ALU.subtract)\
                .then_inc(tn_split, 1)
            pool.wait_ge(slots_ready, 1)
            for c in range(TC // 4 * 3, TC):
                for e in range(E):
                    last = pool.tensor_scalar(onehot[:, c, e, :], iota_row[:, :], slot_of[:, c, e:e + 1], None,
                                              ALU.is_equal)
                last.then_inc(hot_pool, 1)

        @block.scalar
        def _(act):
            act.dma_start(x_in[:, :, :], x.rearrange("b (c p) d -> p (b c) d", p=P)).then_inc(x_loaded, 16)
            act.dma_start(wqkv_raw[:, :, :], Wqkv.rearrange("(c p) d -> p c d", p=P)).then_inc(wqkv_in, 16)
            act.wait_ge(x_loaded, 16)
            act.activation(sq0[:, :, :], x_in[:, :, :], ACT.Square).then_inc(norm_sq, 1)
            act.wait_ge(cols_ready, 1)
            act.activation(silu[:, 0, :], cols[:, 0:B], ACT.Exp, scale=-1.0).then_inc(cond_exp, 1)

            def into_h(k):
                act.wait_ge(norm_T, 2 * k + 1)
                if k == 0:
                    act.wait_ge(affine_ready, 1)
                act.activation(h_T[:, 0:N], bank[1][:, :], ACT.Identity, bias=affine[:, k, 1, 0:1],
                               scale=affine[:, k, 0, 0:1]).then_inc(h_act, 1)

            into_h(0)
            for b in range(B):
                act.wait_ge(qkv0_done, 3 * b + 2)
                act.activation(kT0[:, b * N:b * N + N], bank[5 + b][:, :], ACT.Identity, bias=col("k_b"))\
                   .then_inc(k0_ready, 1)

            def turned0(g):
                act.wait_ge(pT0_done, g + 1)
                wait(act, o0_done, g - 1)
                act.activation(pT0[:, g % 2, :, :].rearrange("p c n -> p (c n)"), bank[3 + g % 2][:, :],
                               ACT.Copy).then_inc(pT0_copied, 1)

            for g in range(TC):
                act.wait_ge(max0_done, g + 1)
                wait(act, pT0_done, g - 1)
                act.activation(p0[:, g % 2, :], bank[1 + g % 2][:, :], ACT.Exp, bias=soft0[:, g, 0:1],
                               accum_out=soft0[:, g, 1:2]).then_inc(exp0_done, 1)
                if g:
                    turned0(g - 1)
            turned0(TC - 1)
            act.wait_ge(mid_ready, 2)
            act.activation(sq0[:, :, :], x_mid[:, :, :], ACT.Square).then_inc(norm_sq, 1)
            for n in range(WC // 4 + KC // 4):
                if n < WC // 4:
                    act.wait_ge(wT_done, n + 1)
                    kind, h0 = (1, 0, 2)[n * 4 // KC], n * 8 % H
                    act.activation(wqkv_T[:, h0:h0 + 8, kind, :],
                                   bank[(6, 7)[n % 2]][:, :].rearrange("p (h d) -> p h d", d=HD), ACT.Copy)\
                       .then_inc(wT_copied, 1)
                else:
                    act.wait_ge(wT_done, n + 1)
                    m = n - WC // 4
                    act.activation(wout_T[:, 4 * m:4 * m + 4, :].rearrange("p c d -> p (c d)"),
                                   bank[(6, 7)[n % 2]][:, :], ACT.Copy).then_inc(wT_copied, 1)
            act.wait_ge(wT_done, WC // 4 + KC // 4 + 1)
            act.activation(wgate_T[:, :], bank[6][:, 0:E], ACT.Copy).then_inc(wT_copied, 1)
            into_h(1)
            for n in range(B * HC):
                b, c = n // HC, n % HC
                act.wait_ge(u0_done, n + 1)
                act.activation(u0[:, c, b * N:b * N + N], bank[3 + n % 2][:, :], ACT.Gelu,
                               bias=col("mlp_b1", c)).then_inc(gelu0_done, 1)
            act.wait_ge(norm_in, 1)
            act.activation(sq0[:, :, :], xn[:, :, :], ACT.Square).then_inc(norm_sq, 1)
            into_h(2)

            qkv = pair[:, :, :].rearrange("p a (c w) -> p (a c) w", c=2)

            def unit_in(u, j):
                wait(act, qkv_done, u + 1)
                wait(act, sq_summed, u)
                act.activation(qk_sq[:, :, :, :].rearrange("p c t d -> p c (t d)"), qkv[:, :, 0:2 * HD],
                               ACT.Square).then_inc(sq_done, 1)
                wait(act, pv_done, 4 * u - 12)
                act.activation(v_s[:, j % PER, :, 0:HD], qkv[:, :, 2 * HD:3 * HD], ACT.Copy)\
                   .then_inc(v_copied, 1)

            def unit_affine(u):
                wait(act, kqT_done, u + 1)
                wait(act, lows_done, u)
                act.activation(kq32[:, :], bank[5][:, :], ACT.Identity, bias=col("kq_b"), scale=col("kq_g"))\
                   .then_inc(kq_affine, 1)

            def chunk_exp(g, c):
                wait(act, max_done, g + 1)
                wait(act, probsT_done, g - 1)
                act.activation(probs[:, c % 2, :], bank[c % 2][:, :], ACT.Exp, bias=negmax[:, c:c + 1])\
                   .then_inc(exp_done, 1)

            def copy_probs(g, c):
                wait(act, probsT_done, g + 1)
                wait(act, pv_done, g - 1)
                act.activation(probs_T[:, c % 2, :, :].rearrange("p c n -> p (c n)"), bank[2 + c % 2][:, :],
                               ACT.Copy).then_inc(probs_copied, 1)

            def body(i, first=False, last=False):
                for j in range(PER):
                    u = i * PER + j
                    for c in range(NC):
                        g = u * NC + c
                        if c == 0 and not (last and j == PER - 1):
                            unit_affine(u + 1)
                        if c == 1 and not (last and j >= PER - 2):
                            unit_in(u + 2, j + 2)
                        if not (first and j == 0 and c < 2):
                            copy_probs(g - 2, c)
                        chunk_exp(g, c)

            unit_in(0, 0)
            unit_in(1, 1)
            unit_affine(0)
            body(0, first=True)
            with act.Fori(1, STEPS - 1) as i:
                body(i)
            body(STEPS - 1, last=True)
            copy_probs(UNITS * NC - 2, 0)
            copy_probs(UNITS * NC - 1, 1)

            for t in range(TC):
                act.wait_ge(oT_done, 2 * t + 1)
                wait(act, out_done, t - 1)
                act.activation(oT[:, t % 2, 0:4, :].rearrange("p c n -> p (c n)"), bank[2 * (t % 2)][:, :],
                               ACT.Copy).then_inc(oT_act, 1)
            act.wait_ge(xaT_done, 1)
            act.activation(xa_T[:, 0:N], bank[6], ACT.Copy).then_inc(xaT_act, 1)
            act.wait_ge(logits_sub, 1)
            act.activation(gate_x[:, :, :], gate_x[:, :, :], ACT.Exp).then_inc(gate_exp, 1)
            act.wait_ge(tn_centred, 2)
            act.activation(tn_sq[:, :, :], tn[:, :, :], ACT.Square).then_inc(tn_squared, 1)
            for n in range(2 * E):
                act.wait_ge(fcT_done, n + 1)
                dst = fc1_T[:, n, :] if n < E else fc2_T[:, n - E, :, :].rearrange("p c d -> p (c d)")
                act.activation(dst, bank[1 + n % 4][:, :], ACT.Copy).then_inc(fcT_copied, 1)
            for c in range(TC):
                for q in range(2):
                    act.wait_ge(hotT_done, 2 * c + q + 1)
                    act.activation(onehot_T[:, 4 * q:4 * q + 4, c * P:c * P + P],
                                   bank[5 + q][:, :].rearrange("p (e n) -> p e n", e=4), ACT.Copy)\
                       .then_inc(hotT_copied, 1)
                    if c == TC - 1:
                        act.wait_ge(xg_done, q + 1)
                        act.activation(xg[:, 4 * q:4 * q + 4, :].rearrange("p e n -> p (e n)"),
                                       bank[1 + q][:, :], ACT.Identity, bias=col("mlp_b"),
                                       scale=col("mlp_g")).then_inc(xg_ready, 1)
            for e in range(E):
                act.wait_ge(fc1_done, e + 1)
                wait(act, fc2_done, e - 1)
                for c in range(DC):
                    last = act.activation(ug[:, e % 2, c, :], bank[1 + e % 2][:, c * CAP:c * CAP + CAP],
                                          ACT.Gelu_apprx_tanh, bias=col("b1s", e * DC + c))
                last.then_inc(gelu_done, 1)
            act.wait_ge(sum_done, 1)
            act.activation(sum_T[:, 0:N], bank[7], ACT.Copy).then_inc(sum_copied, 1)

        @block.vector
        def _(dve):
            steps = [0]

            def link(ins):
                steps[0] += 1
                ins.then_inc(dve_step, 1)
                dve.wait_ge(dve_step, steps[0])

            def sum_squares(k, sq):
                dve.wait_ge(norm_sq, k + 1)
                dve.tensor_reduce(sumsq[:, :], sq[:, :, :], AX, ALU.add).then_inc(norm_ss, 1)

            def scaled(k, src):
                dve.wait_ge(norm_rstd, k + 1)
                dve.tensor_tensor(xn[:, :, :], src[:, :, :], spread(rstd[:, :], [P, TC, D]), ALU.mult)\
                   .then_inc(norm_done, 1)

            def into_h(k):
                dve.wait_ge(norm_T, 2 * k + 2)
                dve.tensor_scalar(h_T[:, N:TOK], bank[2][:, :], affine[:, k, 0, 1:2], affine[:, k, 1, 1:2],
                                  ALU.mult, ALU.add).then_inc(h_dve, 1)

            sum_squares(0, sq0)
            dve.wait_ge(cols_T, 1)
            link(dve.tensor_copy(cols[:, :], bank[0][:, 0:NROWS]))
            r = ROWS["kq_g"][0]
            dve.tensor_scalar(cols[HD:P, r:r + 2], cols[HD:P, r:r + 2], float(HD) ** -0.5, None, ALU.mult)\
               .then_inc(cols_ready, 1)
            dve.wait_ge(ada_T, 1)
            dve.tensor_copy(wada_T[:, :], bank[3][:, 0:P]).then_inc(ada_copied, 1)
            dve.wait_ge(cond_exp, 1)
            link(dve.tensor_scalar(silu[:, 0, :], silu[:, 0, :], 1.0, None, ALU.add))
            link(dve.reciprocal(silu[:, 1, :], silu[:, 0, :]))
            dve.tensor_tensor(silu[:, 2, :], silu[:, 1, :], cols[:, 0:B], ALU.mult).then_inc(silu_ready, 1)
            scaled(0, x_in)
            dve.wait_ge(ada_done, 1)
            for k, (fb, w) in enumerate((("film1_b", "norm1_w"), ("film2_b", "norm2_w"))):
                film = bank[4][:, 4 * k:4 * k + 4]
                link(dve.tensor_scalar(affine[:, k, 0, :], film[:, 0:B], col(fb), 1.0, ALU.add, ALU.add))
                dve.tensor_scalar(affine[:, k, 0, :], affine[:, k, 0, :], col(w), None, ALU.mult)
                dve.tensor_scalar(affine[:, k, 1, :], film[:, B:2 * B], col(fb, 1), None, ALU.add)
            for b in range(B):
                dve.tensor_copy(affine[:, 2, 0, b:b + 1], col("ln1_g"))
            link(dve.tensor_scalar(affine[:, 2, 1, :], bank[4][:, 8:8 + B], col("b_ada"), col("ln1_b"),
                                   ALU.add, ALU.add))
            dve.tensor_copy(silu[:, 0, :], silu[:, 2, :]).then_inc(affine_ready, 1)
            into_h(0)
            dve.wait_ge(bcast_in, 48)
            for b in range(B):
                dve.wait_ge(qkv0_done, 3 * b + 1)
                dve.tensor_scalar(qT0[:, b * N:b * N + N], bank[3 + b][:, :], col("q_b"), float(D) ** -0.5,
                                  ALU.add, ALU.mult).then_inc(q0_ready, 1)
                dve.wait_ge(qkv0_done, 3 * b + 3)
                dve.tensor_tensor(v0[:, b * NC:b * NC + NC, :],
                                  bank[(7, 0)[b]][:, :].rearrange("p (c d) -> p c d", d=D),
                                  vb0[:, :].unsqueeze(1).to_broadcast([P, NC, D]), ALU.add).then_inc(v0_ready, 1)

            def attended0(b):
                dve.wait_ge(o0_done, NC * (b + 1))
                dve.tensor_copy(oT0[:, b * N:b * N + N], bank[5 + b][:, :]).then_inc(o0_copied, 1)

            def batch_out0(b):
                dve.wait_ge(proj0_done, b + 1)
                dve.wait_ge(xpb_ready, 1)
                dve.tensor_tensor(x_mid[:, b * NC:b * NC + NC, :], x_in[:, b * NC:b * NC + NC, :],
                                  bank[(7, 0)[b]][:, :].rearrange("p (c d) -> p c d", d=D), ALU.add)\
                   .then_inc(mid_ready, 1)

            for g in range(TC + 1):
                if g < TC:
                    dve.wait_ge(s0_done, g + 1)
                    dve.tensor_reduce(soft0[:, g, 0:1], bank[1 + g % 2][:, :], AX, ALU.max, negate=True)\
                       .then_inc(max0_done, 1)
                if g:
                    k = g - 1
                    dve.wait_ge(exp0_done, k + 1)
                    link(dve.reciprocal(soft0[:, k, 2:3], soft0[:, k, 1:2]))
                    dve.tensor_scalar(p0[:, k % 2, :], p0[:, k % 2, :], soft0[:, k, 2:3], None, ALU.mult)\
                       .then_inc(p0_ready, 1)
                if g == NC + 2:
                    attended0(0)
                if g == NC + 4:
                    batch_out0(0)
            attended0(1)
            batch_out0(1)
            sum_squares(1, sq0)
            scaled(1, x_mid)
            into_h(1)
            dve.wait_ge(wT_copied, WC // 4)
            link(dve.tensor_reduce(wmean[:, :, :], wqkv_T[:, :, 0:2, :], AX, ALU.add, negate=True))
            dve.tensor_scalar(wmean[:, :, :], wmean[:, :, :], 1.0 / HD, None, ALU.mult).then_inc(w_summed, 1)
            dve.wait_ge(w_centred, 1)
            dve.tensor_copy(w_hi[:, :, :], wqkv_T[:, :, :, :].rearrange("p h t d -> p h (t d)"))\
               .then_inc(w_centred, 1)
            for b in range(B):
                dve.wait_ge(y0_done, b + 1)
                dve.wait_ge(xmb_ready, 1)
                dve.tensor_tensor(x_blk[:, b * NC:b * NC + NC, :], x_mid[:, b * NC:b * NC + NC, :],
                                  bank[(7, 0)[b]][:, :].rearrange("p (c d) -> p c d", d=D), ALU.add)\
                   .then_inc(dve_step, 1)
                steps[0] += 1
            dve.wait_ge(dve_step, steps[0])
            link(dve.tensor_reduce(centre[:, :], x_blk[:, :, :], AX, ALU.add, negate=True))
            link(dve.tensor_scalar(centre[:, :], centre[:, :], 1.0 / D, None, ALU.mult))
            dve.tensor_tensor(xn[:, :, :], x_blk[:, :, :], spread(centre[:, :], [P, TC, D]), ALU.add)\
               .then_inc(norm_in, 1)
            sum_squares(2, sq0)
            scaled(2, xn)
            into_h(2)
            dve.wait_ge(h_act, 3)
            dve.wait_ge(h_dve, 3)
            link(dve.tensor_copy(h_hi[:, :], h_T[:, :]))
            dve.tensor_tensor(h_lo[:, :], h_T[:, :], h_hi[:, :].bitcast(F32), ALU.subtract)\
               .then_inc(h_split, 1)

            qkv = pair[:, :, :].rearrange("p a (c w) -> p (a c) w", c=2)

            def unit_ss(u):
                wait(dve, sq_done, u + 1)
                dve.tensor_reduce(qk_ss[:, :, :], qk_sq[:, :, :, :], AX, ALU.add).then_inc(sq_summed, 1)
                wait(dve, sq_summed, u + 1)
                wait(dve, rstd_done, u)
                dve.tensor_scalar(qk_ms[:, :, :], qk_ss[:, :, :], 1.0 / HD, EPS1, ALU.mult, ALU.add)\
                   .then_inc(ss_done, 1)

            def unit_norm(u, slot):
                wait(dve, rstd_done, u + 1)
                wait(dve, v_copied, u + 1)
                wait(dve, kqT_done, u - 1)
                dve.tensor_tensor(qk_n[:, slot, :, :, :],
                                  qkv[:, :, 0:2 * HD].rearrange("p c (t d) -> p c t d", d=HD),
                                  spread(qk_rstd[:, :, :], [P, NC, 2, HD]), ALU.mult).then_inc(normed, 1)

            def unit_high(u, slot):
                wait(dve, kq_affine, u + 1)
                wait(dve, scores_done, 4 * u - 4)
                dve.tensor_copy(k_s[:, slot, :], kq32[:, :]).then_inc(highs_done, 1)
                wait(dve, highs_done, u + 1)
                dve.tensor_copy(q_s[0:HD, slot, :], k_s[HD:P, slot, :].bitcast(F32)).then_inc(q_hi_moved, 1)

            def unit_low(u, slot):
                wait(dve, lows_done, u + 1)
                dve.tensor_copy(q_s[HD:P, slot, :], lows[HD:P, slot, :].bitcast(F32))
                wait(dve, q_hi_moved, u + 1)
                dve.tensor_copy(k_s[HD:P, slot, :], k_s[0:HD, slot, :].bitcast(F32)).then_inc(split_done, 1)

            def chunk_max(g, s):
                wait(dve, scores_done, g + 1)
                dve.tensor_reduce(negmax[:, s:s + 1], bank[s % 2][:, :], AX, ALU.max, negate=True)\
                   .then_inc(max_done, 1)

            def unit_out(u, j, head):
                o = bank[4][:, 0:NC * (HD + 1)].rearrange("p (c w) -> p c w", c=NC)
                wait(dve, pv_done, 4 * u + 4)
                dve.reciprocal(o_rec[:, :], o[:, :, HD]).then_inc(o_rec_done, 1)
                wait(dve, o_rec_done, u + 1)
                b = j % B
                dve.tensor_tensor(o_all[:, b * NC:b * NC + NC, bass.ds(head * HD, HD)], o[:, :, 0:HD],
                                  spread(o_rec[:, :], [P, NC, HD]), ALU.mult).then_inc(o_normed, 1)

            def body(i, first=False, last=False):
                for j in range(PER):
                    u = i * PER + j
                    for c in range(NC):
                        g = u * NC + c
                        if c == 3 and not (first and j == 0):
                            unit_out(u - 1, j + 1, 2 * i + (j + 3) // 2 - 2)
                        chunk_max(g, c)
                        if c == 0 and not (last and j == PER - 1):
                            unit_high(u + 1, (j + 1) % 2)
                        if c == 1 and not (last and j >= PER - 2):
                            unit_ss(u + 2)
                        if c == 2 and not (last and j == PER - 1):
                            unit_low(u + 1, (j + 1) % 2)
                        if c == 3 and not (last and j >= PER - 2):
                            unit_norm(u + 2, j % 2)

            unit_ss(0)
            unit_norm(0, 0)
            unit_ss(1)
            unit_high(0, 0)
            unit_low(0, 0)
            unit_norm(1, 1)
            body(0, first=True)
            with dve.Fori(1, STEPS - 1) as i:
                body(i)
            body(STEPS - 1, last=True)
            unit_out(UNITS - 1, PER - 1, H - 1)

            for t in range(TC + 1):
                if t < TC:
                    dve.wait_ge(oT_done, 2 * t + 2)
                    wait(dve, out_done, t - 1)
                    dve.tensor_copy(oT[:, t % 2, 4:8, :].rearrange("p c n -> p (c n)"),
                                    bank[2 * (t % 2) + 1][:, :]).then_inc(oT_dve, 1)
                if t:
                    dve.wait_ge(out_done, t)
                    dve.tensor_tensor(x_att[:, t - 1, :], x_blk[:, t - 1, :], bank[4 + (t - 1) % 2][:, 0:D],
                                      ALU.add).then_inc(att_ready, 1)
            dve.wait_ge(att_ready, TC)
            link(dve.tensor_reduce(centre[:, :], x_att[:, :, :], AX, ALU.add, negate=True))
            dve.tensor_scalar(centre[:, :], centre[:, :], 1.0 / D, None, ALU.mult).then_inc(tn_centred, 1)
            dve.wait_ge(xaT_done, 2)
            dve.tensor_copy(xa_T[:, N:TOK], bank[7]).then_inc(xaT_dve, 1)
            logits = bank[5][:, 0:TC * E].rearrange("p (c e) -> p c e", e=E)
            dve.wait_ge(logits_done, 1)
            link(dve.tensor_reduce(gate_m[:, 0, :], logits, AX, ALU.max))
            dve.tensor_tensor(gate_x[:, :, :], logits, spread(gate_m[:, 0, :], [P, TC, E]), ALU.subtract)\
               .then_inc(logits_sub, 1)
            dve.wait_ge(gate_exp, 1)
            link(dve.tensor_reduce(gate_m[:, 0, :], gate_x[:, :, :], AX, ALU.add))
            link(dve.reciprocal(gate_m[:, 1, :], gate_m[:, 0, :]))
            link(dve.tensor_tensor(gate[:, :, :], gate_x[:, :, :], spread(gate_m[:, 1, :], [P, TC, E]), ALU.mult))
            link(dve.tensor_copy(gate_r[:, :, :, 0], gate[:, :, :]))
            dve.wait_ge(tn_squared, 1)
            dve.tensor_reduce(sumsq[:, :], tn_sq[:, :, :], AX, ALU.add).then_inc(tn_ss, 1)
            dve.tensor_tensor(gate_r[:, :, :, 1], gate[:, :, :], gate_r[:, :, :, 0].bitcast(F32), ALU.subtract)\
               .then_inc(gate_split, 1)

            over = lambda t: t.unsqueeze(1).to_broadcast([P, TC, E])
            for c in range(CANDS):
                start = (c + 1) << (BITS - DIGIT)
                dve.memset(offset[:, 0, c, :], float(start)).then_inc(digit_step, 1)
                dve.memset(cand[:, c, :], start).then_inc(digit_step, 1)
            dve.memset(thr[:, :], 0).then_inc(digit_step, 1)
            counts = bank[0][:, 0:CANDS * E].rearrange("p (c e) -> p c e", e=E)
            INITS, OPS = 1 + 2 * CANDS, 7

            def settle(n, slot):
                done = INITS + OPS * n
                dve.wait_ge(digit_step, done - 1)
                for half in range(2):
                    at = slice(half * NC, half * NC + NC)
                    dve.tensor_tensor(at_least[:, at, :, :],
                                      gate[:, at, :].unsqueeze(2).to_broadcast([P, NC, CANDS, E]),
                                      cand[:, :, :].bitcast(F32).unsqueeze(1).to_broadcast([P, NC, CANDS, E]),
                                      ALU.is_ge).then_inc(cmp_done, 1)
                dve.tensor_scalar(next_offset[:, :, :], offset[:, slot, :, :], 1.0 / (1 << DIGIT), None,
                                  ALU.mult).then_inc(digit_step, 1)
                dve.tensor_scalar(offset[:, 1 - slot, :, :], offset[:, slot, :, :], 1.0 / (1 << DIGIT), None,
                                  ALU.mult).then_inc(digit_step, 1)
                dve.wait_ge(digit_step, done + 1)
                dve.tensor_tensor(next_base[:, :, :], next_offset[:, :, :],
                                  thr[:, :].unsqueeze(1).to_broadcast([P, CANDS, E]), ALU.bitwise_or)\
                   .then_inc(digit_step, 1)
                dve.wait_ge(count_done, n + 1)
                dve.scalar_tensor_tensor(out=hit[:, :, :], in0=counts, scalar=CAP - 0.5,
                                         in1=offset[:, slot, 0:1, :].to_broadcast([P, CANDS, E]),
                                         op0=ALU.is_ge, op1=ALU.mult).then_inc(digit_step, 1)
                dve.wait_ge(digit_step, done + 4)
                with nc.allow_low_precision(reason="whole numbers, at most 7 times a power of two"):
                    dve.tensor_reduce(digit[:, :], hit[:, :, :].rearrange("p c e -> p e c"), AX, ALU.add)\
                       .then_inc(digit_step, 1)
                dve.wait_ge(digit_step, done + 5)
                dve.tensor_tensor(cand[:, :, :], next_base[:, :, :],
                                  digit[:, :].unsqueeze(1).to_broadcast([P, CANDS, E]), ALU.bitwise_or)\
                   .then_inc(digit_step, 1)
                dve.tensor_tensor(thr[:, :], thr[:, :], digit[:, :], ALU.bitwise_or).then_inc(digit_step, 1)

            with dve.Fori(0, DIGITS // 2) as m:
                for slot in range(2):
                    settle(2 * m + slot, slot)
            dve.wait_ge(digit_step, INITS + OPS * DIGITS)
            dve.tensor_tensor(above[:, :, :], gate[:, :, :], over(thr[:, :].bitcast(F32)), ALU.is_gt)\
               .then_inc(masks_ready, 1)
            dve.tensor_tensor(ties[:, :, :], gate[:, :, :], over(thr[:, :].bitcast(F32)), ALU.is_equal)\
               .then_inc(masks_ready, 1)
            dve.wait_ge(ranks_done, 1)
            link(dve.tensor_scalar(need[:, :], bank[0][:, 0:E], -1.0, float(CAP), ALU.mult, ALU.add))
            ranks = bank[0][:, 64:64 + TC * E].rearrange("p (c e) -> p c e", e=E)
            link(dve.tensor_tensor(rank[:, :, :], ranks, over(need[:, :]), ALU.is_lt))
            link(dve.tensor_tensor(rank[:, :, :], rank[:, :, :], ties[:, :, :], ALU.mult))
            dve.tensor_tensor(taken[:, :, :], rank[:, :, :], above[:, :, :], ALU.add).then_inc(taken_ready, 1)
            dve.wait_ge(taken_ready, 1)
            dve.wait_ge(slots_done, 1)
            slots = bank[0][:, 128:128 + TC * E].rearrange("p (c e) -> p c e", e=E)
            link(dve.scalar_tensor_tensor(out=slot_of[:, :, :].rearrange("p c e -> p (c e)"),
                                          in0=bank[0][:, 128:128 + TC * E], scalar=-NOWHERE,
                                          in1=taken[:, :, :].rearrange("p c e -> p (c e)"),
                                          op0=ALU.add, op1=ALU.mult))
            dve.tensor_scalar(slot_of[:, :, :], slot_of[:, :, :], NOWHERE, None, ALU.add).then_inc(slots_ready, 1)
            dve.wait_ge(slots_ready, 1)
            for c in range(TC // 4 * 3):
                for e in range(E):
                    last = dve.tensor_scalar(onehot[:, c, e, :], iota_row[:, :], slot_of[:, c, e:e + 1], None,
                                             ALU.is_equal)
                last.then_inc(hot_dve, 1)
            for e in range(E):
                dve.wait_ge(wslot_done, e + 1)
                dve.tensor_reduce(w_slot[:, e:e + 1], bank[0][:, 256 + 2 * e:258 + 2 * e], AX, ALU.add)\
                   .then_inc(wslot_ready, 1)
                dve.wait_ge(wslot_ready, e + 1)
                dve.wait_ge(fc2_done, e + 1)
                link(dve.tensor_tensor(y_sum[:, e % 2, :], b2_all[:, e, :], bank[3 + e % 2][:, 0:D], ALU.add))
                link(dve.tensor_scalar(y_hi[:, e, :], y_sum[:, e % 2, :], w_slot[:, e:e + 1], None, ALU.mult))
                dve.scalar_tensor_tensor(out=y_lo[:, e, :], in0=y_sum[:, e % 2, :], scalar=w_slot[:, e:e + 1],
                                         in1=y_hi[:, e, :].bitcast(F32), op0=ALU.mult, op1=ALU.subtract)\
                   .then_inc(y_ready, 1)
            dve.wait_ge(sum_done, 2)
            dve.wait_ge(sum_copied, 1)
            dve.tensor_copy(sum_T[:, N:TOK], bank[5][:, :]).then_inc(sum_copied, 1)
            for half in range(2):
                dve.wait_ge(sumT_done, half + 1)
                dve.tensor_tensor(final[:, half * NC:half * NC + NC, :], x_att[:, half * NC:half * NC + NC, :],
                                  bank[1 + half][:, :].rearrange("p (c d) -> p c d", d=D), ALU.add)\
                   .then_inc(final_ready, 1)

        @block.tensor
        def _(pe):
            def turn4(dst, srcs):
                for n, s in enumerate(srcs):
                    last = pe.transpose(dst[:, n * P:n * P + P], s, ident[:, :])
                return last

            pe.wait_ge(consts, 1)
            pe.wait_ge(rows_in, 16 * N_ROW_DMAS)
            pe.transpose(bank[0][:, 0:NROWS], rows[:, :], ident[0:NROWS, 0:NROWS]).then_inc(cols_T, 1)
            pe.wait_ge(wada_in, 16)
            pe.transpose(bank[3][:, 0:P], wada[:, :], ident[:, :]).then_inc(ada_T, 1)
            pe.wait_ge(cols_ready, 1)
            pe.wait_ge(films_in, 32)
            for k, w in enumerate((film1, film2)):
                for part in range(2):
                    at = 4 * k + 2 * part
                    last = pe.matmul(bank[4][:, at:at + B], w[:, part * D:part * D + D], cols[:, 0:B],
                                     start=True, stop=True)
            pe.wait_ge(ada_copied, 1)
            pe.wait_ge(silu_ready, 1)
            pe.matmul(bank[4][:, 8:8 + B], wada_T[:, :], silu[:, 2, :], start=True, stop=True)\
              .then_inc(ada_done, 1)

            def turn_norm(k):
                pe.wait_ge(norm_done, k + 1)
                for b in range(B):
                    turn4(bank[1 + b], [xn[:, b * NC + c, :] for c in range(NC)]).then_inc(norm_T, 1)

            turn_norm(0)
            pe.wait_ge(qkvo_in, 64)
            pe.wait_ge(h_act, 1)
            for b in range(B):
                hb = h_T[:, b * N:b * N + N]
                if b == 1:
                    pe.wait_ge(h_dve, 1)
                pe.matmul(bank[3 + b][:, :], wq0[:, :], hb, start=True, stop=True).then_inc(qkv0_done, 1)
                pe.matmul(bank[5 + b][:, :], wk0[:, :], hb, start=True, stop=True).then_inc(qkv0_done, 1)
                for c in range(NC):
                    last = pe.matmul(bank[(7, 0)[b]][:, c * D:c * D + D],
                                     h_T[:, (b * NC + c) * P:(b * NC + c + 1) * P], wv0[:, :],
                                     start=True, stop=True)
                last.then_inc(qkv0_done, 1)

            def scores0(g):
                b = g // NC
                pe.wait_ge(q0_ready, b + 1)
                pe.wait_ge(k0_ready, b + 1)
                wait(pe, exp0_done, g - 1)
                pe.matmul(bank[1 + g % 2][:, :], qT0[:, g * P:g * P + P], kT0[:, b * N:b * N + N],
                          start=True, stop=True).then_inc(s0_done, 1)

            def turn0(g):
                pe.wait_ge(p0_ready, g + 1)
                if g < 2:
                    pe.wait_ge(q0_ready, 2)
                wait(pe, pT0_copied, g - 1)
                turn4(bank[3 + g % 2], [p0[:, g % 2, c * P:c * P + P] for c in range(NC)]).then_inc(pT0_done, 1)

            def mix0(g):
                b, n = g // NC, g % NC
                pe.wait_ge(pT0_copied, g + 1)
                pe.wait_ge(v0_ready, b + 1)
                for c in range(NC):
                    last = pe.matmul(bank[5 + b][:, n * P:n * P + P], v0[:, b * NC + c, :],
                                     pT0[:, g % 2, c, :], start=(c == 0), stop=(c == NC - 1))
                last.then_inc(o0_done, 1)

            def proj0(b):
                pe.wait_ge(o0_copied, b + 1)
                for c in range(NC):
                    last = pe.matmul(bank[(7, 0)[b]][:, c * D:c * D + D],
                                     oT0[:, (b * NC + c) * P:(b * NC + c + 1) * P], wp0[:, :],
                                     start=True, stop=True)
                last.then_inc(proj0_done, 1)

            for g in range(TC + 3):
                if g < TC:
                    scores0(g)
                if 1 <= g < TC + 1:
                    turn0(g - 1)
                if 2 <= g < TC + 2:
                    mix0(g - 2)
                if g == NC + 3:
                    proj0(0)
            proj0(1)

            pe.wait_ge(wqkv_in, 16)
            pe.wait_ge(wout_in, 32)
            pe.wait_ge(mid_ready, 2)
            for n in range(WC // 4 + KC // 4):
                wait(pe, wT_copied, n - 1)
                src = [wqkv_raw[:, 4 * n + c, :] for c in range(4)] if n < WC // 4 else \
                    [o_all[:, 0, (4 * (n - WC // 4) + c) * P:(4 * (n - WC // 4) + c + 1) * P] for c in range(4)]
                turn4(bank[6 + n % 2], src).then_inc(wT_done, 1)
            pe.wait_ge(wT_copied, WC // 4 + KC // 4)
            pe.transpose(bank[6][:, 0:E], wgate[:, :], ident[0:E, 0:E]).then_inc(wT_done, 1)

            turn_norm(1)
            pe.wait_ge(mlp_in, 32)
            pe.wait_ge(h_act, 2)
            pe.wait_ge(h_dve, 2)

            def up0(n):
                b, c = n // HC, n % HC
                wait(pe, gelu0_done, n - 1)
                pe.matmul(bank[3 + n % 2][:, :], w10[:, c * P:c * P + P], h_T[:, b * N:b * N + N],
                          start=True, stop=True).then_inc(u0_done, 1)

            def down0(b):
                pe.wait_ge(gelu0_done, HC * (b + 1))
                pe.wait_ge(wT_copied, WC // 4 + KC // 4)
                for c in range(NC):
                    for k in range(HC):
                        last = pe.matmul(bank[(7, 0)[b]][:, c * D:c * D + D],
                                         u0[:, k, (b * NC + c) * P:(b * NC + c + 1) * P], w20[:, k, :],
                                         start=(k == 0), stop=(k == HC - 1))
                last.then_inc(y0_done, 1)

            for n in range(HC + 2):
                up0(n)
            down0(0)
            for n in range(HC + 2, 2 * HC):
                up0(n)
            down0(1)
            turn_norm(2)
            pe.wait_ge(h_split, 1)
            pe.wait_ge(w_split, 1)
            pe.wait_ge(wT_copied, WC // 4 + KC // 4 + 1)

            qkv = pair[:, :, :].rearrange("p a (c w) -> p (a c) w", c=2)

            def project(u, b, head):
                wait(pe, normed, u)
                wait(pe, v_copied, u)
                for c in range(NC):
                    at = (b * NC + c) * P
                    for n, (h_part, w_part) in enumerate(((h_hi, w_hi), (h_hi, w_lo), (h_lo, w_hi))):
                        last = pe.matmul(qkv[:, c, 0:3 * HD], h_part[:, at:at + P],
                                         w_part[:, bass.ds(head, 1), :].rearrange("p h w -> p (h w)"),
                                         start=(n == 0), stop=(n == 2))
                last.then_inc(qkv_done, 1)

            def turn_unit(u, slot):
                wait(pe, normed, u + 1)
                wait(pe, kq_affine, u)
                turn4(bank[5], [qk_n[:, slot, c, :, :].rearrange("p t d -> p (t d)") for c in range(NC)])\
                    .then_inc(kqT_done, 1)

            def scores(g, u, c, slot):
                if c == 0:
                    wait(pe, split_done, u + 1)
                wait(pe, exp_done, g - 1)
                at = slice(c * P, c * P + P)
                pe.matmul(bank[c % 2][:, :], q_s[:, slot, at], k_s[:, slot, :], start=True, stop=False)
                pe.matmul(bank[c % 2][:, :], q_s[0:HD, slot, at], lows[0:HD, slot, :], start=False, stop=True)\
                  .then_inc(scores_done, 1)

            def turn_probs(g, c):
                wait(pe, exp_done, g + 1)
                wait(pe, probs_copied, g - 1)
                turn4(bank[2 + c % 2], [probs[:, c % 2, k * P:k * P + P] for k in range(NC)])\
                    .then_inc(probsT_done, 1)

            def mix(g, u, c, slot):
                wait(pe, probs_copied, g + 1)
                if c == 0:
                    wait(pe, v_copied, u + 1)
                    wait(pe, o_normed, u)
                for k in range(NC):
                    last = pe.matmul(bank[4][:, c * (HD + 1):(c + 1) * (HD + 1)], probs_T[:, c % 2, k, :],
                                     v_s[:, slot, k, :], start=(k == 0), stop=(k == NC - 1))
                last.then_inc(pv_done, 1)

            def body(i, first=False, last=False):
                for j in range(PER):
                    u = i * PER + j
                    for c in range(NC):
                        g = u * NC + c
                        scores(g, u, c, j % 2)
                        if c == 0 and not (last and j == PER - 1):
                            turn_unit(u + 1, (j + 1) % 2)
                        if not (first and j == 0 and c < 2):
                            turn_probs(g - 2, c % 2)
                        if not (first and j == 0 and c < 3):
                            back = u if c == 3 else u - 1
                            mix(g - 3, back, (c + 1) % NC, j if c == 3 else (j - 1) % PER)
                        if c == 0 and not (last and j >= PER - 2):
                            project(u + 2, j % B, 2 * i + (j + 2) // 2)

            project(0, 0, 0)
            turn_unit(0, 0)
            project(1, 1, 0)
            body(0, first=True)
            with pe.Fori(1, STEPS - 1) as i:
                body(i)
            body(STEPS - 1, last=True)
            G = UNITS * NC
            turn_probs(G - 2, 0)
            mix(G - 3, UNITS - 1, 1, PER - 1)
            turn_probs(G - 1, 1)
            mix(G - 2, UNITS - 1, 2, PER - 1)
            mix(G - 1, UNITS - 1, 3, PER - 1)

            def turn_out(t):
                if t < 2:
                    pe.wait_ge(o_normed, UNITS)
                else:
                    pe.wait_ge(oT_act, t - 1)
                    pe.wait_ge(oT_dve, t - 1)
                for half in range(2):
                    turn4(bank[2 * (t % 2) + half],
                          [o_all[:, t, (4 * half + c) * P:(4 * half + c + 1) * P] for c in range(4)])\
                        .then_inc(oT_done, 1)

            turn_out(0)
            for t in range(TC):
                if t + 1 < TC:
                    turn_out(t + 1)
                pe.wait_ge(oT_act, t + 1)
                pe.wait_ge(oT_dve, t + 1)
                wait(pe, att_ready, t - 1)
                for k in range(KC):
                    last = pe.matmul(bank[4 + t % 2][:, 0:D], oT[:, t % 2, k, :], wout_T[:, k, :],
                                     start=(k == 0), stop=(k == KC - 1))
                last.then_inc(out_done, 1)
            pe.wait_ge(att_ready, TC)
            for b in range(B):
                turn4(bank[6 + b], [x_att[:, b * NC + c, :] for c in range(NC)]).then_inc(xaT_done, 1)
            pe.wait_ge(xaT_act, 1)
            pe.wait_ge(xaT_dve, 1)
            for c in range(TC):
                last = pe.matmul(bank[5][:, c * E:c * E + E], xa_T[:, c * P:c * P + P], wgate_T[:, :],
                                 start=True, stop=True)
            last.then_inc(logits_done, 1)
            pe.wait_ge(fc_in, 48)

            def turn_experts(n):
                wait(pe, fcT_copied, n - 3)
                src = [fc1_raw[:, n, c, :] for c in range(4)] if n < E else \
                    [fc2_raw[:, n - E, c * P:c * P + P] for c in range(4)]
                turn4(bank[1 + n % 4], src).then_inc(fcT_done, 1)

            turn_experts(0)
            turn_experts(1)
            for n in range(DIGITS):
                for c in range(TC):
                    if c % NC == 0:
                        pe.wait_ge(cmp_done, 2 * n + 1 + c // NC)
                    last = pe.matmul(bank[0][:, 0:CANDS * E], ones_bf[:, :],
                                     at_least[:, c, :, :].rearrange("p c e -> p (c e)"),
                                     start=(c == 0), stop=(c == TC - 1))
                last.then_inc(count_done, 1)
                for k in range(2 * n + 2, min(2 * n + 4, 2 * E)):
                    turn_experts(k)

            def before(at, mask, done):
                flat = lambda lo, hi: bank[0][:, at + lo * E:at + hi * E]
                pe.matmul(flat(0, TC), before_bf[:, :], mask[:, :, :].rearrange("p c e -> p (c e)"),
                          start=True, stop=False, skip_group_check=True)
                for c in range(TC - 1):
                    last = pe.matmul(flat(c + 1, TC).rearrange("p (c e) -> p c e", e=E), ones_bf[:, :],
                                     mask[:, c, :].unsqueeze(1).to_broadcast([P, TC - 1 - c, E]),
                                     start=False, stop=(c == TC - 2), skip_group_check=True)
                last.then_inc(done, 1)

            pe.wait_ge(masks_ready, 2)
            for c in range(TC):
                pe.matmul(bank[0][:, 0:E], ones_bf[:, :], above[:, c, :], start=(c == 0), stop=(c == TC - 1))
            before(64, ties, ranks_done)
            pe.wait_ge(taken_ready, 1)
            before(128, taken, slots_done)

            pe.wait_ge(tn_split, 1)
            pe.wait_ge(fcT_copied, 2 * E)
            for c in range(TC):
                if c < TC // 4 * 3:
                    pe.wait_ge(hot_dve, c + 1)
                else:
                    pe.wait_ge(hot_pool, c + 1 - TC // 4 * 3)
                for q in range(2):
                    for n, part in enumerate((tn_hi, tn_lo)):
                        last = pe.matmul(bank[1 + q][:, :], part[:, c, :],
                                         onehot[:, c, 4 * q:4 * q + 4, :].rearrange("p e n -> p (e n)"),
                                         start=(c == 0 and n == 0), stop=(c == TC - 1 and n == 1))
                    if c == TC - 1:
                        last.then_inc(xg_done, 1)
                for q in range(2):
                    if c:
                        pe.wait_ge(hotT_copied, 2 * c - 1 + q)
                    turn4(bank[5 + q], [onehot[:, c, 4 * q + e, :].bitcast(F32) for e in range(4)])\
                        .then_inc(hotT_done, 1)
            pe.wait_ge(gate_split, 1)
            pe.wait_ge(slots_ready, 1)

            def slot_weights(e):
                wait(pe, wslot_ready, e)
                for c in range(TC):
                    last = pe.matmul(bank[0][:, 256 + 2 * e:258 + 2 * e], onehot[:, c, e, :], gate_r[:, c, e, :],
                                     start=(c == 0), stop=(c == TC - 1))
                last.then_inc(wslot_done, 1)

            def up(e):
                if e < 2:
                    pe.wait_ge(xg_ready, 2)
                wait(pe, gelu_done, e - 1)
                for c in range(DC):
                    last = pe.matmul(bank[1 + e % 2][:, c * CAP:c * CAP + CAP], fc1_T[:, e, c * P:c * P + P],
                                     xg[:, e, :], start=True, stop=True)
                last.then_inc(fc1_done, 1)

            def down(e):
                pe.wait_ge(gelu_done, e + 1)
                wait(pe, y_ready, e - 1)
                for c in range(DC):
                    last = pe.matmul(bank[3 + e % 2][:, 0:D], ug[:, e % 2, c, :], fc2_T[:, e, c, :],
                                     start=(c == 0), stop=(c == DC - 1))
                last.then_inc(fc2_done, 1)

            def scatter(e):
                if e == 0:
                    pe.wait_ge(hotT_copied, 2 * TC)
                pe.wait_ge(y_ready, e + 1)
                for b, dst in enumerate((bank[7], bank[5])):
                    for n, part in enumerate((y_hi, y_lo)):
                        last = pe.matmul(dst[:, :], part[:, e, :], onehot_T[:, e, b * N:b * N + N],
                                         start=(e == 0 and n == 0), stop=(e == E - 1 and n == 1))
                    if e == E - 1:
                        last.then_inc(sum_done, 1)

            slot_weights(0)
            up(0)
            for e in range(E):
                if e + 1 < E:
                    up(e + 1)
                down(e)
                if e + 1 < E:
                    slot_weights(e + 1)
                if e:
                    scatter(e - 1)
            scatter(E - 1)
            for b in range(B):
                pe.wait_ge(sum_copied, b + 1)
                turn4(bank[1 + b], [sum_T[:, (b * NC + c) * P:(b * NC + c + 1) * P] for c in range(NC)])\
                    .then_inc(sumT_done, 1)


_INS = ['x', 'cond_1024'] + ['L0_cond_' + n for n in (
    'norm1_w', 'film1_w', 'film1_b', 'q_w', 'q_b', 'k_w', 'k_b', 'v_w', 'v_b', 'proj_w', 'proj_b', 'norm2_w',
    'film2_w', 'film2_b', 'mlp_w1', 'mlp_b1', 'mlp_w2', 'mlp_b2')] + ['L1_cond_' + n for n in (
        'W_ada', 'b_ada', 'ln1_g', 'ln1_b', 'Wqkv', 'qn_g', 'qn_b', 'kn_g', 'kn_b', 'Wout', 'mlp_g', 'mlp_b',
        'Wgate', 'fc1s', 'b1s', 'fc2s', 'b2s')]


def kernel(**inputs):
    import numpy as np
    import concourse.bacc as bacc
    from concourse.bass_utils import run_bass_kernel_spmd

    nc = bacc.Bacc("TRN2", target_bir_lowering=False, num_devices=1)
    arrays, args = {}, []
    for name in _INS:
        a = np.ascontiguousarray(inputs[name])
        arrays[f"in_{name}_dram"] = a
        args.append(nc.dram_tensor(f"in_{name}_dram", a.shape, mybir.dt.from_np(a.dtype),
                                   kind="ExternalInput").ap())
    args.append(nc.dram_tensor("out_dram", inputs["x"].shape, F32, kind="ExternalOutput").ap())
    film_attention_then_expert_choice(nc, *args)
    r = run_bass_kernel_spmd(nc, [arrays], core_ids=[0])
    return r.results[0]["out_dram"]
```

```python
from contextlib import ExitStack

import concourse.bass as bass
from concourse import mybir

P = 128
F32 = mybir.dt.float32
F32R = mybir.dt.float32r
BF16 = mybir.dt.bfloat16
I32 = mybir.dt.int32
ALU = mybir.AluOpType
ACT = mybir.ActivationFunctionType
AX = mybir.AxisListType.X
BYTES = {F32: 4, F32R: 4, BF16: 2, I32: 4}

ROWS = {}
for _name, _n in (("cond", 2), ("norm1_w", 1), ("film1_b", 2), ("q_b", 1), ("k_b", 1), ("norm2_w", 1),
                  ("film2_b", 2), ("mlp_b1", 4), ("b_ada", 1), ("ln1_g", 1), ("ln1_b", 1), ("kq_g", 1),
                  ("kq_b", 1), ("mlp_g", 1), ("mlp_b", 1), ("b1s", 32)):
    ROWS[_name] = (sum(n for _, n in ROWS.values()), _n)
NROWS = sum(n for _, n in ROWS.values())
EARLY = ROWS["norm2_w"][0]


def wait(eng, semaphore, value):
    if isinstance(value, int) and value <= 0:
        return
    eng.wait_ge(semaphore, value)


def spread(ap, shape):
    return ap.unsqueeze(len(shape) - 1).to_broadcast(shape)


def film_attention_then_expert_choice(
        nc, x, cond, norm1_w, film1_w, film1_b, q_w, q_b, k_w, k_b, v_w, v_b, proj_w, proj_b,
        norm2_w, film2_w, film2_b, mlp_w1, mlp_b1, mlp_w2, mlp_b2,
        W_ada, b_ada, ln1_g, ln1_b, Wqkv, qn_g, qn_b, kn_g, kn_b, Wout, mlp_g, mlp_b,
        Wgate, fc1s, b1s, fc2s, b2s, out):
    B, N, D = x.shape
    TOK = B * N
    TC = TOK // P
    NC = N // P
    HD = qn_g.shape[0]
    H = Wqkv.shape[0] // 3 // HD
    WC = Wqkv.shape[0] // P
    KC = H * HD // P
    HID = mlp_w1.shape[1]
    HC = HID // P
    E, DD, _ = fc1s.shape
    CAP = TOK // E
    DC = DD // P
    UNITS = H * B
    PER = 4
    STEPS = UNITS // PER
    EPS0, EPS1 = 1e-6, 1e-5
    BITS = 30
    DIGIT = 3
    CANDS = (1 << DIGIT) - 1
    DIGITS = BITS // DIGIT
    NOWHERE = 255.0
    assert D == P and CAP == P and B == 2 and NC == 4 and HD == 64 and HC == DC == 4 and E == 8

    ctx = ExitStack()
    with ctx:
        class Area:
            def __init__(self, start):
                self.at = start

            def __call__(self, name, shape, dt=F32):
                size = BYTES[dt]
                for n in shape[1:]:
                    size *= n
                t = nc.alloc_sbuf_tensor_at(name, shape, dt, offset=self.at)
                self.at += (size + 31) // 32 * 32
                return t

        def sem(name):
            return ctx.enter_context(nc.semaphore(name))

        pair0 = ctx.enter_context(nc.psum_tensor("pair0", [P, 2, 512], F32))
        bank = [pair0[:, 0, :], pair0[:, 1, :]]
        bank += [ctx.enter_context(nc.psum_tensor(f"bank{i}", [P, 512], F32)) for i in range(2, 6)]
        pair = ctx.enter_context(nc.psum_tensor("pair", [P, 2, 512], F32))
        bank += [pair[:, 0, :], pair[:, 1, :]]

        keep = Area((nc.sbuf_base + 31) // 32 * 32)
        ident = keep("ident", [P, P])
        ones_bf = keep("ones_bf", [P, P], BF16)
        before_bf = keep("before_bf", [P, P], BF16)
        iota_row = keep("iota_row", [P, P])
        minus_half = keep("minus_half", [P, TC])
        early_rows = keep("early_rows", [EARLY, P])
        late_rows = keep("late_rows", [NROWS - EARLY, P])
        cols = keep("cols", [P, NROWS])
        affine = keep("affine", [P, 3, 2, B])
        silu = keep("silu", [P, 3, B])
        x_att = keep("x_att", [P, TC, D])
        wout_T = keep("wout_T", [P, KC, D])
        wgate_T = keep("wgate_T", [P, E])
        table_call = keep("table_call", [P, 2])
        centre = keep("centre", [P, TC])
        sumsq = keep("sumsq", [P, TC])
        meansq = keep("meansq", [P, TC])
        rstd = keep("rstd", [P, TC])
        area_start = keep.at

        early = Area(area_start)
        x_in = early("x_in", [P, TC, D])
        h_T = early("h_T", [P, TOK])
        h_hi = early("h_hi", [P, TOK], F32R)
        h_lo = early("h_lo", [P, TOK], F32R)
        fc_start = early.at
        sq0 = early("sq0", [P, TC, D])
        xn = early("xn", [P, TC, D])
        mlp_start = early.at
        qT0 = early("qT0", [P, TOK])
        kT0 = early("kT0", [P, TOK])
        v0 = early("v0", [P, TC, D])
        oT0 = early("oT0", [P, TOK])
        u0 = Area(mlp_start)("u0", [P, HC, TOK])
        x_mid = early("x_mid", [P, TC, D])
        p0 = early("p0", [P, 2, N])
        pT0 = early("pT0", [P, 2, NC, P])
        soft0 = early("soft0", [P, TC, 3])
        film1 = early("film1", [P, 2 * D])
        film2 = early("film2", [P, 2 * D])
        wq0 = early("wq0", [P, D])
        wk0 = early("wk0", [P, D])
        wv0 = early("wv0", [P, D])
        wp0 = early("wp0", [P, D])
        w10 = early("w10", [P, HID])
        w20 = early("w20", [P, HC, D])
        wada = early("wada", [P, D])
        wada_T = early("wada_T", [P, D])
        wgate = early("wgate", [E, D])
        vb0 = early("vb0", [P, D])
        pb0 = early("pb0", [P, D])
        mb0 = early("mb0", [P, D])
        wout = early("wout", [P, H * HD])
        w_all = early("w_all", [P, H, 2 * HD + D])
        wmean = early("wmean", [P, H, 2])

        experts = Area(fc_start)
        fc1_raw = experts("fc1_raw", [P, E, DC, D])
        fc2_raw = experts("fc2_raw", [P, E, DD])
        fc1_T = experts("fc1_T", [P, E, DD])
        fc2_T = experts("fc2_T", [P, E, DC, D])
        b2_all = experts("b2_all", [P, E, D])

        loop = Area(max(early.at, experts.at))
        wqkv_raw = Area(loop.at)("wqkv_raw", [P, WC, D])
        w_start = loop.at
        w_hi = loop("w_hi", [P, H, 2 * HD + D], F32R)
        w_lo = loop("w_lo", [P, H, 2 * HD + D], F32R)
        loop2_start = loop.at
        qk_sq = loop("qk_sq", [P, NC, 2, HD])
        qk_ss = loop("qk_ss", [P, NC, 2])
        qk_ms = loop("qk_ms", [P, NC, 2])
        qk_rstd = loop("qk_rstd", [P, NC, 2])
        qk_n = loop("qk_n", [P, 2, NC, 2, HD])
        v_new = loop("v_new", [P, 2, NC, D])
        v_s = loop("v_s", [P, PER, NC, D])
        kq32 = loop("kq32", [P, 2, N // 2])
        q_s = loop("q_s", [P, 2, 2, N], F32R)
        k_s = loop("k_s", [P, 2, 2, N], F32R)
        lows = loop("lows", [P, 2, 2, N], F32R)
        negmax = loop("negmax", [P, 4])
        probs = loop("probs", [P, 2, N])
        probs_T = loop("probs_T", [P, 2, NC, P])
        row_sum = loop("row_sum", [P, 2, NC])
        o_rec = loop("o_rec", [P, NC])

        moe = Area(loop2_start)
        moe2 = Area(w_start)
        onehot = moe("onehot", [P, TC, E, CAP], F32R)
        onehot_T = moe("onehot_T", [P, E, TOK], F32R)
        tn = moe2("tn", [P, TC, D])
        tn_hi = moe2("tn_hi", [P, TC, D], F32R)
        tn_lo = moe2("tn_lo", [P, TC, D], F32R)
        xa_T = moe2("xa_T", [P, TOK])
        tn_sq = moe2("tn_sq", [P, TC, D])
        y_hi = Area(area_start)("y_hi", [P, E, D], F32R)
        y_lo = Area(area_start + 4 * E * D)("y_lo", [P, E, D], F32R)
        y_sum = Area(area_start + 8 * E * D)("y_sum", [P, 2, D])
        final = Area(area_start + 12 * E * D)("final", [P, TC, D])
        sum_T = Area(area_start + 16 * E * D)("sum_T", [P, TOK])
        xg = moe("xg", [P, E, CAP])
        ug = moe("ug", [P, 2, DC, CAP])
        gate = moe("gate", [P, TC, E])
        gate_x = moe("gate_x", [P, TC, E])
        gate_m = moe("gate_m", [P, 2, TC])
        gate_r = moe("gate_r", [P, TC, E, 2], F32R)
        at_least = moe("at_least", [P, TC, CANDS, E], BF16)
        above = moe("above", [P, TC, E], BF16)
        ties = moe("ties", [P, TC, E], BF16)
        taken = moe("taken", [P, TC, E], BF16)
        rank = moe("rank", [P, TC, E])
        slot_of = moe("slot_of", [P, TC, E])
        need = moe("need", [P, E])
        thr = moe("thr", [P, E], I32)
        digit = moe("digit", [P, E], I32)
        cand = moe("cand", [P, CANDS, E], I32)
        next_offset = moe("next_offset", [P, CANDS, E], I32)
        hit = moe("hit", [P, CANDS, E])
        next_base = moe("next_base", [P, CANDS, E], I32)
        offset = moe("offset", [P, 2, CANDS, E])
        w_rows = Area(area_start + 20 * E * D)("w_rows", [E, 2, N])
        w_slot = moe("w_slot", [P, E])

        early_in, late_in, film1_in, film2_in, wada_in, x_loaded, qkv_in, bcast_in, mlp_in, wqkv_in, wout_in, fc_in = (
            sem(n) for n in ("early_in", "late_in", "film1_in", "film2_in", "wada_in", "x_loaded", "qkv_in", "bcast_in", "mlp_in",
                             "wqkv_in", "wout_in", "fc_in"))
        proj_in = sem("proj_in")
        consts = sem("consts")
        dve_step, pool_step = sem("dve_step"), sem("pool_step")
        cols_T, cols_ready, cond_exp, silu_ready, film1_done, ada_done, affine_ready = (
            sem(n) for n in ("cols_T", "cols_ready", "cond_exp", "silu_ready", "film1_done",
                             "ada_done", "affine_ready"))
        norm_in, norm_sq, norm_ss, norm_rstd, norm_done, norm_T, h_act, h_dve, h_split = (
            sem(n) for n in ("norm_in", "norm_sq", "norm_ss", "norm_rstd", "norm_done", "norm_T",
                             "h_act", "h_dve", "h_split"))
        xpb_ready, xmb_ready = sem("xpb_ready"), sem("xmb_ready")
        qkv0_done, q0_ready, k0_ready, v0_ready = (
            sem(n) for n in ("qkv0_done", "q0_ready", "k0_ready", "v0_ready"))
        s0_done, max0_done, exp0_done, p0_ready, pT0_done, pT0_copied, o0_done, o0_copied, proj0_done, mid_ready = (
            sem(n) for n in ("s0_done", "max0_done", "exp0_done", "p0_ready", "pT0_done", "pT0_copied",
                             "o0_done", "o0_copied", "proj0_done", "mid_ready"))
        u0_done, gelu0_done, y0_done = sem("u0_done"), sem("gelu0_done"), sem("y0_done")
        wT_done, wT_copied, w_summed, w_centred, w_split = (
            sem(n) for n in ("wT_done", "wT_copied", "w_summed", "w_centred", "w_split"))
        qkv_done, sq_done, ss_done, rstd_done, normed, v_taken, v_placed = (
            sem(n) for n in ("qkv_done", "sq_done", "ss_done", "rstd_done", "normed", "v_taken", "v_placed"))
        kqT_done, kq_affine, highs_done, lows_done, q_hi_moved, split_done, o_normed = (
            sem(n) for n in ("kqT_done", "kq_affine", "highs_done", "lows_done", "q_hi_moved", "split_done",
                             "o_normed"))
        o_rec_done = sem("o_rec_done")
        sq_summed = sem("sq_summed")
        scores_done, max_done, exp_done, probsT_done, probs_copied, pv_done = (
            sem(n) for n in ("scores_done", "max_done", "exp_done", "probsT_done", "probs_copied", "pv_done"))
        xaT_done, xaT_act, xaT_dve, logits_done, logits_sub, gate_exp = (
            sem(n) for n in ("xaT_done", "xaT_act", "xaT_dve", "logits_done", "logits_sub", "gate_exp"))
        tn_means, tn_centred, tn_ss, tn_split = (
            sem(n) for n in ("tn_means", "tn_centred", "tn_ss", "tn_split"))
        digit_step, cmp_done, count_done = sem("digit_step"), sem("cmp_done"), sem("count_done")
        masks_ready, ranks_done, taken_ready, slots_done, slots_ready, hot_dve, hot_pool, gate_split = (
            sem(n) for n in ("masks_ready", "ranks_done", "taken_ready", "slots_done", "slots_ready",
                             "hot_dve", "hot_pool", "gate_split"))
        fcT_done, fcT_copied = sem("fcT_done"), sem("fcT_copied")
        xg_done, xg_ready, wslot_done, wslot_ready, hotT_done, hotT_copied = (
            sem(n) for n in ("xg_done", "xg_ready", "wslot_done", "wslot_ready", "hotT_done",
                             "hotT_copied"))
        w_rows_done, w_rows_copied = sem("w_rows_done"), sem("w_rows_copied")
        sum_copied, sumT_done = sem("sum_copied"), sem("sumT_done")
        fc1_done, gelu_done, fc2_done, y_ready, sum_done, final_ready, stored = (
            sem(n) for n in ("fc1_done", "gelu_done", "fc2_done", "y_ready", "sum_done", "final_ready",
                             "stored"))

        def banks_of(p):
            return pair0 if isinstance(p, int) and p == 1 else pair

        def in_banks(p):
            return banks_of(p)[:, :, :].rearrange("p a (c w) -> p (a c) w", c=2)

        def piece_at(t, p_in, lo=0, hi=P):
            half = p_in % 2 * (N // 2)
            return t[lo:hi, p_in // 2 % 2, :, half:half + N // 2]

        def group_unused(p, p_in):
            return 4 * (p - 2) if p_in % 2 == 0 else 4 * (p - 3)

        def attended(b):
            return UNITS - (B - 1 - b) * PER // B

        POOL_HEADS = H * 3 // 4
        QK_BANKS, WOUT_BANKS, V_BANKS = 2 * KC // 4, KC // 4, H // 4
        W_BANKS = QK_BANKS + WOUT_BANKS + V_BANKS

        def col(name, i=0):
            return cols[:, ROWS[name][0] + i:ROWS[name][0] + i + 1]

        as_row = lambda v: v.rearrange("(a d) -> a d", d=P)
        late_at = lambda name: ROWS[name][0] - EARLY
        early_loads = [(early_rows[ROWS[name][0]:ROWS[name][0] + ROWS[name][1], :], src) for name, src in (
            ("cond", cond), ("norm1_w", as_row(norm1_w)), ("film1_b", as_row(film1_b)), ("q_b", as_row(q_b)),
            ("k_b", as_row(k_b)))]
        late_loads = [(late_rows[late_at(name):late_at(name) + ROWS[name][1], :], src) for name, src in (
            ("norm2_w", as_row(norm2_w)), ("film2_b", as_row(film2_b)),
            ("mlp_b1", as_row(mlp_b1)), ("b_ada", as_row(b_ada)), ("ln1_g", as_row(ln1_g)),
            ("ln1_b", as_row(ln1_b)), ("mlp_g", as_row(mlp_g)), ("mlp_b", as_row(mlp_b)),
            ("b1s", b1s.rearrange("e (a d) -> (e a) d", d=P)))]
        for name, halves in (("kq_g", (kn_g, qn_g)), ("kq_b", (kn_b, qn_b))):
            r = late_at(name)
            for half, v in enumerate(halves):
                late_loads.append((late_rows[r:r + 1, half * HD:half * HD + HD], v.rearrange("(a d) -> a d", a=1)))

        block = ctx.enter_context(nc.Block())

        @block.sync
        def _(sp):
            for dst, src in early_loads:
                sp.dma_start(dst, src).then_inc(early_in, 16)
            sp.dma_start(film1[:, :], film1_w).then_inc(film1_in, 16)
            for t, src in ((wq0, q_w), (wk0, k_w), (wv0, v_w)):
                sp.dma_start(t[:, :], src).then_inc(qkv_in, 16)
            for t, src in ((vb0, v_b), (pb0, proj_b), (mb0, mlp_b2)):
                sp.dma_start(t[:, :], src.rearrange("(a d) -> a d", a=1).to_broadcast([P, D]))\
                  .then_inc(bcast_in, 16)
            sp.dma_start(wada[:, :], W_ada).then_inc(wada_in, 16)
            for dst, src in late_loads:
                sp.dma_start(dst, src).then_inc(late_in, 16)
            sp.dma_start(film2[:, :], film2_w).then_inc(film2_in, 16)
            sp.dma_start(wp0[:, :], proj_w).then_inc(proj_in, 16)
            sp.dma_start(w10[:, :], mlp_w1).then_inc(mlp_in, 16)
            sp.dma_start(w20[:, :, :], mlp_w2.rearrange("(c p) d -> p c d", p=P)).then_inc(mlp_in, 16)
            sp.dma_start(wout[:, :], Wout).then_inc(wout_in, 16)
            sp.dma_start(wgate[:, :], Wgate).then_inc(wout_in, 16)
            sp.wait_ge(qkv_done, 1)
            sp.wait_ge(h_split, 2)
            sp.wait_ge(w_split, 3)
            sp.dma_start(fc1_raw[:, :, :, :], fc1s.rearrange("e (c p) d -> p e c d", p=P)).then_inc(fc_in, 16)
            sp.dma_start(fc2_raw[:, :, :], fc2s.rearrange("e d h -> d e h")).then_inc(fc_in, 16)
            sp.dma_start(b2_all[:, :, :], b2s.unsqueeze(0).to_broadcast([P, E, D])).then_inc(fc_in, 16)
            for half in range(2):
                sp.wait_ge(final_ready, half + 1)
                sp.dma_start(out[half].rearrange("(c p) d -> p c d", p=P),
                             final[:, half * NC:half * NC + NC, :]).then_inc(stored, 16)
            sp.wait_ge(stored, 32)

        @block.gpsimd
        def _(pool):
            steps = [0]

            def link(ins):
                steps[0] += 1
                ins.then_inc(pool_step, 1)
                pool.wait_ge(pool_step, steps[0])

            link(pool.memset(ident[:, :], 0.0))
            pool.affine_select(out=ident[:, :], in_=ident[:, :], compare_op=ALU.not_equal, fill=1.0, base=0,
                               pattern=[[-1, P]], channel_multiplier=1).then_inc(consts, 1)
            pool.memset(minus_half[:, :], -0.5).then_inc(consts, 1)
            link(pool.memset(ones_bf[:, :], 1.0))
            pool.affine_select(out=before_bf[:, :], in_=ones_bf[:, :], compare_op=ALU.is_gt, fill=0.0, base=0,
                               pattern=[[1, P]], channel_multiplier=-1).then_inc(consts, 1)
            pool.iota(iota_row[:, :], [[1, P]], base=0, channel_multiplier=0,
                      allow_small_or_imprecise_dtypes=True).then_inc(consts, 1)
            pool.wait_ge(consts, 2)

            def norm_scale(k, b, eps):
                pool.wait_ge(norm_ss, 2 * k + b + 1)
                at = slice(b * NC, b * NC + NC)
                link(pool.tensor_scalar(meansq[:, at], sumsq[:, at], 1.0 / D, eps, ALU.mult, ALU.add))
                pool.tensor_tensor(rstd[:, at], meansq[:, at], minus_half[:, at], ALU.pow).then_inc(norm_rstd, 1)

            norm_scale(0, 0, EPS0)
            norm_scale(0, 1, EPS0)
            pool.wait_ge(x_loaded, 16)
            pool.wait_ge(bcast_in, 48)
            pool.wait_ge(norm_done, 2)
            bias = lambda t: t[:, :].unsqueeze(1).to_broadcast([P, TC, D])
            pool.tensor_tensor(x_in[:, :, :], x_in[:, :, :], bias(pb0), ALU.add).then_inc(xpb_ready, 1)
            norm_scale(1, 0, EPS0)
            norm_scale(1, 1, EPS0)
            pool.wait_ge(norm_done, 4)
            pool.tensor_tensor(x_mid[:, :, :], x_mid[:, :, :], bias(mb0), ALU.add).then_inc(xmb_ready, 1)
            pool.wait_ge(w_summed, 1)
            for t in range(2):
                at = slice(t * HD, t * HD + HD)
                last = pool.tensor_tensor(w_all[:, :, at], w_all[:, :, at],
                                          spread(wmean[:, :, t], [P, H, HD]), ALU.add)
            last.then_inc(w_centred, 1)
            pool.wait_ge(w_centred, 2)

            def weights_low(lo, hi):
                pool.tensor_tensor(w_lo[:, lo:hi, :], w_all[:, lo:hi, :], w_hi[:, lo:hi, :].bitcast(F32),
                                   ALU.subtract).then_inc(w_split, 1)

            weights_low(0, POOL_HEADS // 2)
            norm_scale(2, 0, EPS1)
            weights_low(POOL_HEADS // 2, POOL_HEADS)
            norm_scale(2, 1, EPS1)

            def piece_scale(p, lows_before):
                wait(pool, ss_done, p + 1)
                wait(pool, normed, p)
                wait(pool, lows_done, lows_before)
                pool.tensor_tensor(qk_rstd[:, :, :].rearrange("p c t -> p (c t)"),
                                   qk_ms[:, :, :].rearrange("p c t -> p (c t)"),
                                   minus_half[:, 0:2 * NC], ALU.pow).then_inc(rstd_done, 1)

            def piece_low(p, p_in, scales_before):
                wait(pool, highs_done, p + 1)
                wait(pool, rstd_done, scales_before)
                wait(pool, scores_done, group_unused(p, p_in))
                pool.tensor_tensor(piece_at(lows, p_in), kq32[:, :, :], piece_at(k_s, p_in).bitcast(F32),
                                   ALU.subtract).then_inc(lows_done, 1)

            def body(i, last=False):
                for j in range(PER):
                    u = i * PER + j
                    if not (last and j >= PER - 3):
                        piece_scale(u + 3, u + 2)
                    if not (last and j >= PER - 2):
                        piece_low(u + 2, j + 2, UNITS if last else u + 4)

            piece_scale(0, 0)
            piece_scale(1, 0)
            piece_low(0, 0, 2)
            piece_low(1, 1, 2)
            piece_scale(2, 2)
            body(0)
            with pool.Fori(1, STEPS - 1) as i:
                body(i)
            body(STEPS - 1, last=True)

            for b in range(B):
                at = slice(b * NC, b * NC + NC)
                pool.wait_ge(tn_means, NC * (b + 1))
                pool.tensor_tensor(tn[:, at, :], x_att[:, at, :], spread(centre[:, at], [P, NC, D]), ALU.add)\
                    .then_inc(tn_centred, 1)
            pool.wait_ge(tn_ss, TC)
            link(pool.tensor_scalar(meansq[:, :], sumsq[:, :], 1.0 / D, EPS1, ALU.mult, ALU.add))
            link(pool.tensor_tensor(rstd[:, :], meansq[:, :], minus_half[:, :], ALU.pow))
            link(pool.tensor_tensor(tn[:, :, :], tn[:, :, :], spread(rstd[:, :], [P, TC, D]), ALU.mult))
            link(pool.tensor_copy(tn_hi[:, :, :], tn[:, :, :]))
            pool.tensor_tensor(tn_lo[:, :, :], tn[:, :, :], tn_hi[:, :, :].bitcast(F32), ALU.subtract)\
                .then_inc(tn_split, 1)
            pool.wait_ge(slots_ready, 1)
            for c in range(TC // 4 * 3, TC):
                for e in range(E):
                    last = pool.tensor_scalar(onehot[:, c, e, :], iota_row[:, :], slot_of[:, c, e:e + 1], None,
                                              ALU.is_equal)
                last.then_inc(hot_pool, 1)

        @block.scalar
        def _(act):
            act.dma_start(x_in[:, :, :], x.rearrange("b (c p) d -> p (b c) d", p=P)).then_inc(x_loaded, 16)
            act.dma_start(wqkv_raw[:, :, :], Wqkv.rearrange("(c p) d -> p c d", p=P)).then_inc(wqkv_in, 16)
            act.wait_ge(x_loaded, 16)

            def square(src, b):
                act.activation(sq0[:, b * NC:b * NC + NC, :], src[:, b * NC:b * NC + NC, :], ACT.Square)\
                   .then_inc(norm_sq, 1)

            square(x_in, 0)
            square(x_in, 1)
            act.wait_ge(cols_ready, 1)
            act.activation(silu[:, 0, :], cols[:, 0:B], ACT.Exp, scale=-1.0).then_inc(cond_exp, 1)

            def into_h(k):
                act.wait_ge(norm_T, 2 * k + 1)
                if k < 2:
                    act.wait_ge(affine_ready, k + 1)
                act.activation(h_T[:, 0:N], bank[1][:, :], ACT.Identity, bias=affine[:, k, 1, 0:1],
                               scale=affine[:, k, 0, 0:1]).then_inc(h_act, 1)

            into_h(0)
            for b in range(B):
                act.wait_ge(qkv0_done, 3 * b + 2)
                act.activation(kT0[:, b * N:b * N + N], bank[5 + b][:, :], ACT.Identity, bias=col("k_b"))\
                   .then_inc(k0_ready, 1)

            def turned0(g):
                act.wait_ge(pT0_done, g + 1)
                wait(act, o0_done, g - 1)
                act.activation(pT0[:, g % 2, :, :].rearrange("p c n -> p (c n)"), bank[3 + g % 2][:, :],
                               ACT.Copy).then_inc(pT0_copied, 1)

            for g in range(TC):
                act.wait_ge(max0_done, g + 1)
                wait(act, pT0_done, g - 1)
                act.activation(p0[:, g % 2, :], bank[1 + g % 2][:, :], ACT.Exp, bias=soft0[:, g, 0:1],
                               accum_out=soft0[:, g, 1:2]).then_inc(exp0_done, 1)
                if g >= 2:
                    turned0(g - 2)
            turned0(TC - 2)
            turned0(TC - 1)
            for b in range(B):
                act.wait_ge(mid_ready, b + 1)
                square(x_mid, b)
            def copy_weights(n):
                act.wait_ge(wT_done, n + 1)
                src = bank[5 + n % 3]
                if n < QK_BANKS:
                    t, h0 = (1, 0)[n * 4 // KC], n * 8 % H
                    act.activation(w_all[:, h0:h0 + 8, t * HD:t * HD + HD],
                                   src[:, :].rearrange("p (h d) -> p h d", d=HD), ACT.Copy)\
                       .then_inc(wT_copied, 1)
                elif n < QK_BANKS + WOUT_BANKS:
                    m = n - QK_BANKS
                    act.activation(wout_T[:, 4 * m:4 * m + 4, :].rearrange("p c d -> p (c d)"), src[:, :],
                                   ACT.Copy).then_inc(wT_copied, 1)
                else:
                    m = n - QK_BANKS - WOUT_BANKS
                    h0 = m // 2 * 8
                    heads = w_all[:, h0:h0 + 8, 2 * HD:2 * HD + D].rearrange("p (k t) d -> p t k d", t=2)
                    act.activation(heads[:, m % 2, :, :],
                                   src[:, :].rearrange("p (h d) -> p h d", d=D), ACT.Copy)\
                       .then_inc(wT_copied, 1)

            for n in range(QK_BANKS + WOUT_BANKS):
                copy_weights(n)
            into_h(1)
            for n in range(B * HC):
                b, c = n // HC, n % HC
                act.wait_ge(u0_done, n + 1)
                act.activation(u0[:, c, b * N:b * N + N], bank[3 + n % 2][:, :], ACT.Gelu,
                               bias=col("mlp_b1", c)).then_inc(gelu0_done, 1)
                if n < V_BANKS:
                    copy_weights(QK_BANKS + WOUT_BANKS + n)
                if n == V_BANKS:
                    act.wait_ge(wT_done, W_BANKS + 1)
                    act.activation(wgate_T[:, :], bank[6][:, 0:E], ACT.Copy).then_inc(wT_copied, 1)
            act.wait_ge(norm_in, 1)
            square(xn, 0)
            act.wait_ge(consts, 2)
            act.activation(table_call[:, 0:1], minus_half[:, 0:1], ACT.Exp)
            into_h(2)
            act.wait_ge(norm_in, 2)
            square(xn, 1)


            def piece_in(p, p_in):
                wait(act, qkv_done, p + 1)
                wait(act, sq_summed, p)
                qkv = in_banks(p)
                act.activation(qk_sq[:, :, :, :].rearrange("p c t d -> p c (t d)"), qkv[:, :, 0:2 * HD],
                               ACT.Square).then_inc(sq_done, 1)
                wait(act, v_placed, p - 1)
                act.activation(v_new[:, p_in % 2, :, :], qkv[:, :, 2 * HD:2 * HD + D], ACT.Copy)\
                   .then_inc(v_taken, 1)

            def piece_place(p, p_in):
                wait(act, v_taken, p + 1)
                wait(act, pv_done, 4 * p - 8)
                heads, chunks = p_in // 2 % 2 * 2, p_in % 2 * 2
                act.activation(v_s[:, heads:heads + 2, chunks:chunks + 2, :],
                               v_new[:, p_in % 2, :, :].rearrange("p (c h) d -> p h c d", h=2), ACT.Copy)\
                   .then_inc(v_placed, 1)

            def piece_affine(p):
                wait(act, kqT_done, p + 1)
                wait(act, lows_done, p)
                act.activation(kq32[:, :, :].rearrange("p h n -> p (h n)"), bank[5][:, :], ACT.Identity,
                               bias=col("kq_b"), scale=col("kq_g")).then_inc(kq_affine, 1)

            def chunk_exp(g, u, c, j):
                wait(act, max_done, g + 1)
                if c == 0:
                    wait(act, o_rec_done, u - 1)
                wait(act, probsT_done, g - 1)
                act.activation(probs[:, c % 2, :], bank[c % 2][:, :], ACT.Exp, bias=negmax[:, c:c + 1],
                               accum_out=row_sum[:, j % 2, c:c + 1]).then_inc(exp_done, 1)

            def copy_probs(g, c):
                wait(act, probsT_done, g + 1)
                wait(act, pv_done, g - 1)
                act.activation(probs_T[:, c % 2, :, :].rearrange("p c n -> p (c n)"), bank[2 + c % 2][:, :],
                               ACT.Copy).then_inc(probs_copied, 1)

            def body(i, first=False, last=False):
                for j in range(PER):
                    u = i * PER + j
                    for c in range(NC):
                        g = u * NC + c
                        if c == 0 and not (last and j >= PER - 3):
                            piece_in(u + 3, j + 3)
                        if c == 1 and not (last and j >= PER - 2):
                            piece_affine(u + 2)
                        if not (first and j == 0 and c < 2):
                            copy_probs(g - 2, c)
                        chunk_exp(g, u, c, j)
                        if c == 3 and not (last and j >= PER - 2):
                            piece_place(u + 2, j + 2)

            piece_in(0, 0)
            piece_in(1, 1)
            piece_affine(0)
            piece_place(0, 0)
            piece_affine(1)
            piece_in(2, 2)
            piece_place(1, 1)
            body(0, first=True)
            with act.Fori(1, STEPS - 1) as i:
                body(i)
            body(STEPS - 1, last=True)
            copy_probs(UNITS * NC - 2, 0)
            copy_probs(UNITS * NC - 1, 1)

            for b in range(B):
                act.wait_ge(o_normed, attended(b))
                for t in range(b * NC, b * NC + NC):
                    act.activation(tn_sq[:, t, :], x_att[:, t, :], ACT.Identity, scale=-1.0 / D,
                                   accum_out=centre[:, t:t + 1]).then_inc(tn_means, 1)
                if b == 0:
                    act.wait_ge(xaT_done, 1)
                    act.activation(xa_T[:, 0:N], bank[6], ACT.Copy).then_inc(xaT_act, 1)
            act.wait_ge(logits_sub, 1)
            act.activation(gate_x[:, :, :], gate_x[:, :, :], ACT.Exp).then_inc(gate_exp, 1)
            act.activation(table_call[:, 1:2], minus_half[:, 0:1], ACT.Gelu_apprx_tanh)
            act.wait_ge(tn_means, TC)
            for t in range(TC):
                act.wait_ge(tn_centred, t // NC + 1)
                act.activation(tn_sq[:, t, :], tn[:, t, :], ACT.Square, accum_out=sumsq[:, t:t + 1])\
                   .then_inc(tn_ss, 1)
            for n in range(2 * E):
                act.wait_ge(fcT_done, n + 1)
                dst = fc1_T[:, n, :] if n < E else fc2_T[:, n - E, :, :].rearrange("p c d -> p (c d)")
                act.activation(dst, bank[1 + n % 4][:, :], ACT.Copy).then_inc(fcT_copied, 1)
            for c in range(TC):
                if c == TC - 1:
                    for q in range(2):
                        act.wait_ge(xg_done, q + 1)
                        act.activation(xg[:, 4 * q:4 * q + 4, :].rearrange("p e n -> p (e n)"),
                                       bank[1 + q][:, :], ACT.Identity, bias=col("mlp_b"),
                                       scale=col("mlp_g")).then_inc(xg_ready, 1)
                for q in range(2):
                    act.wait_ge(hotT_done, 2 * c + q + 1)
                    act.activation(onehot_T[:, 4 * q:4 * q + 4, c * P:c * P + P],
                                   bank[5 + q][:, :].rearrange("p (e n) -> p e n", e=4), ACT.Copy)\
                       .then_inc(hotT_copied, 1)
            for e in range(E):
                act.wait_ge(fc1_done, e + 1)
                wait(act, fc2_done, e - 1)
                for c in range(DC):
                    last = act.activation(ug[:, e % 2, c, :], bank[1 + e % 2][:, c * CAP:c * CAP + CAP],
                                          ACT.Gelu_apprx_tanh, bias=col("b1s", e * DC + c))
                last.then_inc(gelu_done, 1)
            act.wait_ge(sum_done, 1)
            act.activation(sum_T[:, 0:N], bank[7], ACT.Copy).then_inc(sum_copied, 1)

        @block.vector
        def _(dve):
            steps = [0]

            def link(ins):
                steps[0] += 1
                ins.then_inc(dve_step, 1)
                dve.wait_ge(dve_step, steps[0])

            def sum_squares(k, b):
                dve.wait_ge(norm_sq, 2 * k + b + 1)
                at = slice(b * NC, b * NC + NC)
                dve.tensor_reduce(sumsq[:, at], sq0[:, at, :], AX, ALU.add).then_inc(norm_ss, 1)

            def scaled(k, b, src):
                dve.wait_ge(norm_rstd, 2 * k + b + 1)
                at = slice(b * NC, b * NC + NC)
                dve.tensor_tensor(xn[:, at, :], src[:, at, :], spread(rstd[:, at], [P, NC, D]), ALU.mult)\
                   .then_inc(norm_done, 1)

            def into_h(k):
                dve.wait_ge(norm_T, 2 * k + 2)
                dve.tensor_scalar(h_T[:, N:TOK], bank[2][:, :], affine[:, k, 0, 1:2], affine[:, k, 1, 1:2],
                                  ALU.mult, ALU.add).then_inc(h_dve, 1)

            sum_squares(0, 0)
            sum_squares(0, 1)
            dve.wait_ge(cols_T, 1)
            dve.tensor_copy(cols[:, 0:EARLY], bank[0][:, 0:EARLY]).then_inc(cols_ready, 1)
            dve.wait_ge(cond_exp, 1)
            link(dve.tensor_scalar(silu[:, 0, :], silu[:, 0, :], 1.0, None, ALU.add))
            link(dve.reciprocal(silu[:, 1, :], silu[:, 0, :]))
            dve.tensor_tensor(silu[:, 2, :], silu[:, 1, :], cols[:, 0:B], ALU.mult).then_inc(silu_ready, 1)
            scaled(0, 0, x_in)

            def film_affine(k, film, fb, w):
                link(dve.tensor_scalar(affine[:, k, 0, :], film[:, 0:B], col(fb), 1.0, ALU.add, ALU.add))
                dve.tensor_scalar(affine[:, k, 0, :], affine[:, k, 0, :], col(w), None, ALU.mult)
                link(dve.tensor_scalar(affine[:, k, 1, :], film[:, B:2 * B], col(fb, 1), None, ALU.add))

            dve.wait_ge(film1_done, 1)
            film_affine(0, bank[4], "film1_b", "norm1_w")
            dve.tensor_copy(silu[:, 0, :], silu[:, 2, :]).then_inc(affine_ready, 1)
            scaled(0, 1, x_in)

            def late_cols():
                dve.wait_ge(cols_T, 2)
                link(dve.tensor_copy(cols[:, EARLY:NROWS], bank[0][:, 0:NROWS - EARLY]))
                r = ROWS["kq_g"][0]
                dve.tensor_scalar(cols[HD:P, r:r + 2], cols[HD:P, r:r + 2], float(HD) ** -0.5, None, ALU.mult)
                dve.tensor_copy(wada_T[:, :], bank[0][:, P:2 * P]).then_inc(cols_ready, 1)

            def late_affine():
                dve.wait_ge(ada_done, 1)
                film_affine(1, bank[0], "film2_b", "norm2_w")
                for b in range(B):
                    dve.tensor_copy(affine[:, 2, 0, b:b + 1], col("ln1_g"))
                link(dve.tensor_scalar(affine[:, 2, 1, :], bank[0][:, 8:8 + B], col("b_ada"), col("ln1_b"),
                                       ALU.add, ALU.add))
                dve.tensor_copy(silu[:, 1, :], silu[:, 2, :]).then_inc(affine_ready, 1)

            into_h(0)
            dve.wait_ge(bcast_in, 48)
            for b in range(B):
                dve.wait_ge(qkv0_done, 3 * b + 1)
                dve.tensor_scalar(qT0[:, b * N:b * N + N], bank[3 + b][:, :], col("q_b"), float(D) ** -0.5,
                                  ALU.add, ALU.mult).then_inc(q0_ready, 1)
                dve.wait_ge(qkv0_done, 3 * b + 3)
                dve.tensor_tensor(v0[:, b * NC:b * NC + NC, :],
                                  bank[(7, 0)[b]][:, :].rearrange("p (c d) -> p c d", d=D),
                                  vb0[:, :].unsqueeze(1).to_broadcast([P, NC, D]), ALU.add).then_inc(v0_ready, 1)

            def attended0(b):
                dve.wait_ge(o0_done, NC * (b + 1))
                dve.tensor_copy(oT0[:, b * N:b * N + N], bank[5 + b][:, :]).then_inc(o0_copied, 1)

            def batch_out0(b):
                dve.wait_ge(proj0_done, b + 1)
                dve.wait_ge(xpb_ready, 1)
                dve.tensor_tensor(x_mid[:, b * NC:b * NC + NC, :], x_in[:, b * NC:b * NC + NC, :],
                                  bank[(7, 0)[b]][:, :].rearrange("p (c d) -> p c d", d=D), ALU.add)\
                   .then_inc(mid_ready, 1)

            for g in range(TC + 1):
                if g < TC:
                    dve.wait_ge(s0_done, g + 1)
                    dve.tensor_reduce(soft0[:, g, 0:1], bank[1 + g % 2][:, :], AX, ALU.max, negate=True)\
                       .then_inc(max0_done, 1)
                if g:
                    k = g - 1
                    dve.wait_ge(exp0_done, k + 1)
                    link(dve.reciprocal(soft0[:, k, 2:3], soft0[:, k, 1:2]))
                    dve.tensor_scalar(p0[:, k % 2, :], p0[:, k % 2, :], soft0[:, k, 2:3], None, ALU.mult)\
                       .then_inc(p0_ready, 1)
                if g == 2:
                    late_cols()
                if g == 4:
                    late_affine()
                if g == NC + 2:
                    attended0(0)
                if g == NC + 4:
                    batch_out0(0)
            attended0(1)
            sum_squares(1, 0)
            batch_out0(1)
            scaled(1, 0, x_mid)
            sum_squares(1, 1)
            scaled(1, 1, x_mid)
            into_h(1)
            dve.wait_ge(wT_copied, QK_BANKS)
            link(dve.tensor_reduce(wmean[:, :, :],
                                   w_all[:, :, 0:2 * HD].rearrange("p h (t d) -> p h t d", d=HD), AX, ALU.add, negate=True))
            dve.tensor_scalar(wmean[:, :, :], wmean[:, :, :], 1.0 / HD, None, ALU.mult).then_inc(w_summed, 1)
            dve.wait_ge(w_centred, 1)
            dve.wait_ge(wT_copied, W_BANKS)
            dve.tensor_copy(w_hi[:, :, :], w_all[:, :, :]).then_inc(w_centred, 1)

            def block_out(b):
                at = slice(b * NC, b * NC + NC)
                dve.wait_ge(y0_done, b + 1)
                dve.wait_ge(xmb_ready, 1)
                link(dve.tensor_tensor(x_att[:, at, :], x_mid[:, at, :],
                                       bank[(7, 0)[b]][:, :].rearrange("p (c d) -> p c d", d=D), ALU.add))
                link(dve.tensor_reduce(centre[:, at], x_att[:, at, :], AX, ALU.add, negate=True))
                link(dve.tensor_scalar(centre[:, at], centre[:, at], 1.0 / D, None, ALU.mult))
                dve.tensor_tensor(xn[:, at, :], x_att[:, at, :], spread(centre[:, at], [P, NC, D]), ALU.add)\
                   .then_inc(norm_in, 1)

            def split_h(b):
                at = slice(b * N, b * N + N)
                dve.wait_ge((h_act, h_dve)[b], 3)
                link(dve.tensor_copy(h_hi[:, at], h_T[:, at]))
                dve.tensor_tensor(h_lo[:, at], h_T[:, at], h_hi[:, at].bitcast(F32), ALU.subtract)\
                   .then_inc(h_split, 1)

            block_out(0)
            sum_squares(2, 0)
            rest = slice(POOL_HEADS, H)
            dve.wait_ge(w_centred, 2)
            dve.tensor_tensor(w_lo[:, rest, :], w_all[:, rest, :], w_hi[:, rest, :].bitcast(F32),
                              ALU.subtract).then_inc(w_split, 1)
            scaled(2, 0, xn)
            block_out(1)
            split_h(0)
            sum_squares(2, 1)


            def piece_ss(p):
                wait(dve, sq_done, p + 1)
                dve.tensor_reduce(qk_ss[:, :, :], qk_sq[:, :, :, :], AX, ALU.add).then_inc(sq_summed, 1)
                wait(dve, sq_summed, p + 1)
                wait(dve, rstd_done, p)
                dve.tensor_scalar(qk_ms[:, :, :], qk_ss[:, :, :], 1.0 / HD, EPS1, ALU.mult, ALU.add)\
                   .then_inc(ss_done, 1)

            def piece_norm(p, p_in):
                wait(dve, rstd_done, p + 1)
                wait(dve, v_taken, p + 1)
                wait(dve, kqT_done, p - 1)
                dve.tensor_tensor(qk_n[:, p_in % 2, :, :, :],
                                  in_banks(p)[:, :, 0:2 * HD].rearrange("p c (t d) -> p c t d", d=HD),
                                  spread(qk_rstd[:, :, :], [P, NC, 2, HD]), ALU.mult).then_inc(normed, 1)

            def piece_high(p, p_in):
                wait(dve, kq_affine, p + 1)
                wait(dve, scores_done, group_unused(p, p_in))
                dve.tensor_copy(piece_at(k_s, p_in), kq32[:, :, :]).then_inc(highs_done, 1)
                wait(dve, highs_done, p + 1)
                dve.tensor_copy(piece_at(q_s, p_in, 0, HD), piece_at(k_s, p_in, HD, P).bitcast(F32))\
                   .then_inc(q_hi_moved, 1)

            def piece_low(p, p_in):
                wait(dve, lows_done, p + 1)
                dve.tensor_copy(piece_at(q_s, p_in, HD, P), piece_at(lows, p_in, HD, P).bitcast(F32))
                wait(dve, q_hi_moved, p + 1)
                dve.tensor_copy(piece_at(k_s, p_in, HD, P), piece_at(k_s, p_in, 0, HD).bitcast(F32))\
                   .then_inc(split_done, 1)

            def chunk_max(g, s):
                wait(dve, scores_done, g + 1)
                dve.tensor_reduce(negmax[:, s:s + 1], bank[s % 2][:, :], AX, ALU.max, negate=True)\
                   .then_inc(max_done, 1)

            def unit_out(u, slot, b):
                o = bank[4][:, :].rearrange("p (c d) -> p c d", d=D)
                wait(dve, pv_done, 4 * u + 4)
                dve.reciprocal(o_rec[:, :], row_sum[:, slot, :]).then_inc(o_rec_done, 1)
                wait(dve, o_rec_done, u + 1)
                wait(dve, o_normed, u)
                for c in range(NC):
                    at = x_att[:, b * NC + c, :]
                    last = dve.scalar_tensor_tensor(out=at, in0=o[:, c, :], scalar=o_rec[:, c:c + 1], in1=at,
                                                    op0=ALU.mult, op1=ALU.add)
                last.then_inc(o_normed, 1)

            def body(i, first=False, last=False):
                for j in range(PER):
                    u = i * PER + j
                    for c in range(NC):
                        g = u * NC + c
                        if c == 3 and not (first and j == 0):
                            unit_out(u - 1, (j + 1) % 2, (j + 3) // 2 % 2)
                        chunk_max(g, c)
                        if c == 0 and not (last and j >= PER - 3):
                            piece_ss(u + 3)
                        if c == 1 and not (last and j >= PER - 2):
                            piece_high(u + 2, j + 2)
                        if c == 2 and not (last and j >= PER - 3):
                            piece_norm(u + 3, j + 3)
                        if c == 3 and not (last and j >= PER - 2):
                            piece_low(u + 2, j + 2)

            piece_ss(0)
            scaled(2, 1, xn)
            piece_norm(0, 0)
            piece_ss(1)
            into_h(2)
            split_h(1)
            piece_norm(1, 1)
            piece_high(0, 0)
            piece_low(0, 0)
            piece_high(1, 1)
            piece_ss(2)
            piece_low(1, 1)
            piece_norm(2, 2)
            body(0, first=True)
            with dve.Fori(1, STEPS - 1) as i:
                body(i)
            body(STEPS - 1, last=True)
            unit_out(UNITS - 1, 1, B - 1)
            dve.wait_ge(o_normed, UNITS)

            for c in range(CANDS):
                start = (c + 1) << (BITS - DIGIT)
                dve.memset(offset[:, 0, c, :], float(start)).then_inc(digit_step, 1)
                dve.memset(cand[:, c, :], start).then_inc(digit_step, 1)
            dve.memset(thr[:, :], 0).then_inc(digit_step, 1)
            dve.wait_ge(xaT_done, 2)
            dve.tensor_copy(xa_T[:, N:TOK], bank[6]).then_inc(xaT_dve, 1)
            logits = bank[7][:, 0:TC * E].rearrange("p (c e) -> p c e", e=E)
            dve.wait_ge(logits_done, 1)
            link(dve.tensor_reduce(gate_m[:, 0, :], logits, AX, ALU.max))
            dve.tensor_tensor(gate_x[:, :, :], logits, spread(gate_m[:, 0, :], [P, TC, E]), ALU.subtract)\
               .then_inc(logits_sub, 1)
            dve.wait_ge(gate_exp, 1)
            link(dve.tensor_reduce(gate_m[:, 0, :], gate_x[:, :, :], AX, ALU.add))
            link(dve.reciprocal(gate_m[:, 1, :], gate_m[:, 0, :]))
            link(dve.tensor_tensor(gate[:, :, :], gate_x[:, :, :], spread(gate_m[:, 1, :], [P, TC, E]), ALU.mult))

            over = lambda t: t.unsqueeze(1).to_broadcast([P, TC, E])
            counts = bank[0][:, 0:CANDS * E].rearrange("p (c e) -> p c e", e=E)
            INITS, OPS = 1 + 2 * CANDS, 7

            def settle(n, slot):
                done = INITS + OPS * n
                dve.wait_ge(digit_step, done - 1)
                for half in range(2):
                    at = slice(half * NC, half * NC + NC)
                    dve.tensor_tensor(at_least[:, at, :, :],
                                      gate[:, at, :].unsqueeze(2).to_broadcast([P, NC, CANDS, E]),
                                      cand[:, :, :].bitcast(F32).unsqueeze(1).to_broadcast([P, NC, CANDS, E]),
                                      ALU.is_ge).then_inc(cmp_done, 1)
                dve.tensor_scalar(next_offset[:, :, :], offset[:, slot, :, :], 1.0 / (1 << DIGIT), None,
                                  ALU.mult).then_inc(digit_step, 1)
                dve.tensor_scalar(offset[:, 1 - slot, :, :], offset[:, slot, :, :], 1.0 / (1 << DIGIT), None,
                                  ALU.mult).then_inc(digit_step, 1)
                dve.wait_ge(digit_step, done + 1)
                dve.tensor_tensor(next_base[:, :, :], next_offset[:, :, :],
                                  thr[:, :].unsqueeze(1).to_broadcast([P, CANDS, E]), ALU.bitwise_or)\
                   .then_inc(digit_step, 1)
                dve.wait_ge(count_done, n + 1)
                dve.scalar_tensor_tensor(out=hit[:, :, :], in0=counts, scalar=CAP - 0.5,
                                         in1=offset[:, slot, 0:1, :].to_broadcast([P, CANDS, E]),
                                         op0=ALU.is_ge, op1=ALU.mult).then_inc(digit_step, 1)
                dve.wait_ge(digit_step, done + 4)
                with nc.allow_low_precision(reason="whole numbers, at most 7 times a power of two"):
                    dve.tensor_reduce(digit[:, :], hit[:, :, :].rearrange("p c e -> p e c"), AX, ALU.add)\
                       .then_inc(digit_step, 1)
                dve.wait_ge(digit_step, done + 5)
                dve.tensor_tensor(cand[:, :, :], next_base[:, :, :],
                                  digit[:, :].unsqueeze(1).to_broadcast([P, CANDS, E]), ALU.bitwise_or)\
                   .then_inc(digit_step, 1)
                dve.tensor_tensor(thr[:, :], thr[:, :], digit[:, :], ALU.bitwise_or).then_inc(digit_step, 1)

            with dve.Fori(0, DIGITS // 2) as m:
                for slot in range(2):
                    settle(2 * m + slot, slot)
            dve.wait_ge(digit_step, INITS + OPS * DIGITS)
            dve.tensor_tensor(above[:, :, :], gate[:, :, :], over(thr[:, :].bitcast(F32)), ALU.is_gt)\
               .then_inc(masks_ready, 1)
            dve.tensor_tensor(ties[:, :, :], gate[:, :, :], over(thr[:, :].bitcast(F32)), ALU.is_equal)\
               .then_inc(masks_ready, 1)
            link(dve.tensor_copy(gate_r[:, :, :, 0], gate[:, :, :]))
            dve.tensor_tensor(gate_r[:, :, :, 1], gate[:, :, :], gate_r[:, :, :, 0].bitcast(F32), ALU.subtract)\
               .then_inc(gate_split, 1)
            dve.wait_ge(ranks_done, 1)
            link(dve.tensor_scalar(need[:, :], bank[0][:, 0:E], -1.0, float(CAP), ALU.mult, ALU.add))
            ranks = bank[0][:, 64:64 + TC * E].rearrange("p (c e) -> p c e", e=E)
            link(dve.tensor_tensor(rank[:, :, :], ranks, over(need[:, :]), ALU.is_lt))
            link(dve.tensor_tensor(rank[:, :, :], rank[:, :, :], ties[:, :, :], ALU.mult))
            dve.tensor_tensor(taken[:, :, :], rank[:, :, :], above[:, :, :], ALU.add).then_inc(taken_ready, 1)
            dve.wait_ge(taken_ready, 1)
            dve.wait_ge(slots_done, 1)
            slots = bank[0][:, 128:128 + TC * E].rearrange("p (c e) -> p c e", e=E)
            link(dve.scalar_tensor_tensor(out=slot_of[:, :, :].rearrange("p c e -> p (c e)"),
                                          in0=bank[0][:, 128:128 + TC * E], scalar=-NOWHERE,
                                          in1=taken[:, :, :].rearrange("p c e -> p (c e)"),
                                          op0=ALU.add, op1=ALU.mult))
            dve.tensor_scalar(slot_of[:, :, :], slot_of[:, :, :], NOWHERE, None, ALU.add).then_inc(slots_ready, 1)
            dve.wait_ge(slots_ready, 1)
            for c in range(TC // 4 * 3):
                for e in range(E):
                    last = dve.tensor_scalar(onehot[:, c, e, :], iota_row[:, :], slot_of[:, c, e:e + 1], None,
                                             ALU.is_equal)
                last.then_inc(hot_dve, 1)
            def copy_weights(q):
                dve.wait_ge(w_rows_done, q + 1)
                dve.tensor_copy(w_rows[:, q, :], bank[7 - q][0:E, :]).then_inc(w_rows_copied, 1)

            def join_weights(q):
                at = 256 + E * E // 2 * q
                dve.wait_ge(wslot_done, q + 1)
                dve.tensor_reduce(w_slot[:, E // 2 * q:E // 2 * (q + 1)],
                                  bank[0][:, at:at + E // 2 * (E + 2)].rearrange("p (e k) -> p e k", k=E + 2)[:, :, 0:2],
                                  AX, ALU.add).then_inc(wslot_ready, 1)
                dve.wait_ge(wslot_ready, q + 1)

            copy_weights(0)
            for e in range(E):
                if e % (E // 2) == 0:
                    join_weights(e // (E // 2))
                dve.wait_ge(fc2_done, e + 1)
                link(dve.tensor_tensor(y_sum[:, e % 2, :], b2_all[:, e, :], bank[3 + e % 2][:, 0:D], ALU.add))
                link(dve.tensor_scalar(y_hi[:, e, :], y_sum[:, e % 2, :], w_slot[:, e:e + 1], None, ALU.mult))
                dve.scalar_tensor_tensor(out=y_lo[:, e, :], in0=y_sum[:, e % 2, :], scalar=w_slot[:, e:e + 1],
                                         in1=y_hi[:, e, :].bitcast(F32), op0=ALU.mult, op1=ALU.subtract)\
                   .then_inc(y_ready, 1)
                if e == 1:
                    copy_weights(1)
            dve.wait_ge(sum_done, 2)
            dve.wait_ge(sum_copied, 1)
            dve.tensor_copy(sum_T[:, N:TOK], bank[5][:, :]).then_inc(sum_copied, 1)
            for half in range(2):
                dve.wait_ge(sumT_done, half + 1)
                dve.tensor_tensor(final[:, half * NC:half * NC + NC, :], x_att[:, half * NC:half * NC + NC, :],
                                  bank[1 + half][:, :].rearrange("p (c d) -> p c d", d=D), ALU.add)\
                   .then_inc(final_ready, 1)

        @block.tensor
        def _(pe):
            def turn4(dst, srcs):
                for n, s in enumerate(srcs):
                    last = pe.transpose(dst[:, n * P:n * P + P], s, ident[:, :])
                return last

            pe.wait_ge(consts, 1)
            pe.wait_ge(early_in, 16 * len(early_loads))
            pe.transpose(bank[0][:, 0:EARLY], early_rows[:, :], ident[0:EARLY, 0:EARLY]).then_inc(cols_T, 1)
            pe.wait_ge(cols_ready, 1)
            pe.wait_ge(film1_in, 16)

            def film_products(dst, w):
                for part in range(2):
                    last = pe.matmul(dst[:, B * part:B * part + B], w[:, part * D:part * D + D],
                                     cols[:, 0:B], start=True, stop=True)
                return last

            film_products(bank[4], film1).then_inc(film1_done, 1)

            def late_turns():
                pe.wait_ge(late_in, 16 * len(late_loads))
                pe.wait_ge(wada_in, 16)
                pe.wait_ge(v0_ready, 2)
                pe.transpose(bank[0][:, 0:NROWS - EARLY], late_rows[:, :],
                             ident[0:NROWS - EARLY, 0:NROWS - EARLY])
                pe.transpose(bank[0][:, P:2 * P], wada[:, :], ident[:, :]).then_inc(cols_T, 1)

            def late_products():
                pe.wait_ge(cols_ready, 2)
                pe.wait_ge(film2_in, 16)
                pe.wait_ge(silu_ready, 1)
                film_products(bank[0], film2)
                pe.matmul(bank[0][:, 8:8 + B], wada_T[:, :], silu[:, 2, :], start=True, stop=True)\
                  .then_inc(ada_done, 1)

            def turn_norm(k, b):
                pe.wait_ge(norm_done, 2 * k + b + 1)
                turn4(bank[1 + b], [xn[:, b * NC + c, :] for c in range(NC)]).then_inc(norm_T, 1)

            turn_norm(0, 0)
            turn_norm(0, 1)
            pe.wait_ge(qkv_in, 48)
            pe.wait_ge(affine_ready, 1)
            pe.wait_ge(h_act, 1)
            for b in range(B):
                hb = h_T[:, b * N:b * N + N]
                if b == 1:
                    pe.wait_ge(h_dve, 1)
                pe.matmul(bank[3 + b][:, :], wq0[:, :], hb, start=True, stop=True).then_inc(qkv0_done, 1)
                pe.matmul(bank[5 + b][:, :], wk0[:, :], hb, start=True, stop=True).then_inc(qkv0_done, 1)
                for c in range(NC):
                    last = pe.matmul(bank[(7, 0)[b]][:, c * D:c * D + D],
                                     h_T[:, (b * NC + c) * P:(b * NC + c + 1) * P], wv0[:, :],
                                     start=True, stop=True)
                last.then_inc(qkv0_done, 1)

            def scores0(g):
                b = g // NC
                pe.wait_ge(q0_ready, b + 1)
                pe.wait_ge(k0_ready, b + 1)
                wait(pe, exp0_done, g - 1)
                pe.matmul(bank[1 + g % 2][:, :], qT0[:, g * P:g * P + P], kT0[:, b * N:b * N + N],
                          start=True, stop=True).then_inc(s0_done, 1)

            def turn0(g):
                pe.wait_ge(p0_ready, g + 1)
                if g < 2:
                    pe.wait_ge(q0_ready, 2)
                wait(pe, pT0_copied, g - 1)
                turn4(bank[3 + g % 2], [p0[:, g % 2, c * P:c * P + P] for c in range(NC)]).then_inc(pT0_done, 1)

            def mix0(g):
                b, n = g // NC, g % NC
                pe.wait_ge(pT0_copied, g + 1)
                pe.wait_ge(v0_ready, b + 1)
                for c in range(NC):
                    last = pe.matmul(bank[5 + b][:, n * P:n * P + P], v0[:, b * NC + c, :],
                                     pT0[:, g % 2, c, :], start=(c == 0), stop=(c == NC - 1))
                last.then_inc(o0_done, 1)

            def proj0(b):
                pe.wait_ge(o0_copied, b + 1)
                pe.wait_ge(proj_in, 16)
                pe.wait_ge(affine_ready, 2)
                for c in range(NC):
                    last = pe.matmul(bank[(7, 0)[b]][:, c * D:c * D + D],
                                     oT0[:, (b * NC + c) * P:(b * NC + c + 1) * P], wp0[:, :],
                                     start=True, stop=True)
                last.then_inc(proj0_done, 1)

            for g in range(TC + 3):
                if g < TC:
                    scores0(g)
                if 2 <= g < TC + 2:
                    turn0(g - 2)
                if g >= 3:
                    mix0(g - 3)
                if g == 1:
                    late_turns()
                if g == 3:
                    late_products()
                if g == NC + 3:
                    proj0(0)
            proj0(1)

            pe.wait_ge(wqkv_in, 16)
            pe.wait_ge(wout_in, 32)
            pe.wait_ge(o0_copied, 2)
            pe.wait_ge(mid_ready, 1)
            def make_weights(n):
                wait(pe, wT_copied, n - 2)
                dst = bank[5 + n % 3]
                if n < QK_BANKS:
                    last = turn4(dst, [wqkv_raw[:, 4 * n + c, :] for c in range(4)])
                elif n < QK_BANKS + WOUT_BANKS:
                    at = (n - QK_BANKS) * 4
                    last = turn4(dst, [wout[:, (at + c) * P:(at + c + 1) * P] for c in range(4)])
                else:
                    if n == QK_BANKS + WOUT_BANKS:
                        pe.wait_ge(wT_copied, QK_BANKS + WOUT_BANKS)
                    for k in range(4):
                        m = n - QK_BANKS - WOUT_BANKS
                        h = m // 2 * 8 + 2 * k + m % 2
                        part = slice(h % 2 * HD, h % 2 * HD + HD)
                        last = pe.matmul(dst[:, k * D:k * D + D], wqkv_raw[part, 2 * KC + h // 2, :],
                                         wout_T[part, h // 2, :], start=True, stop=True)
                last.then_inc(wT_done, 1)

            for n in range(QK_BANKS + WOUT_BANKS):
                make_weights(n)

            turn_norm(1, 0)
            turn_norm(1, 1)
            pe.wait_ge(mlp_in, 32)
            pe.wait_ge(h_act, 2)

            def up0(n):
                b, c = n // HC, n % HC
                if n == HC:
                    pe.wait_ge(h_dve, 2)
                wait(pe, gelu0_done, n - 1)
                pe.matmul(bank[3 + n % 2][:, :], w10[:, c * P:c * P + P], h_T[:, b * N:b * N + N],
                          start=True, stop=True).then_inc(u0_done, 1)

            def down0(b):
                pe.wait_ge(gelu0_done, HC * (b + 1))
                pe.wait_ge(wT_copied, W_BANKS)
                pe.wait_ge(mid_ready, 2)
                for c in range(NC):
                    for k in range(HC):
                        last = pe.matmul(bank[(7, 0)[b]][:, c * D:c * D + D],
                                         u0[:, k, (b * NC + c) * P:(b * NC + c + 1) * P], w20[:, k, :],
                                         start=(k == 0), stop=(k == HC - 1))
                last.then_inc(y0_done, 1)

            for n in range(HC + 2):
                up0(n)
                if 1 <= n <= V_BANKS:
                    make_weights(QK_BANKS + WOUT_BANKS + n - 1)
            pe.wait_ge(wT_copied, W_BANKS)
            pe.transpose(bank[6][:, 0:E], wgate[:, :], ident[0:E, 0:E]).then_inc(wT_done, 1)
            down0(0)
            for n in range(HC + 2, 2 * HC):
                up0(n)
            down0(1)
            turn_norm(2, 0)
            pe.wait_ge(h_split, 1)
            pe.wait_ge(w_split, 3)
            pe.wait_ge(wT_copied, W_BANKS + 1)

            def project(p, p_in, head):
                if banks_of(p) is pair:
                    wait(pe, normed, p)
                    wait(pe, v_taken, p)
                for c in range(2):
                    at = (p_in // 2 % 2 * NC + p_in % 2 * 2 + c) * P
                    for n, (h_part, w_part) in enumerate(((h_hi, w_hi), (h_hi, w_lo), (h_lo, w_hi))):
                        last = pe.matmul(banks_of(p)[:, c, :], h_part[:, at:at + P],
                                         w_part[:, bass.ds(head, 2), :].rearrange("p h w -> p (h w)"),
                                         start=(n == 0), stop=(n == 2))
                last.then_inc(qkv_done, 1)

            def turn_piece(p, p_in):
                wait(pe, normed, p + 1)
                wait(pe, kq_affine, p)
                turn4(bank[5], [qk_n[:, p_in % 2, 2 * c + h, :, :].rearrange("p t d -> p (t d)")
                                for h in range(2) for c in range(2)]).then_inc(kqT_done, 1)

            def scores(g, u, c, j):
                if c == 0:
                    wait(pe, split_done, u + 2 - j % 2)
                wait(pe, exp_done, g - 1)
                at, slot, h = slice(c * P, c * P + P), j // 2, j % 2
                pe.matmul(bank[c % 2][:, :], q_s[:, slot, h, at], k_s[:, slot, h, :], start=True, stop=False)
                pe.matmul(bank[c % 2][:, :], q_s[0:HD, slot, h, at], lows[0:HD, slot, h, :],
                          start=False, stop=True).then_inc(scores_done, 1)

            def turn_probs(g, c):
                wait(pe, exp_done, g + 1)
                wait(pe, probs_copied, g - 1)
                turn4(bank[2 + c % 2], [probs[:, c % 2, k * P:k * P + P] for k in range(NC)])\
                    .then_inc(probsT_done, 1)

            def mix(g, u, c, slot):
                wait(pe, probs_copied, g + 1)
                if c == 0:
                    wait(pe, v_placed, u + 2 - slot % 2)
                    wait(pe, o_normed, u)
                for k in range(NC):
                    last = pe.matmul(bank[4][:, c * D:c * D + D], probs_T[:, c % 2, k, :],
                                     v_s[:, slot, k, :], start=(k == 0), stop=(k == NC - 1))
                last.then_inc(pv_done, 1)

            def body(i, first=False, last=False):
                for j in range(PER):
                    u = i * PER + j
                    for c in range(NC):
                        g = u * NC + c
                        scores(g, u, c, j)
                        if c == 0 and not (last and j >= PER - 2):
                            turn_piece(u + 2, j + 2)
                        if not (first and j == 0 and c < 2):
                            turn_probs(g - 2, c % 2)
                        if c == 3 and not last:
                            project(u + 4, j, 2 * i + 2)
                        if not (first and j == 0 and c < 3):
                            back = u if c == 3 else u - 1
                            mix(g - 3, back, (c + 1) % NC, j if c == 3 else (j - 1) % PER)

            project(0, 0, 0)
            project(1, 1, 0)
            turn_norm(2, 1)
            turn_piece(0, 0)
            turn_piece(1, 1)
            pe.wait_ge(h_split, 2)
            project(2, 2, 0)
            project(3, 3, 0)
            body(0, first=True)
            with pe.Fori(1, STEPS - 1) as i:
                body(i)
            body(STEPS - 1, last=True)
            G = UNITS * NC
            turn_probs(G - 2, 0)
            mix(G - 3, UNITS - 1, 1, PER - 1)
            turn_probs(G - 1, 1)
            mix(G - 2, UNITS - 1, 2, PER - 1)
            mix(G - 1, UNITS - 1, 3, PER - 1)

            def turn_tokens(b):
                pe.wait_ge(o_normed, attended(b))
                if b:
                    pe.wait_ge(xaT_act, 1)
                turn4(bank[6], [x_att[:, b * NC + c, :] for c in range(NC)]).then_inc(xaT_done, 1)

            def logits(b):
                pe.wait_ge((xaT_act, xaT_dve)[b], 1)
                for c in range(b * NC, b * NC + NC):
                    last = pe.matmul(bank[7][:, c * E:c * E + E], xa_T[:, c * P:c * P + P], wgate_T[:, :],
                                     start=True, stop=True)
                return last

            turn_tokens(0)
            logits(0)
            turn_tokens(1)
            logits(1).then_inc(logits_done, 1)
            pe.wait_ge(fc_in, 48)

            def turn_experts(n):
                wait(pe, fcT_copied, n - 3)
                src = [fc1_raw[:, n, c, :] for c in range(4)] if n < E else \
                    [fc2_raw[:, n - E, c * P:c * P + P] for c in range(4)]
                turn4(bank[1 + n % 4], src).then_inc(fcT_done, 1)

            turn_experts(0)
            turn_experts(1)
            for n in range(DIGITS):
                for c in range(TC):
                    if c % NC == 0:
                        pe.wait_ge(cmp_done, 2 * n + 1 + c // NC)
                    last = pe.matmul(bank[0][:, 0:CANDS * E], ones_bf[:, :],
                                     at_least[:, c, :, :].rearrange("p c e -> p (c e)"),
                                     start=(c == 0), stop=(c == TC - 1))
                last.then_inc(count_done, 1)
                for k in range(2 * n + 2, min(2 * n + 4, 2 * E)):
                    turn_experts(k)

            def before(at, mask, done):
                flat = lambda lo, hi: bank[0][:, at + lo * E:at + hi * E]
                pe.matmul(flat(0, TC), before_bf[:, :], mask[:, :, :].rearrange("p c e -> p (c e)"),
                          start=True, stop=False, skip_group_check=True)
                for c in range(TC - 1):
                    last = pe.matmul(flat(c + 1, TC).rearrange("p (c e) -> p c e", e=E), ones_bf[:, :],
                                     mask[:, c, :].unsqueeze(1).to_broadcast([P, TC - 1 - c, E]),
                                     start=False, stop=(c == TC - 2), skip_group_check=True)
                last.then_inc(done, 1)

            pe.wait_ge(masks_ready, 2)
            for c in range(TC):
                pe.matmul(bank[0][:, 0:E], ones_bf[:, :], above[:, c, :], start=(c == 0), stop=(c == TC - 1))
            before(64, ties, ranks_done)
            pe.wait_ge(taken_ready, 1)
            before(128, taken, slots_done)

            pe.wait_ge(tn_split, 1)
            pe.wait_ge(fcT_copied, 2 * E)
            for c in range(TC):
                if c < TC // 4 * 3:
                    pe.wait_ge(hot_dve, c + 1)
                else:
                    pe.wait_ge(hot_pool, c + 1 - TC // 4 * 3)
                for q in range(2):
                    for n, part in enumerate((tn_hi, tn_lo)):
                        last = pe.matmul(bank[1 + q][:, :], part[:, c, :],
                                         onehot[:, c, 4 * q:4 * q + 4, :].rearrange("p e n -> p (e n)"),
                                         start=(c == 0 and n == 0), stop=(c == TC - 1 and n == 1))
                    if c == TC - 1:
                        last.then_inc(xg_done, 1)
                for q in range(2):
                    if c:
                        pe.wait_ge(hotT_copied, 2 * c - 1 + q)
                    turn4(bank[5 + q], [onehot[:, c, 4 * q + e, :].bitcast(F32) for e in range(4)])\
                        .then_inc(hotT_done, 1)
            pe.wait_ge(gate_split, 1)
            pe.wait_ge(slots_ready, 1)

            def slot_weights(q, chunks):
                for c in chunks:
                    last = pe.matmul(bank[7 - q][0:E, :],
                                     gate_r[:, c, E // 2 * q:E // 2 * (q + 1), :].rearrange("p e n -> p (e n)"),
                                     onehot[:, c, 4 * q:4 * q + 4, :].rearrange("p e n -> p (e n)"),
                                     start=(c == 0), stop=(c == TC - 1))
                if c == TC - 1:
                    last.then_inc(w_rows_done, 1)

            def turn_weights(q):
                pe.wait_ge(w_rows_copied, q + 1)
                for e in range(E // 2):
                    at = 256 + E * (E // 2 * q + e)
                    last = pe.transpose(bank[0][:, at:at + E], w_rows[:, q, e * CAP:e * CAP + CAP], ident[0:E, 0:E])
                last.then_inc(wslot_done, 1)

            def up(e):
                if e < 2:
                    pe.wait_ge(xg_ready, 2)
                wait(pe, gelu_done, e - 1)
                for c in range(DC):
                    last = pe.matmul(bank[1 + e % 2][:, c * CAP:c * CAP + CAP], fc1_T[:, e, c * P:c * P + P],
                                     xg[:, e, :], start=True, stop=True)
                last.then_inc(fc1_done, 1)

            def down(e):
                pe.wait_ge(gelu_done, e + 1)
                wait(pe, y_ready, e - 1)
                for c in range(DC):
                    last = pe.matmul(bank[3 + e % 2][:, 0:D], ug[:, e % 2, c, :], fc2_T[:, e, c, :],
                                     start=(c == 0), stop=(c == DC - 1))
                last.then_inc(fc2_done, 1)

            def scatter(e):
                if e == 0:
                    pe.wait_ge(hotT_copied, 2 * TC)
                pe.wait_ge(y_ready, e + 1)
                for b, dst in enumerate((bank[7], bank[5])):
                    for n, part in enumerate((y_hi, y_lo)):
                        last = pe.matmul(dst[:, :], part[:, e, :], onehot_T[:, e, b * N:b * N + N],
                                         start=(e == 0 and n == 0), stop=(e == E - 1 and n == 1))
                    if e == E - 1:
                        last.then_inc(sum_done, 1)

            slot_weights(0, range(TC // 2))
            up(0)
            slot_weights(0, range(TC // 2, TC))
            for e in range(E):
                if e + 1 < E:
                    up(e + 1)
                down(e)
                if e == 0:
                    turn_weights(0)
                if e == 1:
                    pe.wait_ge(hotT_copied, 2 * TC)
                    slot_weights(1, range(TC))
                if e == 3:
                    turn_weights(1)
                if e:
                    scatter(e - 1)
            scatter(E - 1)
            for b in range(B):
                pe.wait_ge(sum_copied, b + 1)
                turn4(bank[1 + b], [sum_T[:, (b * NC + c) * P:(b * NC + c + 1) * P] for c in range(NC)])\
                    .then_inc(sumT_done, 1)


_INS = ['x', 'cond_1024'] + ['L0_cond_' + n for n in (
    'norm1_w', 'film1_w', 'film1_b', 'q_w', 'q_b', 'k_w', 'k_b', 'v_w', 'v_b', 'proj_w', 'proj_b', 'norm2_w',
    'film2_w', 'film2_b', 'mlp_w1', 'mlp_b1', 'mlp_w2', 'mlp_b2')] + ['L1_cond_' + n for n in (
        'W_ada', 'b_ada', 'ln1_g', 'ln1_b', 'Wqkv', 'qn_g', 'qn_b', 'kn_g', 'kn_b', 'Wout', 'mlp_g', 'mlp_b',
        'Wgate', 'fc1s', 'b1s', 'fc2s', 'b2s')]


def kernel(**inputs):
    import numpy as np
    import concourse.bacc as bacc
    from concourse.bass_utils import run_bass_kernel_spmd

    nc = bacc.Bacc("TRN2", target_bir_lowering=False, num_devices=1)
    arrays, args = {}, []
    for name in _INS:
        a = np.ascontiguousarray(inputs[name])
        arrays[f"in_{name}_dram"] = a
        args.append(nc.dram_tensor(f"in_{name}_dram", a.shape, mybir.dt.from_np(a.dtype),
                                   kind="ExternalInput").ap())
    args.append(nc.dram_tensor("out_dram", inputs["x"].shape, F32, kind="ExternalOutput").ap())
    film_attention_then_expert_choice(nc, *args)
    r = run_bass_kernel_spmd(nc, [arrays], core_ids=[0])
    return r.results[0]["out_dram"]
```
